# Optimizing a Trainium2 kernel written in Bass

```python
import numpy as np
import jax
import jax.numpy as jnp

def _softmax(x, axis=-1):
    return jax.nn.softmax(x, axis=axis)

def _gelu(x):
    return jax.nn.gelu(x, approximate=True)

def _silu(x):
    return jax.nn.silu(x)

def _sigmoid(x):
    return jax.nn.sigmoid(x)

def _layernorm(x, axis=-1, eps=1e-05):
    m = jnp.mean(x, axis=axis, keepdims=True)
    v = jnp.var(x, axis=axis, keepdims=True)
    return (x - m) / jnp.sqrt(v + eps)

def _scatter_add(tgt, idx, src, axis=0):
    return tgt.at[idx].add(src)

def _segment_sum(src, seg, n):
    return jax.ops.segment_sum(src, seg, n)
kernel_name = 'mk_decoder_preln_d2_seqx_r8_ce5e76'

def setup_inputs(seed: int=0):
    np.random.seed(seed)
    _w = jnp.asarray

    def _rec_inputs():
        import jax
        import jax.numpy as jnp
        _rk = jax.random.key(seed)
        x = -7.109e-05 + 0.9999 * jax.random.normal(jax.random.fold_in(_rk, 1), (4, 256, 256), jnp.float32)
        _lenS = 256 - jax.random.randint(jax.random.fold_in(_rk, 7), (4,), 0, max(1, 256 // 4) + 1, jnp.int32)
        _lenS2 = 256 - jax.random.randint(jax.random.fold_in(_rk, 8), (4,), 0, max(1, 256 // 4) + 1, jnp.int32)
        _ctx_512P = jax.random.normal(jax.random.fold_in(_rk, 11), (4, 16, 64), jnp.float32)
        _ctx_512c = jax.random.dirichlet(jax.random.fold_in(_rk, 511), 0.3 * jnp.ones((16,), jnp.float32), (4, 256))
        _ctx_512t = jnp.einsum('bsk,bkd->bsd', _ctx_512c, _ctx_512P)
        _ctx_512t = _ctx_512t * jax.lax.rsqrt(jnp.mean(jnp.square(_ctx_512t)) + 1e-12) * 0.953939
        ctx_512 = 2.81802e-05 + 1.00001 * (_ctx_512t + 0.3 * jax.random.normal(jax.random.fold_in(_rk, 611), (4, 256, 64), jnp.float32))
        return (x, ctx_512)
    x, ctx_512 = _rec_inputs()

    def _L0_attn_setup():
        import jax, jax.numpy as jnp
        import numpy as np
        import math
        D_MODEL = 256
        NUM_HEAD = 16
        HEAD_DIM = D_MODEL // NUM_HEAD

        def _trunc_normal(key, shape, std):
            return jax.random.truncated_normal(key, -3.0, 3.0, shape, dtype=jnp.float32) * std
        key = jax.random.key(seed)
        kx, kp, ko = jax.random.split(key, 3)
        b, s = (4, 256)
        x = jax.random.normal(kx, (b, s, D_MODEL), dtype=jnp.float32)
        sigma_p = math.sqrt(2.0 / (D_MODEL + 3 * D_MODEL))
        w_project = _trunc_normal(kp, (3 * D_MODEL, D_MODEL), sigma_p)
        sigma_o = math.sqrt(2.0 / (D_MODEL + D_MODEL))
        w_out = _trunc_normal(ko, (D_MODEL, D_MODEL), sigma_o)
        return {'x': x, 'w_project': w_project, 'w_out': w_out}
    _L0_attn_all = _L0_attn_setup()
    _L0_attn_in = {k: v for k, v in _L0_attn_all.items() if k in ('w_project', 'w_out')}
    del _L0_attn_all

    def _L0_xattn_setup():
        import jax, jax.numpy as jnp
        import numpy as np
        EPS = 1e-06
        IMAGE_DIMS = 256
        key = jax.random.key(seed)
        k1, k2, k3 = jax.random.split(key, 3)
        B, I, J, D = (16, 256, 256, 64)
        p = jax.random.normal(k1, (B, I, J), dtype=jnp.float32)
        k_v = jax.random.normal(k2, (B, J, D), dtype=jnp.float32)
        W_k = jax.random.normal(k3, (D, D), dtype=jnp.float32) * (1.0 / np.sqrt(D))
        b_k = jnp.zeros((D,), dtype=jnp.float32)
        ln_gamma = jnp.ones((J,), dtype=jnp.float32)
        ln_beta = jnp.zeros((J,), dtype=jnp.float32)
        return {'p': p, 'k_v': k_v, 'W_k': W_k, 'b_k': b_k, 'ln_gamma': ln_gamma, 'ln_beta': ln_beta}
    _L0_xattn_all = _L0_xattn_setup()
    _L0_xattn_in = {k: v for k, v in _L0_xattn_all.items() if k in ('W_k', 'b_k', 'ln_gamma', 'ln_beta')}
    del _L0_xattn_all

    def _L0_ffn_setup():
        import jax, jax.numpy as jnp
        import numpy as np
        D_MODEL = 256
        D_FF = 1024
        GSIZE = 64
        ACT_BITS = 8
        QB = 2 ** (ACT_BITS - 1) - 1
        EPS = 1e-05

        def _ste(x, q):
            return x + jax.lax.stop_gradient(q - x)

        def _quant_weight_1b(w):
            scale = jnp.mean(jnp.abs(w))
            return _ste(w, jnp.sign(w) * scale)

        def _quant_act(x):
            shp = x.shape
            xg = x.reshape(shp[:-1] + (shp[-1] // GSIZE, GSIZE))
            s = jnp.clip(jnp.max(jnp.abs(xg), axis=-1, keepdims=True), EPS, None)
            q = jnp.round(jnp.clip(xg * (QB / s), -QB, QB)) * (s / QB)
            return _ste(x, q.reshape(shp))

        def _bitlinear(x, w):
            return _quant_act(x) @ _quant_weight_1b(w).T
        key = jax.random.key(seed)
        kx, k1, k2, k3 = jax.random.split(key, 4)
        x = jax.random.normal(kx, (4, 256, D_MODEL), dtype=jnp.float32)
        w1 = jax.random.normal(k1, (D_FF, D_MODEL), dtype=jnp.float32) * 0.02
        w2 = jax.random.normal(k2, (D_FF, D_MODEL), dtype=jnp.float32) * 0.02
        w3 = jax.random.normal(k3, (D_MODEL, D_FF), dtype=jnp.float32) * 0.02
        return {'x': x, 'w1': w1, 'w2': w2, 'w3': w3}
    _L0_ffn_all = _L0_ffn_setup()
    _L0_ffn_in = {k: v for k, v in _L0_ffn_all.items() if k in ('w1', 'w2', 'w3')}
    del _L0_ffn_all

    def _L1_attn_setup():
        import jax, jax.numpy as jnp
        import numpy as np
        B, T, C = (2, 256, 256)
        NH, NKV = (16, 4)
        HD = C // NH

        def _rope(x):
            D = x.shape[-1]
            t = x.shape[-2]
            inv_freq = 1.0 / 10000.0 ** (jnp.arange(0, D, 2, dtype=jnp.float32) / D)
            freqs = jnp.arange(t, dtype=jnp.float32)[:, None] * inv_freq[None, :]
            emb = jnp.concatenate([freqs, freqs], axis=-1)
            cos, sin = (jnp.cos(emb), jnp.sin(emb))
            x1, x2 = (x[..., :D // 2], x[..., D // 2:])
            rotated = jnp.concatenate([-x2, x1], axis=-1)
            return x * cos + rotated * sin
        key = jax.random.key(seed)
        ks = jax.random.split(key, 5)
        w = lambda k, shape: jax.random.normal(k, shape, jnp.float32) * 0.02
        return {'x': jax.random.normal(ks[0], (B, T, C), jnp.float32), 'Wq': w(ks[1], (C, C)), 'Wk': w(ks[2], (C, NKV * HD)), 'Wv': w(ks[3], (C, NKV * HD)), 'Wproj': w(ks[4], (C, C))}
    _L1_attn_all = _L1_attn_setup()
    _L1_attn_in = {k: v for k, v in _L1_attn_all.items() if k in ('Wq', 'Wk', 'Wv', 'Wproj')}
    del _L1_attn_all

    def _L1_xattn_setup():
        import jax, jax.numpy as jnp
        import numpy as np
        B, S, L = (2, 128, 128)
        DIM_Q, H, K, D_C, D_CQ, R = (256, 16, 128, 64, 192, 64)

        def _rope_tables(length, dim):
            inv = 1.0 / 10000.0 ** (jnp.arange(0, dim, 2, dtype=jnp.float32) / dim)
            f = jnp.arange(length, dtype=jnp.float32)[:, None] * inv[None, :]
            sin = jnp.repeat(jnp.sin(f), 2, axis=-1)
            cos = jnp.repeat(jnp.cos(f), 2, axis=-1)
            return (sin, cos)

        def _rotate_half(x):
            half = x.shape[-1] // 2
            return jnp.concatenate([-x[..., half:], x[..., :half]], axis=-1)

        def _apply_rope(x, sin, cos):
            return x * cos + _rotate_half(x) * sin
        key = jax.random.key(seed)
        ks = jax.random.split(key, 8)
        return {'hidden_q': jax.random.normal(ks[0], (B, S, DIM_Q), jnp.float32), 'kv_c': jax.random.normal(ks[1], (B, L, D_C), jnp.float32), 'Wq': jax.random.normal(ks[2], (H * K, DIM_Q), jnp.float32) / np.sqrt(DIM_Q).astype(np.float32), 'w_kc_q': jax.random.normal(ks[3], (H, K, D_CQ), jnp.float32) / np.sqrt(K).astype(np.float32), 'w_kc_kv': jax.random.normal(ks[4], (H, K, D_C), jnp.float32) / np.sqrt(K).astype(np.float32), 'W_qr': jax.random.normal(ks[5], (H, D_CQ, R), jnp.float32) / np.float32(np.sqrt(D_CQ) * np.sqrt(R)), 'W_kr': jax.random.normal(ks[6], (H, D_C, R), jnp.float32) / np.sqrt(D_C).astype(np.float32), 'Wo': jax.random.normal(ks[7], (DIM_Q, H * K), jnp.float32) / np.sqrt(H * K).astype(np.float32)}
    _L1_xattn_all = _L1_xattn_setup()
    _L1_xattn_in = {k: v for k, v in _L1_xattn_all.items() if k in ('Wq', 'w_kc_q', 'w_kc_kv', 'W_qr', 'W_kr', 'Wo')}
    del _L1_xattn_all

    def _L1_ffn_setup():
        import jax, jax.numpy as jnp
        import numpy as np
        E = 32
        K = 4
        G = 4
        TG = 2
        H = 256
        F = 128
        FS = 256
        SCALE = 2.0
        B, S = (2, 128)
        N = B * S
        CAP = 2 * (N * K // E)

        def _gate(x, gate_w, gate_bias):
            logits = x @ gate_w.T
            scores = jax.nn.sigmoid(logits)
            sc = scores + gate_bias
            n = x.shape[0]
            grp = sc.reshape(n, G, E // G)
            group_scores = jax.lax.top_k(grp, 2)[0].sum(-1)
            _, gidx = jax.lax.top_k(group_scores, TG)
            gmask = jnp.zeros((n, G), sc.dtype).at[jnp.arange(n)[:, None], gidx].set(1.0)
            smask = jnp.repeat(gmask, E // G, axis=1)
            tmp = jnp.where(smask > 0, sc, 0.0)
            _, topk_idx = jax.lax.top_k(tmp, K)
            topk_w = jnp.take_along_axis(scores, topk_idx, axis=1)
            topk_w = topk_w / (topk_w.sum(-1, keepdims=True) + 1e-20)
            return (topk_idx, topk_w * SCALE)

        def _moe(x, topk_idx, topk_w, w1, w2, w3):
            n = x.shape[0]
            flat_e = topk_idx.reshape(-1)
            oh = jax.nn.one_hot(flat_e, E, dtype=jnp.int32)
            pos = (jnp.cumsum(oh, axis=0) * oh).sum(-1) - 1
            keep = pos < CAP
            slot = jnp.where(keep, pos, CAP)
            x_rep = jnp.repeat(x, K, axis=0)
            buf = jnp.zeros((E, CAP, H), x.dtype).at[flat_e, slot].set(x_rep, mode='drop')
            h = jax.nn.silu(jnp.einsum('ech,ehf->ecf', buf, w1)) * jnp.einsum('ech,ehf->ecf', buf, w3)
            ob = jnp.einsum('ecf,efh->ech', h, w2)
            y = ob[flat_e, jnp.minimum(slot, CAP - 1)]
            y = jnp.where(keep[:, None], y, 0.0)
            return (y.reshape(n, K, H) * topk_w[:, :, None]).sum(1)
        key = jax.random.key(seed)
        ks = jax.random.split(key, 9)
        w = 0.02
        return {'hidden_states': jax.random.normal(ks[0], (B, S, H), jnp.float32), 'gate_w': jax.random.normal(ks[1], (E, H), jnp.float32) * w, 'gate_bias': jax.random.normal(ks[2], (E,), jnp.float32) * w, 'w1': jax.random.normal(ks[3], (E, H, F), jnp.float32) * w, 'w2': jax.random.normal(ks[4], (E, F, H), jnp.float32) * w, 'w3': jax.random.normal(ks[5], (E, H, F), jnp.float32) * w, 'shared_gate': jax.random.normal(ks[6], (H, FS), jnp.float32) * w, 'shared_up': jax.random.normal(ks[7], (H, FS), jnp.float32) * w, 'shared_down': jax.random.normal(ks[8], (FS, H), jnp.float32) * w}
    _L1_ffn_all = _L1_ffn_setup()
    _L1_ffn_in = {k: v for k, v in _L1_ffn_all.items() if k in ('gate_w', 'gate_bias', 'w1', 'w2', 'w3', 'shared_gate', 'shared_up', 'shared_down')}
    del _L1_ffn_all
    return {'x': x, 'ctx_512': ctx_512, 'L0_attn_w_project': _L0_attn_in['w_project'], 'L0_attn_w_out': _L0_attn_in['w_out'], 'L0_xattn_W_k': _L0_xattn_in['W_k'], 'L0_xattn_b_k': _L0_xattn_in['b_k'], 'L0_xattn_ln_gamma': _L0_xattn_in['ln_gamma'], 'L0_xattn_ln_beta': _L0_xattn_in['ln_beta'], 'L0_ffn_w1': _L0_ffn_in['w1'], 'L0_ffn_w2': _L0_ffn_in['w2'], 'L0_ffn_w3': _L0_ffn_in['w3'], 'L1_attn_Wq': _L1_attn_in['Wq'], 'L1_attn_Wk': _L1_attn_in['Wk'], 'L1_attn_Wv': _L1_attn_in['Wv'], 'L1_attn_Wproj': _L1_attn_in['Wproj'], 'L1_xattn_Wq': _L1_xattn_in['Wq'], 'L1_xattn_w_kc_q': _L1_xattn_in['w_kc_q'], 'L1_xattn_w_kc_kv': _L1_xattn_in['w_kc_kv'], 'L1_xattn_W_qr': _L1_xattn_in['W_qr'], 'L1_xattn_W_kr': _L1_xattn_in['W_kr'], 'L1_xattn_Wo': _L1_xattn_in['Wo'], 'L1_ffn_gate_w': _L1_ffn_in['gate_w'], 'L1_ffn_gate_bias': _L1_ffn_in['gate_bias'], 'L1_ffn_w1': _L1_ffn_in['w1'], 'L1_ffn_w2': _L1_ffn_in['w2'], 'L1_ffn_w3': _L1_ffn_in['w3'], 'L1_ffn_shared_gate': _L1_ffn_in['shared_gate'], 'L1_ffn_shared_up': _L1_ffn_in['shared_up'], 'L1_ffn_shared_down': _L1_ffn_in['shared_down']}

def reference(x, ctx_512, L0_attn_w_project, L0_attn_w_out, L0_xattn_W_k, L0_xattn_b_k, L0_xattn_ln_gamma, L0_xattn_ln_beta, L0_ffn_w1, L0_ffn_w2, L0_ffn_w3, L1_attn_Wq, L1_attn_Wk, L1_attn_Wv, L1_attn_Wproj, L1_xattn_Wq, L1_xattn_w_kc_q, L1_xattn_w_kc_kv, L1_xattn_W_qr, L1_xattn_W_kr, L1_xattn_Wo, L1_ffn_gate_w, L1_ffn_gate_bias, L1_ffn_w1, L1_ffn_w2, L1_ffn_w3, L1_ffn_shared_gate, L1_ffn_shared_up, L1_ffn_shared_down):
    import jax
    import jax.numpy as jnp

    def _L0_attn_ref(x, w_project, w_out):
        import jax, jax.numpy as jnp
        import numpy as np
        import math
        D_MODEL = 256
        NUM_HEAD = 16
        HEAD_DIM = D_MODEL // NUM_HEAD

        def _trunc_normal(key, shape, std):
            return jax.random.truncated_normal(key, -3.0, 3.0, shape, dtype=jnp.float32) * std
        b, s, d = x.shape
        qkv = jnp.einsum('bsd,od->bso', x, w_project)
        qkv = qkv.reshape(b, s, 3, NUM_HEAD, HEAD_DIM)
        qkv = jnp.transpose(qkv, (2, 0, 3, 1, 4))
        q, k, v = (qkv[0], qkv[1], qkv[2])
        att = jnp.einsum('bhqd,bhkd->bhqk', q, k) / math.sqrt(HEAD_DIM)
        causal = jnp.triu(jnp.ones((s, s), dtype=bool), k=1)
        att = jnp.where(causal[None, None, :, :], jnp.float32(-1000000000.0), att)
        att = jax.nn.softmax(att, axis=-1)
        out = jnp.einsum('bhqk,bhkd->bhqd', att, v)
        out = jnp.transpose(out, (0, 2, 1, 3)).reshape(b, s, d)
        return jnp.einsum('bsd,od->bso', out, w_out)

    def _L0_xattn_ref(p, k_v, W_k, b_k, ln_gamma, ln_beta):
        import jax, jax.numpy as jnp
        import numpy as np
        EPS = 1e-06
        IMAGE_DIMS = 256
        kv = k_v @ W_k.T + b_k
        out = jnp.einsum('bij,bjd->bid', p, kv)
        scale = IMAGE_DIMS ** (-0.5)
        sim = jnp.einsum('bid,bjd->bij', out, kv) * scale
        mu = jnp.mean(sim, axis=-1, keepdims=True)
        var = jnp.var(sim, axis=-1, keepdims=True)
        sim = (sim - mu) * jax.lax.rsqrt(var + EPS) * ln_gamma + ln_beta
        attn = jax.nn.softmax(sim, axis=-1)
        return attn

    def _L0_ffn_ref(x, w1, w2, w3):
        import jax, jax.numpy as jnp
        import numpy as np
        D_MODEL = 256
        D_FF = 1024
        GSIZE = 64
        ACT_BITS = 8
        QB = 2 ** (ACT_BITS - 1) - 1
        EPS = 1e-05

        def _ste(x, q):
            return x + jax.lax.stop_gradient(q - x)

        def _quant_weight_1b(w):
            scale = jnp.mean(jnp.abs(w))
            return _ste(w, jnp.sign(w) * scale)

        def _quant_act(x):
            shp = x.shape
            xg = x.reshape(shp[:-1] + (shp[-1] // GSIZE, GSIZE))
            s = jnp.clip(jnp.max(jnp.abs(xg), axis=-1, keepdims=True), EPS, None)
            q = jnp.round(jnp.clip(xg * (QB / s), -QB, QB)) * (s / QB)
            return _ste(x, q.reshape(shp))

        def _bitlinear(x, w):
            return _quant_act(x) @ _quant_weight_1b(w).T
        h = jax.nn.silu(_bitlinear(x, w1)) * _bitlinear(x, w2)
        return _bitlinear(h, w3)

    def _L1_attn_ref(x, Wq, Wk, Wv, Wproj):
        import jax, jax.numpy as jnp
        import numpy as np
        B, T, C = (2, 256, 256)
        NH, NKV = (16, 4)
        HD = C // NH

        def _rope(x):
            D = x.shape[-1]
            t = x.shape[-2]
            inv_freq = 1.0 / 10000.0 ** (jnp.arange(0, D, 2, dtype=jnp.float32) / D)
            freqs = jnp.arange(t, dtype=jnp.float32)[:, None] * inv_freq[None, :]
            emb = jnp.concatenate([freqs, freqs], axis=-1)
            cos, sin = (jnp.cos(emb), jnp.sin(emb))
            x1, x2 = (x[..., :D // 2], x[..., D // 2:])
            rotated = jnp.concatenate([-x2, x1], axis=-1)
            return x * cos + rotated * sin
        b, t, c = x.shape
        q = (x @ Wq).reshape(b, t, NH, HD).transpose(0, 2, 1, 3)
        k = (x @ Wk).reshape(b, t, NKV, HD).transpose(0, 2, 1, 3)
        v = (x @ Wv).reshape(b, t, NKV, HD).transpose(0, 2, 1, 3)
        q = _rope(q)
        k = _rope(k)
        rep = NH // NKV
        k = jnp.repeat(k, rep, axis=1)
        v = jnp.repeat(v, rep, axis=1)
        scale = 1.0 / jnp.sqrt(jnp.float32(HD))
        scores = jnp.einsum('bhqd,bhkd->bhqk', q, k) * scale
        causal = jnp.tril(jnp.ones((t, t), dtype=bool))
        scores = jnp.where(causal, scores, jnp.finfo(scores.dtype).min)
        attn = jax.nn.softmax(scores, axis=-1)
        y = jnp.einsum('bhqk,bhkd->bhqd', attn, v)
        y = y.transpose(0, 2, 1, 3).reshape(b, t, c)
        return y @ Wproj

    def _L1_xattn_ref(hidden_q, kv_c, Wq, w_kc_q, w_kc_kv, W_qr, W_kr, Wo):
        import jax, jax.numpy as jnp
        import numpy as np
        B, S, L = (2, 128, 128)
        DIM_Q, H, K, D_C, D_CQ, R = (256, 16, 128, 64, 192, 64)

        def _rope_tables(length, dim):
            inv = 1.0 / 10000.0 ** (jnp.arange(0, dim, 2, dtype=jnp.float32) / dim)
            f = jnp.arange(length, dtype=jnp.float32)[:, None] * inv[None, :]
            sin = jnp.repeat(jnp.sin(f), 2, axis=-1)
            cos = jnp.repeat(jnp.cos(f), 2, axis=-1)
            return (sin, cos)

        def _rotate_half(x):
            half = x.shape[-1] // 2
            return jnp.concatenate([-x[..., half:], x[..., :half]], axis=-1)

        def _apply_rope(x, sin, cos):
            return x * cos + _rotate_half(x) * sin
        Bv, Sv, _ = hidden_q.shape
        _, Lv, _ = kv_c.shape
        q_hk = (hidden_q @ Wq.T).reshape(Bv, Sv, H, K)
        q_big = jnp.einsum('bshk,hkq->bshq', q_hk, w_kc_q)
        sin_q, cos_q = _rope_tables(Sv, D_CQ)
        q_big = _apply_rope(q_big, sin_q[None, :, None, :], cos_q[None, :, None, :])
        sin_k, cos_k = _rope_tables(Lv, D_C)
        kv_r = _apply_rope(kv_c, sin_k[None], cos_k[None])
        q_r = jnp.einsum('bshq,hqr->bhsr', q_big, W_qr)
        k_r = jnp.einsum('bld,hdr->bhlr', kv_r, W_kr)
        scores = jnp.einsum('bhsr,bhlr->bhsl', q_r, k_r)
        attn = jax.nn.softmax(scores, axis=-1)
        ctx_c = jnp.einsum('bhsl,bld->bhsd', attn, kv_r)
        ctx_lat = jnp.einsum('bhsd,hkd->bhsk', ctx_c, w_kc_kv)
        ctx = ctx_lat.transpose(0, 2, 1, 3).reshape(Bv, Sv, H * K)
        return ctx @ Wo.T

    def _L1_ffn_ref(hidden_states, gate_w, gate_bias, w1, w2, w3, shared_gate, shared_up, shared_down):
        import jax, jax.numpy as jnp
        import numpy as np
        E = 32
        K = 4
        G = 4
        TG = 2
        H = 256
        F = 128
        FS = 256
        SCALE = 2.0
        B, S = (2, 128)
        N = B * S
        CAP = 2 * (N * K // E)

        def _gate(x, gate_w, gate_bias):
            logits = x @ gate_w.T
            scores = jax.nn.sigmoid(logits)
            sc = scores + gate_bias
            n = x.shape[0]
            grp = sc.reshape(n, G, E // G)
            group_scores = jax.lax.top_k(grp, 2)[0].sum(-1)
            _, gidx = jax.lax.top_k(group_scores, TG)
            gmask = jnp.zeros((n, G), sc.dtype).at[jnp.arange(n)[:, None], gidx].set(1.0)
            smask = jnp.repeat(gmask, E // G, axis=1)
            tmp = jnp.where(smask > 0, sc, 0.0)
            _, topk_idx = jax.lax.top_k(tmp, K)
            topk_w = jnp.take_along_axis(scores, topk_idx, axis=1)
            topk_w = topk_w / (topk_w.sum(-1, keepdims=True) + 1e-20)
            return (topk_idx, topk_w * SCALE)

        def _moe(x, topk_idx, topk_w, w1, w2, w3):
            n = x.shape[0]
            flat_e = topk_idx.reshape(-1)
            oh = jax.nn.one_hot(flat_e, E, dtype=jnp.int32)
            pos = (jnp.cumsum(oh, axis=0) * oh).sum(-1) - 1
            keep = pos < CAP
            slot = jnp.where(keep, pos, CAP)
            x_rep = jnp.repeat(x, K, axis=0)
            buf = jnp.zeros((E, CAP, H), x.dtype).at[flat_e, slot].set(x_rep, mode='drop')
            h = jax.nn.silu(jnp.einsum('ech,ehf->ecf', buf, w1)) * jnp.einsum('ech,ehf->ecf', buf, w3)
            ob = jnp.einsum('ecf,efh->ech', h, w2)
            y = ob[flat_e, jnp.minimum(slot, CAP - 1)]
            y = jnp.where(keep[:, None], y, 0.0)
            return (y.reshape(n, K, H) * topk_w[:, :, None]).sum(1)
        b, s, h = hidden_states.shape
        x = hidden_states.reshape(-1, h)
        topk_idx, topk_w = _gate(x, gate_w, gate_bias)
        out = _moe(x, topk_idx, topk_w, w1, w2, w3)
        shared = jax.nn.silu(x @ shared_gate) * (x @ shared_up) @ shared_down
        return (out + shared).reshape(b, s, h)
    x = x + _L0_attn_ref(_layernorm(x, axis=-1), L0_attn_w_project, L0_attn_w_out)
    x = x + _L0_xattn_ref(_layernorm(x, axis=-1), ctx_512, L0_xattn_W_k, L0_xattn_b_k, L0_xattn_ln_gamma, L0_xattn_ln_beta)
    x = x + _L0_ffn_ref(_layernorm(x, axis=-1), L0_ffn_w1, L0_ffn_w2, L0_ffn_w3)
    x = x + _L1_attn_ref(_layernorm(x, axis=-1), L1_attn_Wq, L1_attn_Wk, L1_attn_Wv, L1_attn_Wproj)
    x = x + _L1_xattn_ref(_layernorm(x, axis=-1), ctx_512, L1_xattn_Wq, L1_xattn_w_kc_q, L1_xattn_w_kc_kv, L1_xattn_W_qr, L1_xattn_W_kr, L1_xattn_Wo)
    x = x + _L1_ffn_ref(_layernorm(x, axis=-1), L1_ffn_gate_w, L1_ffn_gate_bias, L1_ffn_w1, L1_ffn_w2, L1_ffn_w3, L1_ffn_shared_gate, L1_ffn_shared_up, L1_ffn_shared_down)
    return x

_drawn_inputs = setup_inputs


def setup_inputs(seed=0):
    import zlib

    import numpy as np

    out = dict(_drawn_inputs(seed))
    spreads = {'L0_xattn_b_k': (0.0, 0.8),
     'L0_xattn_ln_gamma': (1.0, 0.6),
     'L0_xattn_ln_beta': (0.0, 0.8)}
    factors = {'L0_xattn_W_k': 8.0,
     'L0_ffn_w1': 3.088,
     'L0_ffn_w2': 2.787,
     'L0_ffn_w3': 2.79,
     'L1_attn_Wq': 8.0,
     'L1_attn_Wk': 8.0,
     'L1_attn_Wv': 2.831,
     'L1_attn_Wproj': 2.92,
     'L1_ffn_gate_w': 7.36,
     'L1_ffn_gate_bias': 8.0,
     'L1_ffn_w1': 7.07,
     'L1_ffn_w2': 6.975,
     'L1_ffn_w3': 6.983,
     'L1_ffn_shared_gate': 3.592,
     'L1_ffn_shared_up': 3.569,
     'L1_ffn_shared_down': 3.533}
    for name, (base, spread) in spreads.items():
        noise = np.random.default_rng([zlib.crc32(name.encode()), seed]).standard_normal(out[name].shape)
        drawn = base * np.exp(spread * noise) if base else spread * noise
        out[name] = jnp.asarray(drawn.astype(out[name].dtype))
    for name, factor in factors.items():
        out[name] = (out[name] * factor).astype(out[name].dtype)
    return out
```

```python
from contextlib import ExitStack

import concourse.bass as bass
from concourse import mybir

F32 = mybir.dt.float32
BF16 = mybir.dt.bfloat16
U32 = mybir.dt.uint32
ALU = mybir.AluOpType
ACT = mybir.ActivationFunctionType
AX = mybir.AxisListType

P = 128
D = 256
NB = 4
SEQ = 256
KD = D // P
NT = NB * SEQ // P
NH = 16
HD = D // NH
PAIRS = NH // 2
FF = 1024
GRP = 64
QB = 127.0
ROUND = 12582912.0
DC = 64
CQ = 192
HC = CQ // 2
NE = 32
TOPK = 4
NG = 4
EG = NE // NG
FE = 128
FS = 256
CAP = 2 * (2 * 128 * TOPK // NE)
EC = 8
NC = NE // EC
SLOTS = EC * CAP
KS = SLOTS // P
STAGES = 6


class Steps:

    def __init__(self, eng, sem):
        self.eng, self.sem, self.done, self.shift = eng, sem, 0, 0

    def mark(self, ins):
        ins.then_inc(self.sem, 1)
        self.done += 1

    def wait(self):
        self.eng.wait_ge(self.sem, self.shift + self.done)

    def wait_apart(self, scrap):
        self.wait()
        self.eng.memset(scrap, 0.0)

    def loop(self, i, first, per):
        self.shift, self.done, self.first, self.per = i * per + first, 0, first, per

    def end(self, count, name):
        assert self.done == self.per, (name, "increments in an iteration:", self.done)
        self.shift, self.done = 0, self.first + count * self.per


def build(nc, a, out):
    ctx = ExitStack()
    with ctx:
        def sb(name, shape, dt=F32):
            return ctx.enter_context(nc.sbuf_tensor(name, shape, dt))

        def sem(name):
            return ctx.enter_context(nc.semaphore(name))

        bank = ctx.enter_context(nc.psum_tensor("bank", [P, 8, 512], F32))
        X = sb("X", [P, NT, D])
        ident = sb("ident", [P, P])
        ident_h = sb("ident_h", [P, P], BF16)
        causal = sb("causal", [P, P])
        causal_h = sb("causal_h", [P, P], BF16)
        parity = sb("parity", [P, 2])
        ones = sb("ones", [P, P])
        halfneg = sb("halfneg", [P, 2])
        epsilons = sb("epsilons", [P, 4])
        scrap = sb("scrap", [P, 1])
        stat = sb("stat", [P, 2, 6])
        mv = sb("mv", [P, 2, 2])
        veps = sb("veps", [P, 2])
        rstd = sb("rstd", [P, 2])
        xn = sb("xn", [P, 2, D])
        xnT = sb("xnT", [P, KD, SEQ])
        wqkv1 = sb("wqkv1", [P, KD, 384])
        wo1 = sb("wo1", [P, KD, D])
        cos1 = sb("cos1", [P, 2, HD])
        sin1 = sb("sin1", [P, 2, HD])
        qT = sb("qT", [P, KD, SEQ])
        kT = sb("kT", [P, 2, KD, SEQ])
        V = sb("V", [P, 2, D])
        nmax = sb("nmax", [P, 2, 4])
        sums = sb("sums", [P, 2, NH])
        rsum = sb("rsum", [P, 2, NH])
        work = sb("work", [P, 14 * 512])
        prob = work[:, 0:1536].rearrange("p (i e k n) -> p i e k n", i=2, e=2, k=3)
        probT = work[:, 1536:3072].rearrange("p (i m n) -> p i m n", i=2, m=6)
        On = sb("On", [P, 2, D])
        OT = sb("OT", [P, KD, SEQ])
        qk_c = work[:, 3072:3712].rearrange("p (r n) -> p r n", r=2)
        qk_s = work[:, 3712:4352].rearrange("p (r n) -> p r n", r=2)
        q_r = work[:, 4352:4864].rearrange("p (r n) -> p r n", r=2)
        k_r = work[:, 4864:5376].rearrange("p (r n) -> p r n", r=2)
        ctxT = sb("ctxT", [DC, NB, SEQ])
        ctxk = sb("ctxk", [P, NT, DC])
        wk = sb("wk", [DC, DC])
        bk_col = sb("bk_col", [DC, 1])
        bk_row = sb("bk_row", [P, DC])
        gamma = sb("gamma", [P, D])
        beta = sb("beta", [P, D])
        ctb = sb("ctb", [DC, SEQ])
        kvT = sb("kvT", [DC, SEQ])
        kvj = sb("kvj", [P, 2, DC])
        outT = sb("outT", [DC, SEQ])
        simn = work[:, 0:512].rearrange("p (r n) -> p r n", r=2)
        simg = work[:, 512:1024].rearrange("p (r n) -> p r n", r=2)
        prob_x = work[:, 1024:1536].rearrange("p (r n) -> p r n", r=2)
        early = sb("early", [P, 2 * EC * 768])
        wqkv0 = early[:, 0:1536].rearrange("p (k n) -> p k n", k=KD)
        wo0 = early[:, 1536:2048].rearrange("p (k n) -> p k n", k=KD)
        w_ff = early[:, 2048:2048 + 6144]
        s1 = w_ff[:, 0:2048].rearrange("p (k n) -> p k n", k=KD)
        s2 = w_ff[:, 2048:4096].rearrange("p (k n) -> p k n", k=KD)
        s3 = w_ff[:, 4096:6144].rearrange("p (k n) -> p k n", k=FF // P)
        Aq = early[:, 0:6144].rearrange("p (h k n) -> p h k n", h=NH, k=KD)
        Gq = early[0:HC, 6144:8192].rearrange("p (h f n) -> p h f n", h=NH, f=2)
        Cx = early[:, 8192:10240].rearrange("p (j n) -> p j n", j=PAIRS)
        hot = early[:, 0:4096].rearrange("p (t n) -> p t n", t=NT)
        hotw = early[:, 4096:8192].rearrange("p (t n) -> p t n", t=NT)
        hotT = early[:, 8192:12288].rearrange("p (t k n) -> p t k n", t=NT, k=KS)
        wabs = sb("wabs", [P, 3])
        wmean = sb("wmean", [P, 3])
        gmax = sb("gmax", [P, 2, 16])
        grcp = sb("grcp", [P, 2, 16])
        gscl = sb("gscl", [P, 2, 16])
        xq = xn
        gate_f = work[:, 0:2048].rearrange("p (r n) -> p r n", r=2)
        hid = work[:, 2048:4096].rearrange("p (r n) -> p r n", r=2)
        hidT = work[:, 4096:6144].rearrange("p (r m n) -> p r m n", r=2, m=8)
        raw = sb("raw", [P, 16384])
        wq_x = raw[:, 0:4096].rearrange("p (h n) -> p h n", h=NH)
        wcq = raw[:, 4096:7168].rearrange("p (h n) -> p h n", h=NH)
        wckv = raw[:, 7168:8192].rearrange("p (h n) -> p h n", h=NH)
        wo_x = raw[:, 8192:12288].rearrange("p (h n) -> p h n", h=NH)
        wqr = raw[0:64, 12288:15360].rearrange("p (h n) -> p h n", h=NH)
        wkr = raw[0:64, 15360:16384].rearrange("p (h n) -> p h n", h=NH)
        cosq = sb("cosq", [HC, 2, SEQ])
        sinq = sb("sinq", [HC, 2, SEQ])
        cosk = sb("cosk", [P, 2, DC])
        sink = sb("sink", [P, 2, DC])
        kvr = sb("kvr", [P, 2, DC])
        kvrT = sb("kvrT", [DC, SEQ])
        kv_c = work[:, 0:128].rearrange("p (r n) -> p r n", r=2)
        kv_s = work[:, 128:256].rearrange("p (r n) -> p r n", r=2)
        qx_c = work[0:HC, 256:1280].rearrange("p (i f n) -> p i f n", i=2, f=2)
        qx_s = work[0:HC, 1280:2304].rearrange("p (i f n) -> p i f n", i=2, f=2)
        qx_r = work[0:HC, 2304:3328].rearrange("p (i f n) -> p i f n", i=2, f=2)
        zT = work[0:DC, 3328:3840].rearrange("p (i n) -> p i n", i=2)
        px = work[:, 3840:4864].rearrange("p (i r n) -> p i r n", i=2, r=2)
        pxT = work[:, 4864:5888].rearrange("p (i k n) -> p i k n", i=2, k=2)
        cn = work[:, 5888:6400].rearrange("p (i r n) -> p i r n", i=2, r=2)
        cT = work[:, 6400:6912].rearrange("p (i n) -> p i n", i=2)
        ew = raw[:, 0:12288].rearrange("p (i w n) -> p i w n", i=2, w=3)
        XN = raw[:, 12288:14336].rearrange("p (t n) -> p t n", t=NT)
        bufT = raw[:, 14336:15360].rearrange("p (k n) -> p k n", k=KD)
        ob = raw[:, 15360:16384].rearrange("p (k n) -> p k n", k=KS)
        gw = sb("gw", [P, KD, NE])
        gbias = sb("gbias", [P, NE])
        sg = sb("sg", [P, KD, FS])
        su = sb("su", [P, KD, FS])
        sd = sb("sd", [P, KD, D])
        later = sb("later", [P, 128 + 32 + 64 + 16])
        before = later[:, 0:128]
        iota_e = later[:, 128:160]
        iota_s = later[:, 160:224]
        earlier = later[:, 224:240]
        sh_g = work[:, 0:512].rearrange("p (f n) -> p f n", f=2)
        sh_h = work[:, 512:1024].rearrange("p (f n) -> p f n", f=2)
        h_g = work[:, 0:512]
        h_T = work[:, 512:1024]
        lg = sb("lg", [P, NT, NE])
        sc = work[:, 1024:1280].rearrange("p (t e) -> p t e", t=NT)
        scb = work[:, 1280:1536].rearrange("p (t e) -> p t e", t=NT)
        top_g = work[:, 1536:1792].rearrange("p (g n) -> p g n", g=NT * NG)
        gs = work[:, 1792:1824].rearrange("p (t g) -> p t g", t=NT)
        cmp_a = work[:, 1824:1952].rearrange("p (t g k) -> p t g k", t=NT, g=NG)
        cmp_b = work[:, 1952:2080].rearrange("p (t g k) -> p t g k", t=NT, g=NG)
        rank = work[:, 2080:2112]
        tmp_e = work[:, 2112:2368].rearrange("p (t e) -> p t e", t=NT)
        top_e = work[:, 2368:2432].rearrange("p (t k) -> p t k", t=NT)
        idx_f = work[:, 2432:2496].rearrange("p (t k) -> p t k", t=NT)
        pick = work[:, 2496:3520].rearrange("p (t e k) -> p t e k", t=NT, e=NE)
        mask = work[:, 3520:3776].rearrange("p (t e) -> p t e", t=NT)
        seen = work[:, 3776:4032].rearrange("p (t e) -> p t e", t=NT)
        wsum = work[:, 4032:4040]
        wrcp = work[:, 4040:4048]
        wgt = work[:, 4048:4304].rearrange("p (t e) -> p t e", t=NT)
        keep = work[:, 4304:4560].rearrange("p (t e) -> p t e", t=NT)
        posm = work[:, 4560:4816].rearrange("p (t e) -> p t e", t=NT)
        idx_u = sb("idx_u", [P, NT, 8], U32)

        s_x = sem("s_x")
        s_const = sem("s_const")
        s_w0 = sem("s_w0")
        s_ctx = sem("s_ctx")
        s_wff = sem("s_wff")
        s_w1 = sem("s_w1")
        s_wx = sem("s_wx")
        s_wm = sem("s_wm")
        experts_in = [sem(f"experts_in{i}") for i in range(2)]
        s_out = sem("s_out")
        setup = sem("setup")
        casts = sem("casts")
        mv_ready = sem("mv_ready")
        veps_ready = sem("veps_ready")
        rstd_ready = sem("rstd_ready")
        xn_ready = sem("xn_ready")
        xnTp_ready = sem("xnTp_ready")
        xnT_ready = sem("xnT_ready")
        x_done = sem("x_done")
        dve_steps = [sem(f"dve_steps{p}") for p in range(6)]
        proj = [sem(f"proj{l}") for l in range(2)]
        roped = sem("roped")
        rope_back = sem("rope_back")
        q_ready = [sem(f"q_ready{l}") for l in range(2)]
        kv_ready = [sem(f"kv_ready{l}") for l in range(2)]
        v_copied = sem("v_copied")
        s_ready = [sem(f"s_ready{l}") for l in range(2)]
        max_ready = [sem(f"max_ready{l}") for l in range(2)]
        p_ready = [sem(f"p_ready{l}") for l in range(2)]
        pT_psum = [sem(f"pT_psum{l}") for l in range(2)]
        pT_ready = [sem(f"pT_ready{l}") for l in range(2)]
        av_done = [sem(f"av_done{l}") for l in range(2)]
        on_ready = [sem(f"on_ready{l}") for l in range(2)]
        oT_psum = [sem(f"oT_psum{l}") for l in range(2)]
        oT_ready = [sem(f"oT_ready{l}") for l in range(2)]
        y_ready = sem("y_ready")
        ctb_ready = sem("ctb_ready")
        kv_psum = sem("kv_psum")
        kvT_ready = sem("kvT_ready")
        kvj_ready = sem("kvj_ready")
        outT_psum = sem("outT_psum")
        outT_ready = sem("outT_ready")
        sim_ready = sem("sim_ready")
        smv_ready = sem("smv_ready")
        sveps_ready = sem("sveps_ready")
        srstd_ready = sem("srstd_ready")
        smax_pre = sem("smax_pre")
        smax_ready = sem("smax_ready")
        srcp_ready = sem("srcp_ready")
        x_half = sem("x_half")
        sexp_ready = sem("sexp_ready")
        wabs_ready = sem("wabs_ready")
        wmean_psum = sem("wmean_psum")
        sign_ready = sem("sign_ready")
        xq_ready = sem("xq_ready")
        hid_psum = sem("hid_psum")
        gate_ready = sem("gate_ready")
        hid_used = sem("hid_used")
        hq_ready = sem("hq_ready")
        hT_psum = sem("hT_psum")
        hT_ready = sem("hT_ready")
        fold_psum = sem("fold_psum")
        fold_act = sem("fold_act")
        fold_dve = sem("fold_dve")
        ctk_ready = sem("ctk_ready")
        kvr_ready = sem("kvr_ready")
        kvrT_psum = sem("kvrT_psum")
        kvrT_ready = sem("kvrT_ready")
        qx_psum = sem("qx_psum")
        qx_cs = sem("qx_cs")
        qx_ready = sem("qx_ready")
        z_psum = sem("z_psum")
        z_ready = sem("z_ready")
        sx_ready = sem("sx_ready")
        mx_ready = sem("mx_ready")
        px_ready = sem("px_ready")
        pxT_psum = sem("pxT_psum")
        pxT_ready = sem("pxT_ready")
        cx_psum = sem("cx_psum")
        cn_ready = sem("cn_ready")
        cT_psum = sem("cT_psum")
        cT_ready = sem("cT_ready")
        xn_kept = sem("xn_kept")
        lg_psum = sem("lg_psum")
        lg_ready = sem("lg_ready")
        sh_psum = sem("sh_psum")
        shg_ready = sem("shg_ready")
        shh_ready = sem("shh_ready")
        esig_ready = sem("esig_ready")
        mask_ready = sem("mask_ready")
        pos_psum = sem("pos_psum")
        hot_ready = sem("hot_ready")
        hotw_ready = sem("hotw_ready")
        gat_psum = sem("gat_psum")
        buf_ready = sem("buf_ready")
        hotT_psum = sem("hotT_psum")
        hotT_ready = sem("hotT_ready")
        eh_psum = sem("eh_psum")
        eg_ready = sem("eg_ready")
        eh_ready = sem("eh_ready")
        ob_psum = sem("ob_psum")
        ob_ready = sem("ob_ready")
        ey_psum = sem("ey_psum")
        ey_used = sem("ey_used")

        block = ctx.enter_context(nc.Block())

        @block.sync
        def _(sp):
            def load(dst, src, s):
                sp.dma_start(dst, src).then_inc(s, 16)

            load(X[:], a["x"].rearrange("(t p) d -> p t d", p=P), s_x)
            load(ident[:], a["ident"], s_const)
            load(wqkv0, a["w_qkv0"].rearrange("(k p) n -> p k n", p=P), s_w0)
            load(causal[:], a["causal"], s_const)
            load(parity[:], a["parity"], s_const)
            load(wo0, a["w_o0"].rearrange("(k p) n -> p k n", p=P), s_w0)
            load(ctxT[:], a["ctxT"].rearrange("d (b s) -> d b s", b=NB), s_ctx)
            load(ctxk[:], a["ctx"].rearrange("(t p) d -> p t d", p=P), s_ctx)
            load(wk[:], a["w_k"], s_ctx)
            load(bk_col[:], a["b_k"].rearrange("(d o) -> d o", o=1), s_ctx)
            load(bk_row[:], a["b_k"].rearrange("(o d) -> o d", o=1).to_broadcast([P, DC]), s_ctx)
            load(gamma[:], a["gamma"].rearrange("(o d) -> o d", o=1).to_broadcast([P, D]), s_ctx)
            load(beta[:], a["beta"].rearrange("(o d) -> o d", o=1).to_broadcast([P, D]), s_ctx)
            load(s1, a["w_f1"].rearrange("(k p) n -> p k n", p=P), s_wff)
            load(s2, a["w_f2"].rearrange("(k p) n -> p k n", p=P), s_wff)
            load(s3, a["w_f3"].rearrange("(k p) n -> p k n", p=P), s_wff)
            load(wqkv1[:], a["w_qkv1"].rearrange("(k p) n -> p k n", p=P), s_w1)
            load(wo1[:], a["w_o1"].rearrange("(k p) n -> p k n", p=P), s_w1)
            load(cos1[:], a["cos1"].rearrange("(r p) n -> p r n", p=P), s_w1)
            load(sin1[:], a["sin1"].rearrange("(r p) n -> p r n", p=P), s_w1)
            load(wq_x, a["w_xq"].rearrange("(h p) n -> p h n", p=P), s_wx)
            load(wcq, a["w_cq"].rearrange("(h p) n -> p h n", p=P), s_wx)
            load(wckv, a["w_ckv"].rearrange("(h p) n -> p h n", p=P), s_wx)
            load(wo_x, a["w_xo"].rearrange("(h p) n -> p h n", p=P), s_wx)
            load(wqr, a["w_qr"].rearrange("r (h n) -> r h n", h=NH), s_wx)
            load(wkr, a["w_kr"].rearrange("r (h n) -> r h n", h=NH), s_wx)
            load(cosq[:], a["cosq"].rearrange("(f j) s -> j f s", j=HC), s_wx)
            load(sinq[:], a["sinq"].rearrange("(f j) s -> j f s", j=HC), s_wx)
            load(cosk[:], a["cosk"].rearrange("(r p) n -> p r n", p=P), s_wx)
            load(sink[:], a["sink"].rearrange("(r p) n -> p r n", p=P), s_wx)
            load(gw[:], a["w_gate"].rearrange("(k p) n -> p k n", p=P), s_wm)
            load(gbias[:], a["b_gate"].rearrange("(o d) -> o d", o=1).to_broadcast([P, NE]), s_wm)
            load(sg[:], a["w_sg"].rearrange("(k p) n -> p k n", p=P), s_wm)
            load(su[:], a["w_su"].rearrange("(k p) n -> p k n", p=P), s_wm)
            load(sd[:], a["w_sd"].rearrange("(k p) n -> p k n", p=P), s_wm)
            load(later[:], a["later"], s_wm)

            if STAGES > 5:
                sp.wait_ge(fold_act, NH + NH // 4 + PAIRS // 2)
                def load_chunk(i, c):
                    for w in range(3):
                        sp.dma_start(ew[:, i, w, :], a["w_e"][c * P:(c + 1) * P, w * 2048:(w + 1) * 2048]
                                     ).then_inc(experts_in[i], 16)
                load_chunk(0, 0)
                load_chunk(1, 1)
                for c in range(2, NC):
                    sp.wait_ge(ob_psum, c - 1)
                    load_chunk(c % 2, c)
            sp.wait_ge(x_done, NB * STAGES + (NC * NT // 2 if STAGES > 5 else 0))
            sp.dma_start(out.rearrange("(t p) d -> p t d", p=P), X[:]).then_inc(s_out, 16)
            sp.wait_ge(s_out, 16)

        @block.gpsimd
        def _(pool):
            pool.memset(ones[:], 1.0).then_inc(setup, 1)
            pool.memset(halfneg[:], -0.5).then_inc(setup, 1)
            pool.memset(epsilons[:, 0:2], 1e-5).then_inc(setup, 1)
            pool.memset(epsilons[:, 2:4], 1e-6).then_inc(setup, 1)
            pool.wait_ge(setup, 4)

            def rstd_of(n, eps, mv_s, veps_s, rstd_s):
                pool.wait_ge(mv_s, 2 * (n + 1))
                pool.tensor_tensor(veps[:], mv[:, :, 1], epsilons[:, 0:2] if eps == 1e-5 else epsilons[:, 2:4],
                                   ALU.add).then_inc(veps_s, 1)
                pool.wait_ge(veps_s, n + 1)
                pool.tensor_tensor(rstd[:], veps[:], halfneg[:], ALU.pow).then_inc(rstd_s, 1)

            def norm(n):
                rstd_of(n, 1e-5, mv_ready, veps_ready, rstd_ready)

            with pool.Fori(0, NB) as b:
                norm(b)
            if STAGES > 1:
                pool.wait_ge(s_ctx, 7 * 16)
                with pool.Fori(0, NB) as b:
                    pool.tensor_copy(ctb[:].unsqueeze(1), ctxT[:, bass.ts(b, 1), :]).then_inc(ctb_ready, 1)
                    norm(b + NB)
                    rstd_of(b, 1e-6, smv_ready, sveps_ready, srstd_ready)
            if STAGES > 2:
                with pool.Fori(0, NB) as b:
                    norm(b + 2 * NB)
            if STAGES > 3:
                with pool.Fori(0, NB) as b:
                    norm(b + 3 * NB)
            if STAGES > 4:
                with pool.Fori(0, NB) as b:
                    norm(b + 4 * NB)
                    for h in range(NH):
                        pool.wait_ge(qx_cs, b * (2 * NH) + 2 * (h + 1))
                        if h >= 2:
                            pool.wait_ge(z_psum, b * NH + (h - 1))
                        for f in range(2):
                            pool.tensor_tensor(qx_r[:, h % 2, f], qx_c[:, h % 2, f], qx_s[:, h % 2, 1 - f],
                                               ALU.add).then_inc(qx_ready, 1)
            if STAGES > 5:
                with pool.Fori(0, NB) as b:
                    norm(b + 5 * NB)
                    pool.wait_ge(xn_ready, b * 2 + (10 * NB + 2))
                    pool.tensor_copy(XN[:, bass.ts(b, 2), :], xn[:]).then_inc(xn_kept, 1)
                for c in range(NC):
                    for t in range(NT):
                        pool.wait_ge(hot_ready, NT * c + t + 1)
                        if c > 0:
                            pool.wait_ge(hotT_psum, NT * (c - 1) + t + 1)
                        pool.tensor_tensor(hotw[:, t].rearrange("p (e n) -> p e n", e=EC),
                                           hot[:, t].rearrange("p (e n) -> p e n", e=EC),
                                           wgt[:, t, c * EC:(c + 1) * EC].unsqueeze(2).to_broadcast([P, EC, CAP]),
                                           ALU.mult).then_inc(hotw_ready, 1)

        @block.scalar
        def _(act):
            act.preload_act_table(ACT.Exp)

            def copy_xnT(n):
                act.wait_ge(xnTp_ready, n + 1)
                act.activation(xnT[:], bank[:, 7, :].rearrange("p (k n) -> p k n", k=KD), ACT.Copy).then_inc(xnT_ready, 1)

            def attention(l, b):
                copy_xnT(b + 3 * NB * l)
                act.wait_ge(proj[l], (b + 1) if l == 0 else (b * 2 + 2))
                src = bank[:, 0, :] if l == 0 else bank[:, 2, :]
                act.activation(qT[:], src.rearrange("p (k n) -> p k n", k=KD), ACT.Copy,
                               scale=float(HD) ** -0.5).then_inc(q_ready[l], 1)
                for j in range(PAIRS):
                    i = j % 2
                    for r in range(2):
                        act.wait_ge(max_ready[l], b * (2 * PAIRS) + (2 * j + r + 1))
                        if r == 0 and j >= 2:
                            act.wait_ge(pT_psum[l], b * PAIRS + (j - 1))
                        for e in range(2):
                            n = SEQ if r else P
                            dst = prob[:, i, e, 1:3, :].rearrange("p k n -> p (k n)") if r else prob[:, i, e, 0, :]
                            act.activation(dst, bank[:, 2 * i + r, e * n:(e + 1) * n], ACT.Exp,
                                           bias=nmax[:, i, 2 * r + e:2 * r + e + 1],
                                           accum_out=sums[:, r, 2 * j + e:2 * j + e + 1]).then_inc(p_ready[l], 1)
                act.wait_ge(oT_psum[l], b + 1)
                act.activation(OT[:], bank[:, 7, :].rearrange("p (k n) -> p k n", k=KD), ACT.Copy).then_inc(oT_ready[l], 1)

            with act.Fori(0, NB) as b:
                attention(0, b)

            if STAGES > 1:
                with act.Fori(0, NB) as b:
                    copy_xnT(b + NB)
                    act.wait_ge(kv_psum, b + 1)
                    act.activation(kvT[:], bank[0:DC, 0, 0:SEQ], ACT.Identity, bias=bk_col[:, 0:1]).then_inc(kvT_ready, 1)
                    act.wait_ge(outT_psum, b + 1)
                    act.activation(outT[:], bank[0:DC, 2, 0:SEQ], ACT.Copy, scale=float(D) ** -0.5).then_inc(outT_ready, 1)
                    act.wait_ge(smax_ready, b + 1)
                    for r in range(2):
                        act.activation(prob_x[:, r, :], simg[:, r, :], ACT.Exp, bias=nmax[:, 0, r:r + 1],
                                       accum_out=sums[:, r, 0:1]).then_inc(sexp_ready, 1)

            if STAGES > 2:
                act.preload_act_table(ACT.Silu)
                act.wait_ge(wabs_ready, 3)
                for w in (s1, s2, s3):
                    act.activation(w, w, ACT.Sign).then_inc(sign_ready, 1)
                act.wait_ge(wmean_psum, 1)
                act.activation(wmean[:], bank[:, 6, 0:3], ACT.Copy, scale=1.0 / (D * FF)).then_inc(sign_ready, 1)
                act.wait_ge(sign_ready, 4)
                with act.Fori(0, NB) as b:
                    copy_xnT(b + 2 * NB)
                    for r in range(2):
                        for c in range(2):
                            act.wait_ge(hid_psum, b * 4 + (2 * r + c + 1))
                            act.activation(gate_f[:, r, c * 512:(c + 1) * 512], bank[:, 2 * c, :], ACT.Silu,
                                           scale=wmean[:, 0:1]).then_inc(gate_ready, 1)
                    for r in range(2):
                        act.wait_ge(hT_psum, b * 2 + (r + 1))
                        act.activation(hidT[:, r], bank[:, 4:6, :].rearrange("p a (m n) -> p (a m) n", m=4),
                                       ACT.Copy).then_inc(hT_ready, 1)

            if STAGES > 3:
                act.preload_act_table(ACT.Exp)
                with act.Fori(0, NB) as b:
                    attention(1, b)

            if STAGES > 4:
                for h in range(NH):
                    act.wait_ge(fold_psum, h + 1)
                    act.activation(Aq[:, h], bank[:, h % 2, 0:2 * CQ].rearrange("p (k n) -> p k n", k=KD),
                                   ACT.Copy).then_inc(fold_act, 1)
                for g in range(NH // 4):
                    act.wait_ge(fold_psum, NH + g + 1)
                    act.activation(Gq[:, 4 * g:4 * g + 4], bank[0:HC, g % 2, :].rearrange("p (h f n) -> p h f n", h=4, f=2),
                                   ACT.Copy).then_inc(fold_act, 1)
                for g in range(PAIRS // 2):
                    act.wait_ge(fold_psum, NH + NH // 4 + g + 1)
                    act.activation(Cx[:, 2 * g:2 * g + 2], bank[:, g % 2, :].rearrange("p (j n) -> p j n", j=2),
                                   ACT.Copy).then_inc(fold_act, 1)
                with act.Fori(0, NB) as b:
                    act.wait_ge(kvrT_psum, b + 1)
                    act.activation(kvrT[:], bank[0:DC, 6, 0:SEQ], ACT.Copy).then_inc(kvrT_ready, 1)
                    copy_xnT(b + 4 * NB)
                    for i in range(1, NH + 4):
                        h = i - 1
                        if h < NH:
                            act.wait_ge(z_psum, b * NH + (h + 1))
                            act.activation(zT[:, h % 2], bank[0:DC, 2, 0:SEQ], ACT.Copy).then_inc(z_ready, 1)
                            act.wait_ge(mx_ready, b * NH + (h + 1))
                            if h >= 2:
                                act.wait_ge(pxT_psum, b * NH + (h - 1))
                            for r in range(2):
                                act.activation(px[:, h % 2, r, :], bank[:, 3 + h % 2, r * SEQ:(r + 1) * SEQ], ACT.Exp,
                                               bias=nmax[:, h % 2, r:r + 1],
                                               accum_out=sums[:, r, h:h + 1]).then_inc(px_ready, 1)
                        h = i - 3
                        if h >= 0 and h % 2 == 1:
                            j = h // 2
                            act.wait_ge(cT_psum, b * PAIRS + (j + 1))
                            act.activation(cT[:, j % 2], bank[:, 2, 256:512], ACT.Copy).then_inc(cT_ready, 1)

            if STAGES > 5:
                act.preload_act_table(ACT.Silu)
                with act.Fori(0, NB) as b:
                    copy_xnT(b + 5 * NB)
                    act.wait_ge(lg_psum, b + 1)
                    act.activation(lg[:, bass.ts(b, 2), :], bank[:, 0, 0:2 * NE].rearrange("p (r e) -> p r e", r=2),
                                   ACT.Copy).then_inc(lg_ready, 1)
                    act.wait_ge(sh_psum, b + 1)
                    act.activation(sh_g, bank[:, 1, :].rearrange("p (f n) -> p f n", f=2), ACT.Silu).then_inc(shg_ready, 1)
                act.preload_act_table(ACT.Exp)
                act.wait_ge(lg_ready, NB)
                act.activation(scb, lg[:], ACT.Exp, scale=-1.0).then_inc(esig_ready, 1)
                act.preload_act_table(ACT.Silu)
                for c in range(NC):
                    act.wait_ge(gat_psum, c + 1)
                    act.activation(bufT, bank[:, 0:2, :], ACT.Copy).then_inc(buf_ready, 1)
                    for t in range(NT):
                        act.wait_ge(hotT_psum, NT * c + t + 1)
                        act.activation(hotT[:, t], bank[:, 2 + t % 2, :].rearrange("p (k n) -> p k n", k=KS),
                                       ACT.Copy).then_inc(hotT_ready, 1)
                    act.wait_ge(eh_psum, c + 1)
                    act.activation(h_g, bank[:, 4, :], ACT.Silu).then_inc(eg_ready, 1)
                    act.wait_ge(ob_psum, c + 1)
                    act.activation(ob, bank[:, 6:8, :].rearrange("p a (k n) -> p (a k) n", k=2), ACT.Copy).then_inc(ob_ready, 1)

        @block.vector
        def _(dve):
            dve.wait_ge(s_const, 3 * 16)
            dve.tensor_copy(ident_h[:], ident[:]).then_inc(casts, 1)
            dve.tensor_copy(causal_h[:], causal[:]).then_inc(casts, 1)
            dve.wait_ge(s_x, 16)

            def norm(n, b, st):
                for r in range(2):
                    st.mark(dve.bn_stats(stat[:, r, :], X[:, bass.ts(b, 2), :][:, r, :]))
                st.wait_apart(scrap[:])
                for r in range(2):
                    dve.bn_aggr(mv[:, r, :], stat[:, r, :]).then_inc(mv_ready, 1)
                dve.wait_ge(mv_ready, 2 * n + 2)
                dve.wait_ge(rstd_ready, n + 1)
                for r in range(2):
                    dve.tensor_scalar(xn[:, r, :], X[:, bass.ts(b, 2), :][:, r, :], mv[:, r, 0:1], rstd[:, r:r + 1],
                                      ALU.subtract, ALU.mult).then_inc(xn_ready, 1)

            def add_y(n, b, col, scale=None):
                dve.wait_ge(y_ready, n + 1)
                xb = X[:, bass.ts(b, 2), :]
                y = col.rearrange("p (r n) -> p r n", r=2)
                if scale is None:
                    dve.tensor_tensor(xb, y, xb, ALU.add).then_inc(x_done, 1)
                else:
                    dve.scalar_tensor_tensor(xb, y, scale, xb, ALU.mult, ALU.add).then_inc(x_done, 1)

            def attention(l, b, st):
                norm(b + 3 * NB * l, b, st)
                if l == 0:
                    dve.wait_ge(proj[0], b + 1)
                    ksrc = bank[:, 1, :]
                    dve.tensor_copy(V[:], bank[:, 2, :].rearrange("p (r n) -> p r n", r=2)).then_inc(kv_ready[0], 1)
                else:
                    dve.wait_ge(proj[1], b * 2 + 1)
                    for r in range(2):
                        src = bank[:, r, 0:320].rearrange("p (h n) -> p h n", n=HD)
                        c = qk_c[:, r, :].rearrange("p (h n) -> p h n", n=HD)
                        s = qk_s[:, r, :].rearrange("p (h n) -> p h n", n=HD)
                        st.mark(dve.tensor_tensor(c, src, cos1[:, r, :].unsqueeze(1).to_broadcast([P, 20, HD]), ALU.mult))
                        for f in range(2):
                            o = 8 * f
                            st.mark(dve.tensor_tensor(s[:, :, o:o + 8], src[:, :, 8 - o:16 - o],
                                                      sin1[:, r, o:o + 8].unsqueeze(1).to_broadcast([P, 20, 8]), ALU.mult))
                    dve.tensor_copy(V[:, :, 0:64], bank[:, 0:2, 320:384]).then_inc(v_copied, 1)
                    st.wait()
                    for r in range(2):
                        dve.tensor_tensor(q_r[:, r, :], qk_c[:, r, 0:256], qk_s[:, r, 0:256], ALU.add).then_inc(roped, 1)
                        kc, ks = (v[:, r, 256:320].rearrange("p (g n) -> p g n", n=HD).unsqueeze(2).to_broadcast([P, 4, 4, HD])
                                  for v in (qk_c, qk_s))
                        dve.tensor_tensor(k_r[:, r, :].rearrange("p (g m n) -> p g m n", g=4, m=4), kc, ks,
                                          ALU.add).then_inc(roped, 1)
                    dve.wait_ge(proj[1], b * 2 + 2)
                    ksrc = bank[:, 3, :]
                for e in range(2):
                    dve.tensor_scalar(kT[:, e], ksrc.rearrange("p (k n) -> p k n", k=KD), parity[:, e:e + 1], None,
                                      ALU.mult).then_inc(kv_ready[l], 1)
                def row_max(j):
                    i = j % 2
                    for r in range(2):
                        dve.wait_ge(s_ready[l], b * (2 * PAIRS) + (2 * j + r + 1))
                        n = SEQ if r else P
                        dve.tensor_reduce(nmax[:, i, 2 * r:2 * r + 2],
                                          bank[:, 2 * i + r, 0:2 * n].rearrange("p (e n) -> p e n", e=2),
                                          AX.X, ALU.max, negate=True).then_inc(max_ready[l], 1)
                row_max(0)
                for j in range(PAIRS):
                    if j + 1 < PAIRS:
                        row_max(j + 1)
                    dve.wait_ge(pT_psum[l], b * PAIRS + (j + 1))
                    if j >= 2:
                        dve.wait_ge(av_done[l], b * PAIRS + (j - 1))
                    dve.tensor_copy(probT[:, j % 2, 0:4, :], bank[:, 4, :].rearrange("p (m n) -> p m n", m=4)).then_inc(pT_ready[l], 1)
                    dve.tensor_copy(probT[:, j % 2, 4:6, :], bank[:, 5, 0:256].rearrange("p (m n) -> p m n", m=2)).then_inc(pT_ready[l], 1)
                dve.wait_ge(p_ready[l], b * (4 * PAIRS) + 4 * PAIRS)
                st.mark(dve.reciprocal(rsum[:], sums[:]))
                dve.wait_ge(av_done[l], b * PAIRS + PAIRS)
                st.wait()
                dve.tensor_tensor(On[:].rearrange("p r (h n) -> p r h n", h=NH),
                                  bank[:, 6, :].rearrange("p (r h n) -> p r h n", r=2, h=NH),
                                  rsum[:].unsqueeze(3).to_broadcast([P, 2, NH, HD]), ALU.mult).then_inc(on_ready[l], 1)
                add_y(b + 2 * NB * l, b, bank[:, 7, :])

            st = Steps(dve, dve_steps[0])
            with dve.Fori(0, NB) as b:
                st.loop(b, 0, 3)
                attention(0, b, st)
            st.end(NB, "attention 0")

            if STAGES > 1:
                st = Steps(dve, dve_steps[1])
                with dve.Fori(0, NB) as b:
                    st.loop(b, 0, 7)
                    dve.wait_ge(x_done, b + 1)
                    norm(b + NB, b, st)
                    dve.wait_ge(kv_psum, b + 1)
                    dve.tensor_tensor(kvj[:], bank[:, 1, 0:2 * DC].rearrange("p (r n) -> p r n", r=2),
                                      bk_row[:].unsqueeze(1).to_broadcast([P, 2, DC]), ALU.add).then_inc(kvj_ready, 1)
                    dve.wait_ge(sim_ready, b + 1)
                    for r in range(2):
                        st.mark(dve.bn_stats(stat[:, r, :], bank[:, 3, r * SEQ:(r + 1) * SEQ]))
                    st.wait_apart(scrap[:])
                    for r in range(2):
                        dve.bn_aggr(mv[:, r, :], stat[:, r, :]).then_inc(smv_ready, 1)
                    dve.wait_ge(smv_ready, 2 * b + 2)
                    dve.wait_ge(srstd_ready, b + 1)
                    for r in range(2):
                        st.mark(dve.tensor_scalar(simn[:, r, :], bank[:, 3, r * SEQ:(r + 1) * SEQ], mv[:, r, 0:1],
                                                  rstd[:, r:r + 1], ALU.subtract, ALU.mult))
                    st.wait()
                    st.mark(dve.tensor_tensor(simg, simn, gamma[:].unsqueeze(1).to_broadcast([P, 2, D]), ALU.mult))
                    st.wait()
                    dve.tensor_tensor(simg, simg, beta[:].unsqueeze(1).to_broadcast([P, 2, D]), ALU.add).then_inc(smax_pre, 1)
                    dve.wait_ge(smax_pre, b + 1)
                    dve.tensor_reduce(nmax[:, 0, 0:2], simg, AX.X, ALU.max, negate=True).then_inc(smax_ready, 1)
                    dve.wait_ge(sexp_ready, 2 * b + 2)
                    dve.reciprocal(rsum[:, :, 0], sums[:, :, 0]).then_inc(srcp_ready, 1)
                    dve.wait_ge(srcp_ready, b + 1)
                    for r in range(2):
                        xb = X[:, bass.ts(b, 2), :][:, r, :]
                        o = dve.scalar_tensor_tensor(xb, prob_x[:, r, :], rsum[:, r, 0:1], xb, ALU.mult, ALU.add)
                        if r:
                            o.then_inc(x_done, 1)
                        else:
                            o.then_inc(x_half, 1)
                st.end(NB, "cross attention 0")

            if STAGES > 2:
                dve.wait_ge(s_wff, 3 * 16)
                for n in range(3):
                    dve.tensor_reduce(wabs[:, n:n + 1], w_ff[:, 2048 * n:2048 * (n + 1)], AX.X, ALU.add,
                                      apply_absolute_value=True).then_inc(wabs_ready, 1)

                def scales(m, k):
                    st.mark(dve.tensor_scalar_max(gscl[:, m, 0:k], gmax[:, m, 0:k], 1e-5))
                    st.wait()
                    st.mark(dve.reciprocal(grcp[:, m, 0:k], gscl[:, m, 0:k]))
                    st.wait()
                    st.mark(dve.tensor_scalar_mul(grcp[:, m, 0:k], grcp[:, m, 0:k], QB))
                    st.mark(dve.tensor_scalar_mul(gscl[:, m, 0:k], gscl[:, m, 0:k], 1.0 / QB))
                    st.wait()

                st = Steps(dve, dve_steps[2])
                with dve.Fori(0, NB) as b:
                    st.loop(b, 0, 23)
                    dve.wait_ge(x_done, b + (NB + 1))
                    norm(b + 2 * NB, b, st)
                    dve.wait_ge(xn_ready, b * 2 + (4 * NB + 2))
                    xg = xn[:].rearrange("p r (g n) -> p (r g) n", n=GRP)
                    st.mark(dve.tensor_reduce(gmax[:, 0, 0:8], xg, AX.X, ALU.max, apply_absolute_value=True))
                    st.wait()
                    scales(0, 8)
                    st.mark(dve.tensor_tensor(xg, xg, grcp[:, 0, 0:8].unsqueeze(2).to_broadcast([P, 8, GRP]), ALU.mult))
                    st.wait()
                    st.mark(dve.tensor_scalar(xg, xg, ROUND, -ROUND, ALU.add, ALU.add))
                    st.wait()
                    dve.tensor_tensor(xg, xg, gscl[:, 0, 0:8].unsqueeze(2).to_broadcast([P, 8, GRP]),
                                      ALU.mult).then_inc(xq_ready, 1)
                    def hidden(r):
                        for c in range(2):
                            dve.wait_ge(gate_ready, b * 4 + (2 * r + c + 1))
                            o = slice(c * 512, (c + 1) * 512)
                            dve.scalar_tensor_tensor(hid[:, r, o], bank[:, 2 * c + 1, :], wmean[:, 1:2], gate_f[:, r, o],
                                                     ALU.mult, ALU.mult).then_inc(hid_used, 1)
                    def quant(r):
                        hg = hid[:, r, :].rearrange("p (g n) -> p g n", n=GRP)
                        dve.wait_ge(hid_used, b * 4 + (2 * r + 2))
                        st.mark(dve.tensor_reduce(gmax[:, r, :], hg, AX.X, ALU.max, apply_absolute_value=True))
                        st.wait()
                        scales(r, 16)
                        st.mark(dve.tensor_tensor(hg, hg, grcp[:, r, :].unsqueeze(2).to_broadcast([P, 16, GRP]), ALU.mult))
                        st.wait()
                        st.mark(dve.tensor_scalar(hg, hg, ROUND, -ROUND, ALU.add, ALU.add))
                        st.wait()
                        dve.tensor_tensor(hg, hg, gscl[:, r, :].unsqueeze(2).to_broadcast([P, 16, GRP]),
                                          ALU.mult).then_inc(hq_ready, 1)
                    hidden(0)
                    quant(0)
                    hidden(1)
                    quant(1)
                    add_y(b + NB, b, bank[:, 6, :], wmean[:, 2:3])
                st.end(NB, "feed forward 0")

            if STAGES > 3:
                dve.wait_ge(s_w1, 4 * 16)
                st = Steps(dve, dve_steps[3])
                with dve.Fori(0, NB) as b:
                    st.loop(b, 0, 9)
                    dve.wait_ge(x_done, b + (2 * NB + 1))
                    attention(1, b, st)
                st.end(NB, "attention 1")

            if STAGES > 4:
                dve.wait_ge(s_wx, 10 * 16)
                st = Steps(dve, dve_steps[4])
                with dve.Fori(0, NB) as b:
                    st.loop(b, 0, 2 + 3 + NH)
                    src = ctxk[:, bass.ts(b, 2), :]
                    st.mark(dve.tensor_tensor(kv_c, src, cosk[:], ALU.mult))
                    for f in range(2):
                        o = DC // 2 * f
                        st.mark(dve.tensor_tensor(kv_s[:, :, o:o + 32], src[:, :, 32 - o:64 - o], sink[:, :, o:o + 32], ALU.mult))
                    st.wait()
                    dve.tensor_tensor(kvr[:], kv_c, kv_s, ALU.add).then_inc(kvr_ready, 1)
                    dve.wait_ge(x_done, b + (3 * NB + 1))
                    norm(b + 4 * NB, b, st)
                    for i in range(NH + 2):
                        if i < NH:
                            h = i
                            dve.wait_ge(qx_psum, b * NH + (h + 1))
                            if h >= 2:
                                dve.wait_ge(qx_ready, b * (2 * NH) + 2 * (h - 1))
                            q = bank[0:HC, h % 2, :].rearrange("p (f n) -> p f n", f=2)
                            dve.tensor_tensor(qx_c[:, h % 2], q, cosq[:], ALU.mult).then_inc(qx_cs, 1)
                            dve.tensor_tensor(qx_s[:, h % 2], q, sinq[:], ALU.mult).then_inc(qx_cs, 1)
                        if i >= 2:
                            h = i - 2
                            dve.wait_ge(pxT_psum, b * NH + (h + 1))
                            if h >= 2:
                                dve.wait_ge(cx_psum, b * NH + (h - 1))
                            dve.tensor_copy(pxT[:, h % 2], bank[:, 5, :].rearrange("p (k n) -> p k n", k=2)).then_inc(pxT_ready, 1)
                        if 1 <= i <= NH:
                            h = i - 1
                            dve.wait_ge(sx_ready, b * NH + (h + 1))
                            dve.tensor_reduce(nmax[:, h % 2, 0:2], bank[:, 3 + h % 2, :].rearrange("p (r n) -> p r n", r=2),
                                              AX.X, ALU.max, negate=True).then_inc(mx_ready, 1)
                        if i >= 2:
                            h = i - 2
                            j, e = h // 2, h % 2
                            dve.wait_ge(px_ready, b * (2 * NH) + 2 * (h + 1))
                            st.mark(dve.reciprocal(rsum[:, :, h], sums[:, :, h]))
                            dve.wait_ge(cx_psum, b * NH + (h + 1))
                            if e == 0 and j >= 2:
                                dve.wait_ge(cT_psum, b * PAIRS + (j - 1))
                            st.wait()
                            dve.tensor_tensor(cn[:, j % 2, :, e * DC:(e + 1) * DC],
                                              bank[:, 6, 0:256].rearrange("p (r n) -> p r n", r=2)[:, :, e * DC:(e + 1) * DC],
                                              rsum[:, :, h:h + 1].to_broadcast([P, 2, DC]), ALU.mult).then_inc(cn_ready, 1)
                    add_y(b + 3 * NB, b, bank[:, 7, :])
                st.end(NB, "cross attention 1")

            if STAGES > 5:
                dve.wait_ge(s_wm, 6 * 16)
                st = Steps(dve, dve_steps[5])
                with dve.Fori(0, NB) as b:
                    st.loop(b, 0, 2)
                    dve.wait_ge(x_done, b + (4 * NB + 1))
                    norm(b + 5 * NB, b, st)
                    dve.wait_ge(shg_ready, b + 1)
                    dve.tensor_tensor(sh_h, bank[:, 2, :].rearrange("p (f n) -> p f n", f=2), sh_g, ALU.mult).then_inc(shh_ready, 1)
                    add_y(b + 4 * NB, b, bank[:, 3, :])
                st.end(NB, "shared expert")

                def step(ins):
                    st.mark(ins)
                    st.wait()

                dve.wait_ge(esig_ready, 1)
                step(dve.tensor_scalar_add(scb, scb, 1.0))
                step(dve.reciprocal(sc, scb))
                step(dve.tensor_tensor(scb, sc, gbias[:].unsqueeze(1).to_broadcast([P, NT, NE]), ALU.add))
                for g in range(NT * NG):
                    st.mark(dve.max(top_g[:, g, :], scb[:, g // NG, EG * (g % NG):EG * (g % NG + 1)]))
                st.wait()
                step(dve.tensor_tensor(gs, top_g.rearrange("p (t g) n -> p t g n", t=NT)[:, :, :, 0],
                                       top_g.rearrange("p (t g) n -> p t g n", t=NT)[:, :, :, 1], ALU.add))
                other = gs.unsqueeze(2).to_broadcast([P, NT, NG, NG])
                own = gs.unsqueeze(3).to_broadcast([P, NT, NG, NG])
                st.mark(dve.tensor_tensor(cmp_a, other, own, ALU.is_gt))
                step(dve.tensor_tensor(cmp_b, other, own, ALU.is_equal))
                step(dve.tensor_tensor(cmp_b, cmp_b, earlier.rearrange("p (g k) -> p g k", g=NG).unsqueeze(1).to_broadcast(
                    [P, NT, NG, NG]), ALU.mult))
                step(dve.tensor_tensor(cmp_a, cmp_a, cmp_b, ALU.add))
                step(dve.tensor_reduce(rank, cmp_a.rearrange("p t g k -> p (t g) k"), AX.X, ALU.add))
                step(dve.tensor_scalar(rank, rank, 2.0, None, ALU.is_lt))
                step(dve.tensor_tensor(tmp_e.rearrange("p t (g n) -> p (t g) n", g=NG),
                                       scb.rearrange("p t (g n) -> p (t g) n", g=NG),
                                       rank.unsqueeze(2).to_broadcast([P, NT * NG, EG]), ALU.mult))
                for t in range(NT):
                    st.mark(dve.max(top_e[:, t, :], tmp_e[:, t, :]))
                st.wait()
                for t in range(NT):
                    st.mark(dve.max_index(idx_u[:, t, :], top_e[:, t, :], tmp_e[:, t, :]))
                st.wait()
                step(dve.tensor_copy(idx_f, idx_u[:]))
                for t in range(NT):
                    st.mark(dve.tensor_tensor(pick[:, t], iota_e.unsqueeze(2).to_broadcast([P, NE, TOPK]),
                                              idx_f[:, t, 0:TOPK].unsqueeze(1).to_broadcast([P, NE, TOPK]), ALU.is_equal))
                st.wait()
                st.mark(dve.tensor_reduce(mask, pick, AX.X, ALU.add))
                st.wait()
                st.mark(dve.memset(seen[:, 0], 0.0))
                st.wait()
                for t in range(1, NT):
                    if t < NT - 1:
                        step(dve.tensor_tensor(seen[:, t], seen[:, t - 1], mask[:, t - 1], ALU.add))
                    else:
                        dve.tensor_tensor(seen[:, t], seen[:, t - 1], mask[:, t - 1], ALU.add).then_inc(mask_ready, 1)
                step(dve.tensor_tensor(wgt, sc, mask, ALU.mult))
                step(dve.tensor_reduce(wsum, wgt, AX.X, ALU.add))
                step(dve.tensor_scalar_add(wsum, wsum, 1e-20))
                step(dve.reciprocal(wrcp, wsum))
                step(dve.tensor_scalar_mul(wrcp, wrcp, 2.0))
                step(dve.tensor_tensor(wgt, wgt, wrcp.unsqueeze(2).to_broadcast([P, NT, NE]), ALU.mult))
                dve.wait_ge(pos_psum, 1)
                pos = bank[:, 4, 0:NT * NE].rearrange("p (t e) -> p t e", t=NT)
                step(dve.scalar_tensor_tensor(keep, pos, float(CAP), mask, ALU.is_lt, ALU.mult))
                step(dve.scalar_tensor_tensor(posm, pos, 1.0, keep, ALU.add, ALU.mult))
                step(dve.tensor_scalar_add(posm, posm, -1.0))
                for c in range(NC):
                    for t in range(NT):
                        if c > 0:
                            dve.wait_ge(hotw_ready, NT * (c - 1) + t + 1)
                        if c > 0 and t == 0:
                            dve.wait_ge(gat_psum, c)
                        dve.tensor_tensor(hot[:, t].rearrange("p (e n) -> p e n", e=EC),
                                          iota_s.unsqueeze(1).to_broadcast([P, EC, CAP]),
                                          posm[:, t, c * EC:(c + 1) * EC].unsqueeze(2).to_broadcast([P, EC, CAP]),
                                          ALU.is_equal).then_inc(hot_ready, 1)
                    dve.wait_ge(eg_ready, c + 1)
                    dve.tensor_tensor(h_T, bank[:, 5, :], h_g, ALU.mult).then_inc(eh_ready, 1)
                    for q in range(NT // 2):
                        n = c * (NT // 2) + q
                        dve.wait_ge(ey_psum, n + 1)
                        xb = X[:, 2 * q:2 * q + 2, :]
                        dve.wait_ge(x_done, 6 * NB + max(0, n - 3))
                        dve.tensor_tensor(xb, bank[:, 0 + n % 2, :].rearrange("p (r n) -> p r n", r=2), xb,
                                          ALU.add).then_inc(x_done, 1)

        @block.tensor
        def _(pe):
            mm, tr = pe.matmul, pe.transpose
            pe.wait_ge(s_const, 3 * 16)
            pe.wait_ge(casts, 2)

            def turn_xn(n, ready=None, count=None, then=None):
                pe.wait_ge(xn_ready if ready is None else ready, 2 * n + 2 if ready is None else count)
                for k in range(KD):
                    for r in range(2):
                        o = tr(bank[:, 7, k * SEQ + r * P:k * SEQ + (r + 1) * P], xn[:, r, k * P:(k + 1) * P], ident[:])
                o.then_inc(xnTp_ready, 1)
                if then:
                    then()
                pe.wait_ge(xnT_ready, n + 1)

            def attention(l, b):
                turn_xn(b + 3 * NB * l)
                if l == 0:
                    for m in range(2):
                        for g in range(2):
                            for k in range(KD):
                                mm(bank[:, m, g * SEQ:(g + 1) * SEQ], wqkv0[:, k, m * D + g * P:m * D + (g + 1) * P],
                                   xnT[:, k, :], start=(k == 0), stop=(k == KD - 1), skip_group_check=True)
                    for r in range(2):
                        for k in range(KD):
                            o = mm(bank[:, 2, r * D:(r + 1) * D], xnT[:, k, r * P:(r + 1) * P], wqkv0[:, k, 2 * D:3 * D],
                                   start=(k == 0), stop=(k == KD - 1), skip_group_check=True)
                    o.then_inc(proj[0], 1)
                else:
                    for r in range(2):
                        for k in range(KD):
                            o = mm(bank[:, r, 0:384], xnT[:, k, r * P:(r + 1) * P], wqkv1[:, k, :],
                                   start=(k == 0), stop=(k == KD - 1))
                    o.then_inc(proj[1], 1)
                    pe.wait_ge(roped, b * 4 + 4)
                    for m, src in enumerate((q_r, k_r)):
                        for k in range(KD):
                            for r in range(2):
                                o = tr(bank[:, 2 + m, k * SEQ + r * P:k * SEQ + (r + 1) * P],
                                       src[:, r, k * P:(k + 1) * P], ident[:])
                    o.then_inc(proj[1], 1)
                    pe.wait_ge(v_copied, b + 1)
                pe.wait_ge(q_ready[l], b + 1)
                pe.wait_ge(kv_ready[l], (b * 3 + 3) if l == 0 else (b * 2 + 2))

                def score(j):
                    g, base, i = j // 4, 32 * (j % 4), j % 2
                    if j >= 2:
                        pe.wait_ge(p_ready[l], b * (4 * PAIRS) + 4 * (j - 1))
                    for r in range(2):
                        n = SEQ if r else P
                        view = bank[:, 2 * i + r, 0:2 * n].rearrange("p (e n) -> p e n", e=2)
                        for e in range(2):
                            mm(view[:, e, :], qT[base:base + 32, g, r * P:(r + 1) * P], kT[base:base + 32, e, g, 0:n],
                               start=(e == 0), stop=False, skip_group_check=True)
                        mm(view[:, :, n - P:n], ident_h[:], causal_h[:].unsqueeze(1).to_broadcast([P, 2, P]),
                           start=False, stop=True, skip_group_check=True).then_inc(s_ready[l], 1)

                def turn(j):
                    pe.wait_ge(p_ready[l], b * (4 * PAIRS) + 4 * (j + 1))
                    if j >= 1:
                        pe.wait_ge(pT_ready[l], b * (2 * PAIRS) + 2 * j)
                    for m in range(6):
                        o = tr(bank[:, 4 + m // 4, (m % 4) * P:(m % 4 + 1) * P], prob[:, j % 2, m // 3, m % 3, :], ident[:])
                    o.then_inc(pT_psum[l], 1)

                def values(j):
                    pe.wait_ge(pT_ready[l], b * (2 * PAIRS) + 2 * (j + 1))
                    for e in range(2):
                        h = 2 * j + e
                        v = h if l == 0 else h // 4
                        for m in range(3):
                            r, k = (0, 0) if m == 0 else (1, m - 1)
                            o = mm(bank[:, 6, r * D + h * HD:r * D + (h + 1) * HD], probT[:, j % 2, 3 * e + m, :],
                                   V[:, k, v * HD:(v + 1) * HD], start=(m < 2), stop=(m != 1), skip_group_check=True)
                    o.then_inc(av_done[l], 1)

                score(0)
                for j in range(PAIRS):
                    if j + 1 < PAIRS:
                        score(j + 1)
                    turn(j)
                    if j >= 1:
                        values(j - 1)
                values(PAIRS - 1)
                pe.wait_ge(on_ready[l], b + 1)
                for k in range(KD):
                    for r in range(2):
                        o = tr(bank[:, 7, k * SEQ + r * P:k * SEQ + (r + 1) * P], On[:, r, k * P:(k + 1) * P], ident[:])
                o.then_inc(oT_psum[l], 1)
                pe.wait_ge(oT_ready[l], b + 1)
                wo = wo0 if l == 0 else wo1
                for r in range(2):
                    for k in range(KD):
                        o = mm(bank[:, 7, r * D:(r + 1) * D], OT[:, k, r * P:(r + 1) * P], wo[:, k, :],
                               start=(k == 0), stop=(k == KD - 1), skip_group_check=True)
                o.then_inc(y_ready, 1)

            pe.wait_ge(s_w0, 2 * 16)
            with pe.Fori(0, NB) as b:
                attention(0, b)

            if STAGES > 1:
                pe.wait_ge(s_ctx, 7 * 16)
                with pe.Fori(0, NB) as b:
                    pe.wait_ge(ctb_ready, b + 1)
                    for r in range(2):
                        mm(bank[:, 1, r * DC:(r + 1) * DC], ctb[:, r * P:(r + 1) * P], wk[:], start=True, stop=True,
                           skip_group_check=True)
                    mm(bank[0:DC, 0, 0:SEQ], wk[:], ctb[:], start=True, stop=True).then_inc(kv_psum, 1)
                    turn_xn(b + NB)
                    pe.wait_ge(kvj_ready, b + 1)
                    for k in range(2):
                        o = mm(bank[0:DC, 2, 0:SEQ], kvj[:, k, :], xnT[:, k, :], start=(k == 0), stop=(k == 1))
                    o.then_inc(outT_psum, 1)
                    pe.wait_ge(outT_ready, b + 1)
                    pe.wait_ge(kvT_ready, b + 1)
                    for r in range(2):
                        o = mm(bank[:, 3, r * SEQ:(r + 1) * SEQ], outT[:, r * P:(r + 1) * P], kvT[:], start=True, stop=True,
                               skip_group_check=True)
                    o.then_inc(sim_ready, 1)

            if STAGES > 2:
                pe.wait_ge(setup, 4)
                pe.wait_ge(wabs_ready, 3)
                mm(bank[:, 6, 0:3], ones[:], wabs[:], start=True, stop=True).then_inc(wmean_psum, 1)
                pe.wait_ge(sign_ready, 4)
                with pe.Fori(0, NB) as b:
                    turn_xn(b + 2 * NB, xq_ready, b + 1)
                    def hidden(r):
                        for c in range(2):
                            if r == 1:
                                pe.wait_ge(hid_used, b * 4 + (c + 1))
                            for w, src in enumerate((s1, s2)):
                                for k in range(KD):
                                    o = mm(bank[:, 2 * c + w, :], xnT[:, k, r * P:(r + 1) * P], src[:, k, c * 512:(c + 1) * 512],
                                           start=(k == 0), stop=(k == KD - 1))
                            o.then_inc(hid_psum, 1)
                    hidden(0)
                    hidden(1)
                    for r in range(2):
                        pe.wait_ge(hq_ready, b * 2 + (r + 1))
                        if r:
                            pe.wait_ge(hT_ready, b * 2 + 1)
                        for m in range(FF // P):
                            o = tr(bank[:, 4 + m // 4, (m % 4) * P:(m % 4 + 1) * P], hid[:, r, m * P:(m + 1) * P], ident[:])
                        o.then_inc(hT_psum, 1)
                        pe.wait_ge(hT_ready, b * 2 + (r + 1))
                        for m in range(FF // P):
                            o = mm(bank[:, 6, r * D:(r + 1) * D], hidT[:, r, m, :], s3[:, m, :], start=(m == 0),
                                   stop=(m == FF // P - 1), skip_group_check=True)
                    o.then_inc(y_ready, 1)

            if STAGES > 3:
                pe.wait_ge(s_w1, 4 * 16)
                with pe.Fori(0, NB) as b:
                    attention(1, b)

            if STAGES > 4:
                pe.wait_ge(s_wx, 10 * 16)
                for h in range(NH):
                    if h >= 2:
                        pe.wait_ge(fold_act, h - 1)
                    for k in range(KD):
                        o = mm(bank[:, h % 2, k * CQ:(k + 1) * CQ], wq_x[:, h, k * P:(k + 1) * P], wcq[:, h, :],
                               start=True, stop=True, skip_group_check=True)
                    o.then_inc(fold_psum, 1)
                for g in range(NH // 4):
                    pe.wait_ge(fold_act, NH + g - 1)
                    for m in range(8):
                        h, f = 4 * g + m // 2, m % 2
                        o = mm(bank[0:HC, g % 2, m * DC:(m + 1) * DC], wqr[:, h, f * HC:(f + 1) * HC], wkr[:, h, :],
                               start=True, stop=True, skip_group_check=True)
                    o.then_inc(fold_psum, 1)
                for g in range(PAIRS // 2):
                    pe.wait_ge(fold_act, NH + NH // 4 + g - 1)
                    for m in range(4):
                        h, j = 4 * g + m, m // 2
                        o = mm(bank[DC * (m % 2):DC * (m % 2 + 1), g % 2, j * D:(j + 1) * D], wckv[:, h, :], wo_x[:, h, :],
                               start=True, stop=True, skip_group_check=True)
                    o.then_inc(fold_psum, 1)
                pe.wait_ge(fold_act, NH + NH // 4 + PAIRS // 2)
                with pe.Fori(0, NB) as b:
                    pe.wait_ge(kvr_ready, b + 1)

                    def turn_kvr():
                        for r in range(2):
                            o = tr(bank[0:DC, 6, r * P:(r + 1) * P], kvr[:, r, :], ident[:])
                        o.then_inc(kvrT_psum, 1)
                    turn_xn(b + 4 * NB, then=turn_kvr)
                    pe.wait_ge(kvrT_ready, b + 1)
                    for i in range(NH + 4):
                        if i < NH:
                            h = i
                            if h >= 2:
                                pe.wait_ge(qx_cs, b * (2 * NH) + 2 * (h - 1))
                            for f in range(2):
                                for k in range(KD):
                                    o = mm(bank[0:HC, h % 2, f * SEQ:(f + 1) * SEQ], Aq[:, h, k, f * HC:(f + 1) * HC],
                                           xnT[:, k, :], start=(k == 0), stop=(k == KD - 1), skip_group_check=True)
                            o.then_inc(qx_psum, 1)
                        if 1 <= i <= NH:
                            h = i - 1
                            pe.wait_ge(qx_ready, b * (2 * NH) + 2 * (h + 1))
                            if h >= 1:
                                pe.wait_ge(z_ready, b * NH + h)
                            if h >= 4:
                                pe.wait_ge(cT_ready, b * PAIRS + (h - 2) // 2)
                            for f in range(2):
                                o = mm(bank[0:DC, 2, 0:SEQ], Gq[:, h, f, :], qx_r[:, h % 2, f, :], start=(f == 0), stop=(f == 1))
                            o.then_inc(z_psum, 1)
                        if 2 <= i < NH + 2:
                            h = i - 2
                            pe.wait_ge(px_ready, b * (2 * NH) + 2 * (h + 1))
                            if h >= 1:
                                pe.wait_ge(pxT_ready, b * NH + h)
                            for k in range(2):
                                for r in range(2):
                                    o = tr(bank[:, 5, k * SEQ + r * P:k * SEQ + (r + 1) * P],
                                           px[:, h % 2, r, k * P:(k + 1) * P], ident[:])
                            o.then_inc(pxT_psum, 1)
                        if 1 <= i <= NH:
                            h = i - 1
                            pe.wait_ge(z_ready, b * NH + (h + 1))
                            for r in range(2):
                                o = mm(bank[:, 3 + h % 2, r * SEQ:(r + 1) * SEQ], zT[:, h % 2, r * P:(r + 1) * P], kvrT[:],
                                       start=True, stop=True, skip_group_check=True)
                            o.then_inc(sx_ready, 1)
                        if 2 <= i < NH + 2:
                            h = i - 2
                            e = h % 2
                            pe.wait_ge(pxT_ready, b * NH + (h + 1))
                            if h >= 1:
                                pe.wait_ge(cn_ready, b * NH + h)
                            for r in range(2):
                                for k in range(2):
                                    o = mm(bank[:, 6, r * P + e * DC:r * P + (e + 1) * DC], pxT[:, h % 2, k, r * P:(r + 1) * P],
                                           kvr[:, k, :], start=(k == 0), stop=(k == 1), skip_group_check=True)
                            o.then_inc(cx_psum, 1)
                        h = i - 3
                        if h >= 0 and h % 2 == 1:
                            j = h // 2
                            pe.wait_ge(cn_ready, b * NH + (h + 1))
                            if j >= 1:
                                pe.wait_ge(cT_ready, b * PAIRS + j)
                            for r in range(2):
                                o = tr(bank[:, 2, 256 + r * P:256 + (r + 1) * P], cn[:, j % 2, r, :], ident[:])
                            o.then_inc(cT_psum, 1)
                        h = i - 4
                        if h >= 0 and h % 2 == 1 or i == NH + 3:
                            jj = [h // 2] if h % 2 == 1 else []
                            for j in jj:
                                pe.wait_ge(cT_ready, b * PAIRS + (j + 1))
                                for r in range(2):
                                    o = mm(bank[:, 7, r * D:(r + 1) * D], cT[:, j % 2, r * P:(r + 1) * P], Cx[:, j, :],
                                           start=(j == 0 and r == 0), stop=(j == PAIRS - 1), skip_group_check=True)
                    o.then_inc(y_ready, 1)

            if STAGES > 5:
                pe.wait_ge(s_wm, 6 * 16)
                with pe.Fori(0, NB) as b:
                    turn_xn(b + 5 * NB)
                    for r in range(2):
                        for k in range(KD):
                            o = mm(bank[:, 0, r * NE:(r + 1) * NE], xnT[:, k, r * P:(r + 1) * P], gw[:, k, :],
                                   start=(k == 0), stop=(k == KD - 1), skip_group_check=True)
                    o.then_inc(lg_psum, 1)
                    for w, src in enumerate((sg, su)):
                        for f in range(2):
                            for k in range(KD):
                                o = mm(bank[:, 1 + w, f * SEQ:(f + 1) * SEQ], src[:, k, f * P:(f + 1) * P], xnT[:, k, :],
                                       start=(k == 0), stop=(k == KD - 1), skip_group_check=True)
                    o.then_inc(sh_psum, 1)
                    pe.wait_ge(shh_ready, b + 1)
                    for r in range(2):
                        for f in range(2):
                            o = mm(bank[:, 3, r * D:(r + 1) * D], sh_h[:, f, r * P:(r + 1) * P], sd[:, f, :],
                                   start=(f == 0), stop=(f == 1), skip_group_check=True)
                    o.then_inc(y_ready, 1)
                pe.wait_ge(mask_ready, 1)
                mm(bank[:, 4, 0:NT * NE], before, mask.rearrange("p t e -> p (t e)"), start=True, stop=False)
                mm(bank[:, 4, 0:NT * NE], ones[:], seen.rearrange("p t e -> p (t e)"), start=False,
                   stop=True).then_inc(pos_psum, 1)
                for c in range(NC):
                    i = c % 2
                    if c > 0:
                        pe.wait_ge(x_done, 6 * NB + 4 * c)
                    else:
                        pe.wait_ge(xn_kept, NB)
                    for t in range(NT):
                        pe.wait_ge(hot_ready, NT * c + t + 1)
                        for k in range(KD):
                            o = mm(bank[:, k, :], XN[:, t, k * P:(k + 1) * P], hot[:, t, :], start=(t == 0), stop=(t == NT - 1))
                    o.then_inc(gat_psum, 1)
                    for t in range(NT):
                        n = NT * c + t
                        pe.wait_ge(hotw_ready, n + 1)
                        if n >= 2:
                            pe.wait_ge(hotT_ready, n - 1)
                        for k in range(KS):
                            o = tr(bank[:, 2 + t % 2, k * P:(k + 1) * P], hotw[:, t, k * P:(k + 1) * P], ident[:])
                        o.then_inc(hotT_psum, 1)
                    pe.wait_ge(buf_ready, c + 1)
                    pe.wait_ge(experts_in[i], 16 * 3 * (c // 2 + 1))
                    for w in range(2):
                        for e in range(EC):
                            for k in range(KD):
                                o = mm(bank[:, 4 + w, e * CAP:(e + 1) * CAP],
                                       ew[:, i, w, (KD * e + k) * FE:(KD * e + k + 1) * FE], bufT[:, k, e * CAP:(e + 1) * CAP],
                                       start=(k == 0), stop=(k == KD - 1), skip_group_check=True)
                    o.then_inc(eh_psum, 1)
                    pe.wait_ge(eh_ready, c + 1)
                    for e in range(EC):
                        s, half = e // 2, CAP * (e % 2)
                        o = mm(bank[half:half + CAP, 6 + s // 2, (s % 2) * D:(s % 2 + 1) * D], h_T[:, e * CAP:(e + 1) * CAP],
                               ew[:, i, 2, e * D:(e + 1) * D], start=True, stop=True, skip_group_check=True)
                    o.then_inc(ob_psum, 1)
                    pe.wait_ge(ob_ready, c + 1)
                    pe.wait_ge(hotT_ready, NT * (c + 1))
                    for q in range(NT // 2):
                        n = c * (NT // 2) + q
                        if q >= 2:
                            pe.wait_ge(x_done, 6 * NB + n - 1)
                        for r in range(2):
                            for s in range(KS):
                                o = mm(bank[:, n % 2, r * D:(r + 1) * D], hotT[:, 2 * q + r, s, :], ob[:, s, :],
                                       start=(s == 0), stop=(s == KS - 1), skip_group_check=True)
                        o.then_inc(ey_psum, 1)


def kernel(x, ctx_512, L0_attn_w_project, L0_attn_w_out, L0_xattn_W_k, L0_xattn_b_k, L0_xattn_ln_gamma, L0_xattn_ln_beta,
           L0_ffn_w1, L0_ffn_w2, L0_ffn_w3, L1_attn_Wq, L1_attn_Wk, L1_attn_Wv, L1_attn_Wproj, L1_xattn_Wq,
           L1_xattn_w_kc_q, L1_xattn_w_kc_kv, L1_xattn_W_qr, L1_xattn_W_kr, L1_xattn_Wo, L1_ffn_gate_w,
           L1_ffn_gate_bias, L1_ffn_w1, L1_ffn_w2, L1_ffn_w3, L1_ffn_shared_gate, L1_ffn_shared_up, L1_ffn_shared_down):
    import numpy as np
    import concourse.bacc as bacc
    from concourse.bass_utils import run_bass_kernel_spmd as run

    f = np.float32
    C = np.ascontiguousarray

    def angles(dim, length):
        inv = (f(1.0) / np.power(f(10000.0), np.arange(0, dim, 2, dtype=f) / f(dim))).astype(f)
        return np.arange(length, dtype=f)[:, None] * inv[None, :]

    t1 = np.concatenate([angles(HD, SEQ)] * 2, axis=1)
    sign1 = np.where(np.arange(HD) < HD // 2, f(-1), f(1))
    tq = np.repeat(angles(CQ, SEQ), 2, axis=1)
    sq = np.sin(tq)
    sinq = np.concatenate([sq[:, HC:], -sq[:, :HC]], axis=1)
    tk = np.repeat(angles(DC, SEQ), 2, axis=1)
    signk = np.where(np.arange(DC) < DC // 2, f(-1), f(1))
    n = np.arange(P)
    later = np.concatenate([
        (n[:, None] < n[None, :]).astype(f),
        np.broadcast_to(np.arange(NE, dtype=f), (P, NE)),
        np.broadcast_to(np.arange(CAP, dtype=f), (P, CAP)),
        np.broadcast_to((np.arange(NG)[None, :] < np.arange(NG)[:, None]).astype(f).ravel(), (P, NG * NG))], axis=1)
    consts = {
        "ident": np.eye(P, dtype=f),
        "causal": np.where(n[None, :] > n[:, None], f(-1e9), f(0)),
        "parity": np.stack([(n // HD) % 2 == 0, (n // HD) % 2 == 1], axis=1).astype(f),
        "cos1": np.cos(t1), "sin1": np.sin(t1) * sign1,
        "cosq": np.cos(tq).T, "sinq": sinq.T,
        "cosk": np.cos(tk), "sink": np.sin(tk) * signk,
        "later": later,
    }
    A = np.asarray

    def rows(w, k):
        return w.reshape(NC, EC, k, P, w.shape[2]).transpose(0, 3, 1, 2, 4).reshape(NC * P, EC * k * w.shape[2])

    arrays = {
        "x": A(x).reshape(NB * SEQ, D),
        "ctx": A(ctx_512).reshape(NB * SEQ, DC),
        "ctxT": A(ctx_512).reshape(NB * SEQ, DC).T,
        "w_qkv0": A(L0_attn_w_project).T, "w_o0": A(L0_attn_w_out).T,
        "w_k": A(L0_xattn_W_k).T, "b_k": A(L0_xattn_b_k), "gamma": A(L0_xattn_ln_gamma), "beta": A(L0_xattn_ln_beta),
        "w_f1": A(L0_ffn_w1).T, "w_f2": A(L0_ffn_w2).T, "w_f3": A(L0_ffn_w3).T,
        "w_qkv1": np.concatenate([A(L1_attn_Wq), A(L1_attn_Wk), A(L1_attn_Wv)], axis=1), "w_o1": A(L1_attn_Wproj),
        "w_xq": A(L1_xattn_Wq), "w_cq": A(L1_xattn_w_kc_q).reshape(NH * P, CQ),
        "w_ckv": A(L1_xattn_w_kc_kv).reshape(NH * P, DC), "w_xo": A(L1_xattn_Wo).T,
        "w_qr": A(L1_xattn_W_qr).transpose(2, 0, 1).reshape(64, NH * CQ),
        "w_kr": A(L1_xattn_W_kr).transpose(2, 0, 1).reshape(64, NH * DC),
        "w_gate": A(L1_ffn_gate_w).T, "b_gate": A(L1_ffn_gate_bias),
        "w_e": np.concatenate([rows(A(L1_ffn_w1), KD), rows(A(L1_ffn_w3), KD), rows(A(L1_ffn_w2), 1)], axis=1),
        "w_sg": A(L1_ffn_shared_gate), "w_su": A(L1_ffn_shared_up), "w_sd": A(L1_ffn_shared_down),
    }
    arrays.update({k: v.astype(f) for k, v in consts.items()})
    arrays = {k: C(v) for k, v in arrays.items()}
    nc = bacc.Bacc("TRN2", target_bir_lowering=False, num_devices=1)
    aps = {k: nc.dram_tensor("in_" + k, v.shape, mybir.dt.from_np(v.dtype), kind="ExternalInput").ap() for k, v in arrays.items()}
    out = nc.dram_tensor("out_x", (NB * SEQ, D), F32, kind="ExternalOutput").ap()
    build(nc, aps, out)
    r = run(nc, [{"in_" + k: v for k, v in arrays.items()}], core_ids=[0])
    return r.results[0]["out_x"].reshape(NB, SEQ, D)
```

```python
from contextlib import ExitStack

import concourse.bass as bass
from concourse import mybir

F32 = mybir.dt.float32
BF16 = mybir.dt.bfloat16
F32R = mybir.dt.float32r
U32 = mybir.dt.uint32
ALU = mybir.AluOpType
ACT = mybir.ActivationFunctionType
AX = mybir.AxisListType

P = 128
D = 256
NB = 4
SEQ = 256
KD = D // P
NT = NB * SEQ // P
NH = 16
HD = D // NH
PAIRS = NH // 2
FF = 1024
GRP = 64
QB = 127.0
ROUND = 12582912.0
DC = 64
CQ = 192
HC = CQ // 2
NE = 32
TOPK = 4
NG = 4
EG = NE // NG
FE = 128
FS = 256
CAP = 2 * (2 * 128 * TOPK // NE)
EC = 8
NC = NE // EC
SLOTS = EC * CAP
KS = SLOTS // P
STAGES = 6


class Steps:

    def __init__(self, eng, sem):
        self.eng, self.sem, self.done, self.shift = eng, sem, 0, 0

    def mark(self, ins):
        ins.then_inc(self.sem, 1)
        self.done += 1

    def wait(self):
        self.eng.wait_ge(self.sem, self.shift + self.done)

    def wait_apart(self, scrap):
        self.wait()
        self.eng.memset(scrap, 0.0)

    def loop(self, i, first, per):
        self.shift, self.done, self.first, self.per = i * per + first, 0, first, per

    def end(self, count, name):
        assert self.done == self.per, (name, "increments in an iteration:", self.done)
        self.shift, self.done = 0, self.first + count * self.per


UNITS = NB * PAIRS
CROSS = NB * NH


def slots():
    for u in range(-2 * PAIRS, UNITS + PAIRS):
        yield u, u // PAIRS, u % PAIRS


def cross_slots():
    for u in range(-1, CROSS + 4):
        yield u, u // NH, u % NH


def build(nc, a, out):
    ctx = ExitStack()
    with ctx:
        def sb(name, shape, dt=F32):
            return ctx.enter_context(nc.sbuf_tensor(name, shape, dt))

        def sem(name):
            return ctx.enter_context(nc.semaphore(name))

        room = (nc.sbuf_base + 31) // 32 * 32
        sb("shared_room", [P, 4096])

        def at(name, shape, start, dt=F32):
            return nc.alloc_sbuf_tensor_at(name, shape, dt, offset=room + start)

        bank = ctx.enter_context(nc.psum_tensor("bank", [P, 8, 512], F32))
        X = sb("X", [P, NT, D])
        ident = sb("ident", [P, P])
        ident_h = sb("ident_h", [P, P], BF16)
        causal = sb("causal", [P, P])
        causal_h = sb("causal_h", [P, P], BF16)
        head_rows = sb("head_rows", [P, 8])
        ones = sb("ones", [P, P])
        halfneg = sb("halfneg", [P, 2])
        epsilons = sb("epsilons", [P, 4])
        scrap = sb("scrap", [P, 1])
        stat = sb("stat", [P, 2, 6])
        mv = sb("mv", [P, 2, 2])
        veps = sb("veps", [P, 2])
        rstd = sb("rstd", [P, 2])
        xns = sb("xns", [P, 2, 2, D])
        xn = xns[:, 0]
        xnTs = sb("xnTs", [P, 2, KD, SEQ])
        xnT = xnTs[:, 0]
        wqkv1 = sb("wqkv1", [P, KD, 384])
        wo1 = sb("wo1", [P, KD, D])
        cos1 = sb("cos1", [P, 2, HD])
        sin1 = sb("sin1", [P, 2, HD])
        qT = at("qT", [P, 2, KD, SEQ], 0)
        kT = at("kT", [P, 2, KD, SEQ], 4096)
        V = at("V", [P, 2, 2, D], 8192)
        nmax = sb("nmax", [P, 2, 4])
        asums = sb("asums", [P, 2, 2, NH])
        sums = sb("sums", [P, 2, NH])
        rsum = sb("rsum", [P, 2, NH])
        work = sb("work", [P, 14 * 512])
        prob = work[:, 0:1536].rearrange("p (i e k n) -> p i e k n", i=2, e=2, k=3)
        probT = work[:, 1536:3072].rearrange("p (i m n) -> p i m n", i=2, m=6)
        On = at("On", [P, 2, D], 12288)
        OT = at("OT", [P, KD, SEQ], 14336)
        qk_c = work[:, 3072:3712].rearrange("p (r n) -> p r n", r=2)
        qk_s = work[:, 3712:4352].rearrange("p (r n) -> p r n", r=2)
        q_r = work[:, 4352:4864].rearrange("p (r n) -> p r n", r=2)
        k_r = work[:, 4864:5376].rearrange("p (r n) -> p r n", r=2)
        kM = work[:, 5376:6400].rearrange("p (i e n) -> p i e n", i=2, e=2)
        ctxT = sb("ctxT", [DC, NB, SEQ])
        ctxk = sb("ctxk", [P, NT, DC])
        wk = sb("wk", [DC, DC])
        bk_col = sb("bk_col", [DC, 1])
        bk_row = sb("bk_row", [P, DC])
        gamma = sb("gamma", [P, D])
        beta = sb("beta", [P, D])
        ctb = sb("ctb", [DC, SEQ])
        kvT = sb("kvT", [DC, SEQ])
        kvj = sb("kvj", [P, 2, DC])
        outT = sb("outT", [DC, SEQ])
        simn = work[:, 0:512].rearrange("p (r n) -> p r n", r=2)
        simg = work[:, 512:1024].rearrange("p (r n) -> p r n", r=2)
        prob_x = work[:, 1024:1536].rearrange("p (r n) -> p r n", r=2)
        early = sb("early", [P, 2 * EC * 768])
        wqkv0 = early[:, 0:1536].rearrange("p (k n) -> p k n", k=KD)
        wo0 = early[:, 1536:2048].rearrange("p (k n) -> p k n", k=KD)
        w_ff = early[:, 2048:2048 + 6144]
        s1 = w_ff[:, 0:2048].rearrange("p (k n) -> p k n", k=KD)
        s2 = w_ff[:, 2048:4096].rearrange("p (k n) -> p k n", k=KD)
        s3 = w_ff[:, 4096:6144].rearrange("p (k n) -> p k n", k=FF // P)
        Aq = early[:, 0:6144].rearrange("p (h k n) -> p h k n", h=NH, k=KD)
        Gq = early[0:HC, 6144:10240].rearrange("p (m e n) -> p m e n", m=2 * NH, e=2)
        Cx = early[:, 10240:12288].rearrange("p (j n) -> p j n", j=PAIRS)
        hot = early[:, 0:4096].rearrange("p (t n) -> p t n", t=NT)
        hotw = early[:, 4096:8192].rearrange("p (t n) -> p t n", t=NT)
        hotT = early[:, 8192:12288].rearrange("p (t k n) -> p t k n", t=NT, k=KS)
        wabs = sb("wabs", [P, 3])
        wmean = sb("wmean", [P, 3])
        gmax = sb("gmax", [P, 2, 16])
        grcp = sb("grcp", [P, 2, 16])
        gscl = sb("gscl", [P, 2, 16])
        xq = xn
        gate_f = work[:, 0:2048].rearrange("p (r n) -> p r n", r=2)
        hid = work[:, 2048:4096].rearrange("p (r n) -> p r n", r=2)
        hidT = work[:, 4096:6144].rearrange("p (r m n) -> p r m n", r=2, m=8)
        raw = sb("raw", [P, 16384])
        wq_x = raw[:, 0:4096].rearrange("p (h n) -> p h n", h=NH)
        wcq = raw[:, 4096:7168].rearrange("p (h n) -> p h n", h=NH)
        wckv = raw[:, 7168:8192].rearrange("p (h n) -> p h n", h=NH)
        wo_x = raw[:, 8192:12288].rearrange("p (h n) -> p h n", h=NH)
        wqr = raw[0:64, 12288:15360].rearrange("p (h n) -> p h n", h=NH)
        wkr = raw[0:64, 15360:16384].rearrange("p (h n) -> p h n", h=NH)
        cosq = sb("cosq", [HC, 2, SEQ])
        sinq = sb("sinq", [HC, 2, SEQ])
        cosk = sb("cosk", [P, 2, DC])
        sink = sb("sink", [P, 2, DC])
        kvr = at("kvr", [P, NT, 2, DC], 10240)
        kk = at("kk", [P, NB, 2, SEQ], 0, F32R)
        zz = at("zz", [P, 2, SEQ], 8192, F32R)
        kv_c = work[:, 0:512].rearrange("p (b r n) -> p b r n", b=NB, r=2)
        kv_s = work[:, 512:1024].rearrange("p (b r n) -> p b r n", b=NB, r=2)
        qx_c = work[0:HC, 256:1280].rearrange("p (i f n) -> p i f n", i=2, f=2)
        qx_s = work[0:HC, 1280:2304].rearrange("p (i f n) -> p i f n", i=2, f=2)
        qx_r = work[0:HC, 2304:3328].rearrange("p (i f n) -> p i f n", i=2, f=2)
        px = work[:, 3840:4864].rearrange("p (i r n) -> p i r n", i=2, r=2)
        pxT = work[:, 4864:5888].rearrange("p (i k n) -> p i k n", i=2, k=2)
        cn = work[:, 5888:6400].rearrange("p (i r n) -> p i r n", i=2, r=2)
        cT = work[:, 6400:6912].rearrange("p (i n) -> p i n", i=2)
        ew = raw[:, 0:12288].rearrange("p (i w n) -> p i w n", i=2, w=3)
        XN = raw[:, 12288:14336].rearrange("p (t n) -> p t n", t=NT)
        bufT = raw[:, 14336:15360].rearrange("p (k n) -> p k n", k=KD)
        ob = raw[:, 15360:16384].rearrange("p (k n) -> p k n", k=KS)
        gw = sb("gw", [P, KD, NE])
        gbias = sb("gbias", [P, NE])
        sg = sb("sg", [P, KD, FS])
        su = sb("su", [P, KD, FS])
        sd = sb("sd", [P, KD, D])
        later = sb("later", [P, 128 + 32 + 64 + 16])
        before = later[:, 0:128]
        iota_e = later[:, 128:160]
        iota_s = later[:, 160:224]
        earlier = later[:, 224:240]
        sh_g = work[:, 0:512].rearrange("p (f n) -> p f n", f=2)
        sh_h = work[:, 512:1024].rearrange("p (f n) -> p f n", f=2)
        h_g = work[:, 0:512]
        h_T = work[:, 512:1024]
        lg = sb("lg", [P, NT, NE])
        sc = work[:, 1024:1280].rearrange("p (t e) -> p t e", t=NT)
        scb = work[:, 1280:1536].rearrange("p (t e) -> p t e", t=NT)
        top_g = work[:, 1536:1792].rearrange("p (g n) -> p g n", g=NT * NG)
        gs = work[:, 1792:1824].rearrange("p (t g) -> p t g", t=NT)
        cmp_a = work[:, 1824:1952].rearrange("p (t g k) -> p t g k", t=NT, g=NG)
        cmp_b = work[:, 1952:2080].rearrange("p (t g k) -> p t g k", t=NT, g=NG)
        rank = work[:, 2080:2112]
        tmp_e = work[:, 2112:2368].rearrange("p (t e) -> p t e", t=NT)
        top_e = work[:, 2368:2432].rearrange("p (t k) -> p t k", t=NT)
        idx_f = work[:, 2432:2496].rearrange("p (t k) -> p t k", t=NT)
        pick = work[:, 2496:3520].rearrange("p (t e k) -> p t e k", t=NT, e=NE)
        mask = work[:, 3520:3776].rearrange("p (t e) -> p t e", t=NT)
        seen = work[:, 3776:4032].rearrange("p (t e) -> p t e", t=NT)
        wsum = work[:, 4032:4040]
        wrcp = work[:, 4040:4048]
        wgt = work[:, 4048:4304].rearrange("p (t e) -> p t e", t=NT)
        keep = work[:, 4304:4560].rearrange("p (t e) -> p t e", t=NT)
        posm = work[:, 4560:4816].rearrange("p (t e) -> p t e", t=NT)
        idx_u = sb("idx_u", [P, NT, 8], U32)

        s_x = sem("s_x")
        s_const = sem("s_const")
        s_w0 = sem("s_w0")
        s_ctx = sem("s_ctx")
        s_wff = sem("s_wff")
        s_w1 = sem("s_w1")
        s_wx = sem("s_wx")
        s_wm = sem("s_wm")
        experts_in = [sem(f"experts_in{i}") for i in range(2)]
        s_out = sem("s_out")
        setup = sem("setup")
        casts = sem("casts")
        mv_ready = sem("mv_ready")
        veps_ready = sem("veps_ready")
        rstd_ready = sem("rstd_ready")
        xn_ready = sem("xn_ready")
        xnTp_ready = sem("xnTp_ready")
        xnT_ready = sem("xnT_ready")
        x_done = sem("x_done")
        dve_steps = [sem(f"dve_steps{p}") for p in range(6)]
        proj = [sem(f"proj{l}") for l in range(2)]
        rope_parts = sem("rope_parts")
        rope_left = sem("rope_left")
        roped = sem("roped")
        q_ready = [sem(f"q_ready{l}") for l in range(2)]
        k_ready = [sem(f"k_ready{l}") for l in range(2)]
        v_ready = [sem(f"v_ready{l}") for l in range(2)]
        kM_ready = [sem(f"kM_ready{l}") for l in range(2)]
        s_ready = [sem(f"s_ready{l}") for l in range(2)]
        max_ready = [sem(f"max_ready{l}") for l in range(2)]
        p_ready = [sem(f"p_ready{l}") for l in range(2)]
        pT_psum = [sem(f"pT_psum{l}") for l in range(2)]
        pT4_ready = [sem(f"pT4_ready{l}") for l in range(2)]
        pT5_ready = [sem(f"pT5_ready{l}") for l in range(2)]
        av_done = [sem(f"av_done{l}") for l in range(2)]
        on_ready = [sem(f"on_ready{l}") for l in range(2)]
        oT_psum = [sem(f"oT_psum{l}") for l in range(2)]
        oT_ready = [sem(f"oT_ready{l}") for l in range(2)]
        y_ready = sem("y_ready")
        ctb_ready = sem("ctb_ready")
        kv_psum = sem("kv_psum")
        kvT_ready = sem("kvT_ready")
        kvj_ready = sem("kvj_ready")
        outT_psum = sem("outT_psum")
        outT_ready = sem("outT_ready")
        sim_ready = sem("sim_ready")
        smv_ready = sem("smv_ready")
        sveps_ready = sem("sveps_ready")
        srstd_ready = sem("srstd_ready")
        smax_pre = sem("smax_pre")
        smax_ready = sem("smax_ready")
        srcp_ready = sem("srcp_ready")
        x_half = sem("x_half")
        sexp_ready = sem("sexp_ready")
        wabs_ready = sem("wabs_ready")
        wmean_psum = sem("wmean_psum")
        sign_ready = sem("sign_ready")
        xq_ready = sem("xq_ready")
        hid_psum = sem("hid_psum")
        gate_ready = sem("gate_ready")
        hid_used = sem("hid_used")
        hq_ready = sem("hq_ready")
        hT_psum = sem("hT_psum")
        hT_ready = sem("hT_ready")
        fold_psum = sem("fold_psum")
        fold_act = sem("fold_act")
        fold_dve = sem("fold_dve")
        ctk_ready = sem("ctk_ready")
        kvr_ready = sem("kvr_ready")
        kvrT_psum = sem("kvrT_psum")
        kk_lead = sem("kk_lead")
        kk_ready = sem("kk_ready")
        qx_psum = sem("qx_psum")
        qx_cs = sem("qx_cs")
        qx_ready = sem("qx_ready")
        z_psum = sem("z_psum")
        z_ready = sem("z_ready")
        z_split = sem("z_split")
        kv_parts = sem("kv_parts")
        sx_ready = sem("sx_ready")
        mx_ready = sem("mx_ready")
        px_ready = sem("px_ready")
        pxT_psum = sem("pxT_psum")
        pxT_ready = sem("pxT_ready")
        cx_psum = sem("cx_psum")
        cn_ready = sem("cn_ready")
        cT_psum = sem("cT_psum")
        cT_ready = sem("cT_ready")
        xn_kept = sem("xn_kept")
        lg_psum = sem("lg_psum")
        lg_ready = sem("lg_ready")
        sh_psum = sem("sh_psum")
        shg_ready = sem("shg_ready")
        shh_ready = sem("shh_ready")
        esig_ready = sem("esig_ready")
        mask_ready = sem("mask_ready")
        pos_psum = sem("pos_psum")
        hot_ready = sem("hot_ready")
        hotw_ready = sem("hotw_ready")
        gat_psum = sem("gat_psum")
        buf_ready = sem("buf_ready")
        hotT_psum = sem("hotT_psum")
        hotT_ready = sem("hotT_ready")
        eh_psum = sem("eh_psum")
        eg_ready = sem("eg_ready")
        eh_ready = sem("eh_ready")
        ob_psum = sem("ob_psum")
        ob_ready = sem("ob_ready")
        ey_psum = sem("ey_psum")
        ey_used = sem("ey_used")

        block = ctx.enter_context(nc.Block())

        @block.sync
        def _(sp):
            def load(dst, src, s):
                sp.dma_start(dst, src).then_inc(s, 16)

            load(X[:], a["x"].rearrange("(t p) d -> p t d", p=P), s_x)
            load(ident[:], a["ident"], s_const)
            load(wqkv0, a["w_qkv0"].rearrange("(k p) n -> p k n", p=P), s_w0)
            load(causal[:], a["causal"], s_const)
            load(head_rows[:], a["head_rows"], s_const)
            load(wo0, a["w_o0"].rearrange("(k p) n -> p k n", p=P), s_w0)
            load(ctxT[:], a["ctxT"].rearrange("d (b s) -> d b s", b=NB), s_ctx)
            load(ctxk[:], a["ctx"].rearrange("(t p) d -> p t d", p=P), s_ctx)
            load(wk[:], a["w_k"], s_ctx)
            load(bk_col[:], a["b_k"].rearrange("(d o) -> d o", o=1), s_ctx)
            load(bk_row[:], a["b_k"].rearrange("(o d) -> o d", o=1).to_broadcast([P, DC]), s_ctx)
            load(gamma[:], a["gamma"].rearrange("(o d) -> o d", o=1).to_broadcast([P, D]), s_ctx)
            load(beta[:], a["beta"].rearrange("(o d) -> o d", o=1).to_broadcast([P, D]), s_ctx)
            load(s1, a["w_f1"].rearrange("(k p) n -> p k n", p=P), s_wff)
            load(s2, a["w_f2"].rearrange("(k p) n -> p k n", p=P), s_wff)
            load(s3, a["w_f3"].rearrange("(k p) n -> p k n", p=P), s_wff)
            load(wqkv1[:], a["w_qkv1"].rearrange("(k p) n -> p k n", p=P), s_w1)
            load(wo1[:], a["w_o1"].rearrange("(k p) n -> p k n", p=P), s_w1)
            load(cos1[:], a["cos1"].rearrange("(r p) n -> p r n", p=P), s_w1)
            load(sin1[:], a["sin1"].rearrange("(r p) n -> p r n", p=P), s_w1)
            load(wq_x, a["w_xq"].rearrange("(h p) n -> p h n", p=P), s_wx)
            load(wcq, a["w_cq"].rearrange("(h p) n -> p h n", p=P), s_wx)
            load(wckv, a["w_ckv"].rearrange("(h p) n -> p h n", p=P), s_wx)
            load(wo_x, a["w_xo"].rearrange("(h p) n -> p h n", p=P), s_wx)
            load(wqr, a["w_qr"].rearrange("r (h n) -> r h n", h=NH), s_wx)
            load(wkr, a["w_kr"].rearrange("r (h n) -> r h n", h=NH), s_wx)
            load(cosq[:], a["cosq"].rearrange("(f j) s -> j f s", j=HC), s_wx)
            load(sinq[:], a["sinq"].rearrange("(f j) s -> j f s", j=HC), s_wx)
            load(cosk[:], a["cosk"].rearrange("(r p) n -> p r n", p=P), s_wx)
            load(sink[:], a["sink"].rearrange("(r p) n -> p r n", p=P), s_wx)
            load(gw[:], a["w_gate"].rearrange("(k p) n -> p k n", p=P), s_wm)
            load(gbias[:], a["b_gate"].rearrange("(o d) -> o d", o=1).to_broadcast([P, NE]), s_wm)
            load(sg[:], a["w_sg"].rearrange("(k p) n -> p k n", p=P), s_wm)
            load(su[:], a["w_su"].rearrange("(k p) n -> p k n", p=P), s_wm)
            load(sd[:], a["w_sd"].rearrange("(k p) n -> p k n", p=P), s_wm)
            load(later[:], a["later"], s_wm)

            if STAGES > 5:
                sp.wait_ge(fold_act, NH + NH // 4 + PAIRS // 2)
                def load_chunk(i, c):
                    for w in range(3):
                        sp.dma_start(ew[:, i, w, :], a["w_e"][c * P:(c + 1) * P, w * 2048:(w + 1) * 2048]
                                     ).then_inc(experts_in[i], 16)
                load_chunk(0, 0)
                load_chunk(1, 1)
                for c in range(2, NC):
                    sp.wait_ge(ob_psum, c - 1)
                    load_chunk(c % 2, c)
            sp.wait_ge(x_done, NB * STAGES + (NC * NT // 2 if STAGES > 5 else 0))
            sp.dma_start(out.rearrange("(t p) d -> p t d", p=P), X[:]).then_inc(s_out, 16)
            sp.wait_ge(s_out, 16)

        @block.gpsimd
        def _(pool):
            pool.memset(ones[:], 1.0).then_inc(setup, 1)
            pool.memset(halfneg[:], -0.5).then_inc(setup, 1)
            pool.memset(epsilons[:, 0:2], 1e-5).then_inc(setup, 1)
            pool.memset(epsilons[:, 2:4], 1e-6).then_inc(setup, 1)
            pool.wait_ge(setup, 4)

            def rstd_of(n, eps, mv_s, veps_s, rstd_s):
                pool.wait_ge(mv_s, 2 * (n + 1))
                pool.tensor_tensor(veps[:], mv[:, :, 1], epsilons[:, 0:2] if eps == 1e-5 else epsilons[:, 2:4],
                                   ALU.add).then_inc(veps_s, 1)
                pool.wait_ge(veps_s, n + 1)
                pool.tensor_tensor(rstd[:], veps[:], halfneg[:], ALU.pow).then_inc(rstd_s, 1)

            def norm(n):
                rstd_of(n, 1e-5, mv_ready, veps_ready, rstd_ready)

            def attention(l):
                for u, b, j in slots():
                    v = u + 2
                    if 0 <= v < UNITS:
                        if v % PAIRS == 0:
                            pool.wait_ge(k_ready[l], v // PAIRS + 1)
                        if v >= 2:
                            pool.wait_ge(s_ready[l], 2 * (v - 1))
                        g, pj = (v % PAIRS) // 4, v % 4
                        for e in range(2):
                            pool.tensor_tensor(kM[:, v % 2, e, :], kT[:, (v // PAIRS) % 2, g, :],
                                               head_rows[:, 2 * pj + e:2 * pj + e + 1].to_broadcast([P, SEQ]),
                                               ALU.mult).then_inc(kM_ready[l], 1)
                    if j == 5 and b + 2 < NB:
                        norm(b + 2 + 3 * NB * l)

            pool.wait_ge(s_const, 3 * 16)
            attention(0)
            if STAGES > 1:
                pool.wait_ge(s_ctx, 7 * 16)
                with pool.Fori(0, NB) as b:
                    pool.tensor_copy(ctb[:].unsqueeze(1), ctxT[:, bass.ts(b, 1), :]).then_inc(ctb_ready, 1)
                    norm(b + NB)
                    rstd_of(b, 1e-6, smv_ready, sveps_ready, srstd_ready)
            if STAGES > 2:
                with pool.Fori(0, NB) as b:
                    norm(b + 2 * NB)
            if STAGES > 3:
                attention(1)
            if STAGES > 4:
                norm(4 * NB)
                for u, b, h in cross_slots():
                    v = u + 1
                    if 0 <= v < CROSS:
                        pool.wait_ge(qx_cs, 2 * (v + 1))
                        if v >= 2:
                            pool.wait_ge(z_psum, v - 1)
                        for f in range(2):
                            pool.tensor_tensor(qx_r[:, v % 2, f], qx_c[:, v % 2, f], qx_s[:, v % 2, 1 - f],
                                               ALU.add).then_inc(qx_ready, 1)
                    if h == 4 and 0 <= b < NB - 1:
                        norm(4 * NB + b + 1)
            if STAGES > 5:
                with pool.Fori(0, NB) as b:
                    norm(b + 5 * NB)
                    pool.wait_ge(xn_ready, b * 2 + (10 * NB + 2))
                    pool.tensor_copy(XN[:, bass.ts(b, 2), :], xn[:]).then_inc(xn_kept, 1)
                for c in range(NC):
                    for t in range(NT):
                        pool.wait_ge(hot_ready, NT * c + t + 1)
                        if c > 0:
                            pool.wait_ge(hotT_psum, NT * (c - 1) + t + 1)
                        pool.tensor_tensor(hotw[:, t].rearrange("p (e n) -> p e n", e=EC),
                                           hot[:, t].rearrange("p (e n) -> p e n", e=EC),
                                           wgt[:, t, c * EC:(c + 1) * EC].unsqueeze(2).to_broadcast([P, EC, CAP]),
                                           ALU.mult).then_inc(hotw_ready, 1)

        @block.scalar
        def _(act):
            act.preload_act_table(ACT.Exp)

            def copy_xnT(n):
                act.wait_ge(xnTp_ready, n + 1)
                act.activation(xnT[:], bank[:, 7, :].rearrange("p (k n) -> p k n", k=KD), ACT.Copy).then_inc(xnT_ready, 1)

            def attention(l):
                def exps(u):
                    i, b, j = u % 2, u // PAIRS, u % PAIRS
                    for r in range(2):
                        act.wait_ge(max_ready[l], 2 * u + r + 1)
                        if r == 0 and u >= 2:
                            act.wait_ge(pT_psum[l], u - 1)
                        if r == 0 and j == 0 and b >= 2:
                            act.wait_ge(on_ready[l], b - 1)
                        for e in range(2):
                            n = SEQ if r else P
                            dst = prob[:, i, e, 1:3, :].rearrange("p k n -> p (k n)") if r else prob[:, i, e, 0, :]
                            act.activation(dst, bank[:, 2 * i + r, e * n:(e + 1) * n], ACT.Exp,
                                           bias=nmax[:, i, 2 * r + e:2 * r + e + 1],
                                           accum_out=asums[:, b % 2, r, 2 * j + e:2 * j + e + 1]).then_inc(p_ready[l], 1)

                shared = bank[:, 7, :].rearrange("p (k n) -> p k n", k=KD)
                for u, b, j in slots():
                    if 0 <= u + 1 < UNITS:
                        exps(u + 1)
                    if 0 <= u < UNITS:
                        act.wait_ge(pT_psum[l], u + 1)
                        if u >= 2:
                            act.wait_ge(av_done[l], u - 1)
                        act.activation(probT[:, u % 2, 4:6, :], bank[:, 5, 0:256].rearrange("p (m n) -> p m n", m=2),
                                       ACT.Copy).then_inc(pT5_ready[l], 1)
                    n, i = b + 1, (b + 1) % 2
                    if 0 <= n < NB:
                        if j == 0:
                            copy_xnT(n + 3 * NB * l)
                        if j == (3 if l else 1):
                            act.wait_ge(proj[l], (4 * n + 3) if l else (3 * n + 1))
                            act.activation(qT[:, i], shared, ACT.Copy, scale=float(HD) ** -0.5).then_inc(q_ready[l], 1)
                        if j == (4 if l else 2):
                            act.wait_ge(proj[l], (4 * n + 4) if l else (3 * n + 2))
                            act.activation(kT[:, i], shared, ACT.Copy).then_inc(k_ready[l], 1)
                        if l == 0 and j == 3:
                            act.wait_ge(proj[l], 3 * n + 3)
                            act.activation(V[:, i], shared, ACT.Copy).then_inc(v_ready[l], 1)
                    if 0 <= b - 1 < NB and j == 5:
                        act.wait_ge(oT_psum[l], b)
                        act.activation(OT[:], shared, ACT.Copy).then_inc(oT_ready[l], 1)

            attention(0)

            if STAGES > 1:
                with act.Fori(0, NB) as b:
                    copy_xnT(b + NB)
                    act.wait_ge(kv_psum, b + 1)
                    act.activation(kvT[:], bank[0:DC, 0, 0:SEQ], ACT.Identity, bias=bk_col[:, 0:1]).then_inc(kvT_ready, 1)
                    act.wait_ge(outT_psum, b + 1)
                    act.activation(outT[:], bank[0:DC, 2, 0:SEQ], ACT.Copy, scale=float(D) ** -0.5).then_inc(outT_ready, 1)
                    act.wait_ge(smax_ready, b + 1)
                    for r in range(2):
                        act.activation(prob_x[:, r, :], simg[:, r, :], ACT.Exp, bias=nmax[:, 0, r:r + 1],
                                       accum_out=sums[:, r, 0:1]).then_inc(sexp_ready, 1)

            if STAGES > 2:
                act.preload_act_table(ACT.Silu)
                act.wait_ge(wabs_ready, 3)
                for w in (s1, s2, s3):
                    act.activation(w, w, ACT.Sign).then_inc(sign_ready, 1)
                act.wait_ge(wmean_psum, 1)
                act.activation(wmean[:], bank[:, 6, 0:3], ACT.Copy, scale=1.0 / (D * FF)).then_inc(sign_ready, 1)
                act.wait_ge(sign_ready, 4)
                with act.Fori(0, NB) as b:
                    copy_xnT(b + 2 * NB)
                    for r in range(2):
                        for c in range(2):
                            act.wait_ge(hid_psum, b * 4 + (2 * r + c + 1))
                            act.activation(gate_f[:, r, c * 512:(c + 1) * 512], bank[:, 2 * c, :], ACT.Silu,
                                           scale=wmean[:, 0:1]).then_inc(gate_ready, 1)
                    for r in range(2):
                        act.wait_ge(hT_psum, b * 2 + (r + 1))
                        act.activation(hidT[:, r], bank[:, 4:6, :].rearrange("p a (m n) -> p (a m) n", m=4),
                                       ACT.Copy).then_inc(hT_ready, 1)

            if STAGES > 3:
                act.preload_act_table(ACT.Exp)
                attention(1)

            if STAGES > 4:
                for h in range(NH):
                    act.wait_ge(fold_psum, h + 1)
                    act.activation(Aq[:, h], bank[:, h % 2, 0:2 * CQ].rearrange("p (k n) -> p k n", k=KD),
                                   ACT.Copy).then_inc(fold_act, 1)
                for g in range(NH // 4):
                    act.wait_ge(fold_psum, NH + g + 1)
                    act.activation(Gq[:, 8 * g:8 * g + 8], bank[0:HC, g % 2, :].rearrange("p (m n) -> p m n", m=8).unsqueeze(
                        2).to_broadcast([HC, 8, 2, DC]), ACT.Copy).then_inc(fold_act, 1)
                for g in range(PAIRS // 2):
                    act.wait_ge(fold_psum, NH + NH // 4 + g + 1)
                    act.activation(Cx[:, 2 * g:2 * g + 2], bank[:, g % 2, :].rearrange("p (j n) -> p j n", j=2),
                                   ACT.Copy).then_inc(fold_act, 1)
                act.wait_ge(kvrT_psum, 1)
                act.activation(kk[:, :, 0, :], bank[:, 5:7, :].rearrange("p a (b n) -> p (a b) n", b=2), ACT.Copy).then_inc(kk_lead, 1)
                copy_xnT(4 * NB)
                for u, b, h in cross_slots():
                    w = u - 4
                    if w >= 0 and w % 2 == 1:
                        j = w // 2
                        act.wait_ge(cT_psum, j + 1)
                        act.activation(cT[:, j % 2], bank[:, 2, 256:512], ACT.Copy).then_inc(cT_ready, 1)
                    w = u - 1
                    if 0 <= w < CROSS:
                        act.wait_ge(mx_ready, w + 1)
                        if w >= 2:
                            act.wait_ge(pxT_psum, w - 1)
                        for r in range(2):
                            act.activation(px[:, w % 2, r, :], bank[:, 3 + w % 2, r * SEQ:(r + 1) * SEQ], ACT.Exp,
                                           bias=nmax[:, w % 2, r:r + 1],
                                           accum_out=sums[:, r, w % NH:w % NH + 1]).then_inc(px_ready, 1)
                    if 0 <= u < CROSS:
                        act.wait_ge(z_psum, u + 1)
                        if u >= 2:
                            act.wait_ge(sx_ready, u - 1)
                        act.activation(zz[:, u % 2], bank[:, 2, 0:SEQ], ACT.Copy).then_inc(z_ready, 1)
                    if 0 <= w < CROSS:
                        act.wait_ge(pxT_psum, w + 1)
                        if w >= 2:
                            act.wait_ge(cx_psum, w - 1)
                        act.activation(pxT[:, w % 2], bank[:, 5, :].rearrange("p (k n) -> p k n", k=2), ACT.Copy).then_inc(pxT_ready, 1)
                    if h == 8 and 0 <= b < NB - 1:
                        act.wait_ge(xnTp_ready, 4 * NB + b + 2)
                        act.activation(xnTs[:, (b + 1) % 2], bank[:, u % 2, :].rearrange("p (k n) -> p k n", k=KD),
                                       ACT.Copy).then_inc(xnT_ready, 1)

            if STAGES > 5:
                act.preload_act_table(ACT.Silu)
                with act.Fori(0, NB) as b:
                    copy_xnT(b + 5 * NB)
                    act.wait_ge(lg_psum, b + 1)
                    act.activation(lg[:, bass.ts(b, 2), :], bank[:, 0, 0:2 * NE].rearrange("p (r e) -> p r e", r=2),
                                   ACT.Copy).then_inc(lg_ready, 1)
                    act.wait_ge(sh_psum, b + 1)
                    act.activation(sh_g, bank[:, 1, :].rearrange("p (f n) -> p f n", f=2), ACT.Silu).then_inc(shg_ready, 1)
                act.preload_act_table(ACT.Exp)
                act.wait_ge(lg_ready, NB)
                act.activation(scb, lg[:], ACT.Exp, scale=-1.0).then_inc(esig_ready, 1)
                act.preload_act_table(ACT.Silu)
                for c in range(NC):
                    act.wait_ge(gat_psum, c + 1)
                    act.activation(bufT, bank[:, 0:2, :], ACT.Copy).then_inc(buf_ready, 1)
                    for t in range(NT):
                        act.wait_ge(hotT_psum, NT * c + t + 1)
                        act.activation(hotT[:, t], bank[:, 2 + t % 2, :].rearrange("p (k n) -> p k n", k=KS),
                                       ACT.Copy).then_inc(hotT_ready, 1)
                    act.wait_ge(eh_psum, c + 1)
                    act.activation(h_g, bank[:, 4, :], ACT.Silu).then_inc(eg_ready, 1)
                    act.wait_ge(ob_psum, c + 1)
                    act.activation(ob, bank[:, 6:8, :].rearrange("p a (k n) -> p (a k) n", k=2), ACT.Copy).then_inc(ob_ready, 1)

        @block.vector
        def _(dve):
            dve.wait_ge(s_const, 3 * 16)
            dve.tensor_copy(ident_h[:], ident[:]).then_inc(casts, 1)
            dve.tensor_copy(causal_h[:], causal[:]).then_inc(casts, 1)
            dve.wait_ge(s_x, 16)

            def norm(n, b, st):
                for r in range(2):
                    st.mark(dve.bn_stats(stat[:, r, :], X[:, bass.ts(b, 2), :][:, r, :]))
                st.wait_apart(scrap[:])
                for r in range(2):
                    dve.bn_aggr(mv[:, r, :], stat[:, r, :]).then_inc(mv_ready, 1)
                dve.wait_ge(mv_ready, 2 * n + 2)
                dve.wait_ge(rstd_ready, n + 1)
                for r in range(2):
                    dve.tensor_scalar(xn[:, r, :], X[:, bass.ts(b, 2), :][:, r, :], mv[:, r, 0:1], rstd[:, r:r + 1],
                                      ALU.subtract, ALU.mult).then_inc(xn_ready, 1)

            def add_y(n, b, col, scale=None):
                dve.wait_ge(y_ready, n + 1)
                xb = X[:, bass.ts(b, 2), :]
                y = col.rearrange("p (r n) -> p r n", r=2)
                if scale is None:
                    dve.tensor_tensor(xb, y, xb, ALU.add).then_inc(x_done, 1)
                else:
                    dve.scalar_tensor_tensor(xb, y, scale, xb, ALU.mult, ALU.add).then_inc(x_done, 1)

            def attention(l, st):
                def row_max(u):
                    i = u % 2
                    for r in range(2):
                        dve.wait_ge(s_ready[l], 2 * u + r + 1)
                        n = SEQ if r else P
                        dve.tensor_reduce(nmax[:, i, 2 * r:2 * r + 2],
                                          bank[:, 2 * i + r, 0:2 * n].rearrange("p (e n) -> p e n", e=2),
                                          AX.X, ALU.max, negate=True).then_inc(max_ready[l], 1)

                def stats(n):
                    for r in range(2):
                        st.mark(dve.bn_stats(stat[:, r, :], X[:, 2 * n + r, :]))
                    st.wait()
                    for r in range(2):
                        dve.bn_aggr(mv[:, r, :], stat[:, r, :]).then_inc(mv_ready, 1)

                def apply(n):
                    c = n + 3 * NB * l
                    dve.wait_ge(mv_ready, 2 * c + 2)
                    dve.wait_ge(rstd_ready, c + 1)
                    for r in range(2):
                        dve.tensor_scalar(xns[:, n % 2, r, :], X[:, 2 * n + r, :], mv[:, r, 0:1], rstd[:, r:r + 1],
                                          ALU.subtract, ALU.mult).then_inc(xn_ready, 1)

                def rope(n, r):
                    dve.wait_ge(proj[1], 4 * n + r + 1)
                    src = bank[:, 7, 0:320].rearrange("p (h n) -> p h n", n=HD)
                    c = qk_c[:, r, :].rearrange("p (h n) -> p h n", n=HD)
                    s = qk_s[:, r, :].rearrange("p (h n) -> p h n", n=HD)
                    dve.tensor_tensor(c, src, cos1[:, r, :].unsqueeze(1).to_broadcast([P, 20, HD]),
                                      ALU.mult).then_inc(rope_parts, 1)
                    for f in range(2):
                        o = 8 * f
                        dve.tensor_tensor(s[:, :, o:o + 8], src[:, :, 8 - o:16 - o],
                                          sin1[:, r, o:o + 8].unsqueeze(1).to_broadcast([P, 20, 8]),
                                          ALU.mult).then_inc(rope_parts, 1)
                    dve.tensor_copy(V[:, n % 2, r, 0:64], bank[:, 7, 320:384]).then_inc(rope_left, 1)
                    dve.wait_ge(rope_parts, 6 * n + 3 * r + 3)
                    dve.tensor_tensor(q_r[:, r, :], qk_c[:, r, 0:256], qk_s[:, r, 0:256], ALU.add).then_inc(roped, 1)
                    kc, ks = (v[:, r, 256:320].rearrange("p (g n) -> p g n", n=HD).unsqueeze(2).to_broadcast([P, 4, 4, HD])
                              for v in (qk_c, qk_s))
                    dve.tensor_tensor(k_r[:, r, :].rearrange("p (g m n) -> p g m n", g=4, m=4), kc, ks,
                                      ALU.add).then_inc(roped, 1)

                for u, b, j in slots():
                    if 0 <= u + 1 < UNITS:
                        row_max(u + 1)
                    if 0 <= u < UNITS:
                        dve.wait_ge(pT_psum[l], u + 1)
                        if u >= 2:
                            dve.wait_ge(av_done[l], u - 1)
                        dve.tensor_copy(probT[:, u % 2, 0:4, :], bank[:, 4, :].rearrange("p (m n) -> p m n", m=4)).then_inc(pT4_ready[l], 1)
                    n = b - 1
                    if 0 <= n < NB and j == 0:
                        dve.wait_ge(p_ready[l], 4 * PAIRS * (n + 1))
                        st.mark(dve.reciprocal(rsum[:], asums[:, n % 2]))
                        dve.wait_ge(av_done[l], PAIRS * (n + 1))
                        st.wait()
                        dve.tensor_tensor(On[:].rearrange("p r (h n) -> p r h n", h=NH),
                                          bank[:, 6, :].rearrange("p (r h n) -> p r h n", r=2, h=NH),
                                          rsum[:].unsqueeze(3).to_broadcast([P, 2, NH, HD]), ALU.mult).then_inc(on_ready[l], 1)
                    if l and j in (1, 2) and 0 <= b + 1 < NB:
                        rope(b + 1, j - 1)
                    if b + 2 < NB:
                        if j == 5:
                            stats(b + 2)
                        if j == 6:
                            apply(b + 2)
                    if 0 <= n < NB and j == 7:
                        dve.wait_ge(y_ready, n + 1 + 2 * NB * l)
                        dve.tensor_tensor(X[:, 2 * n:2 * n + 2, :], bank[:, 7, :].rearrange("p (r n) -> p r n", r=2),
                                          X[:, 2 * n:2 * n + 2, :], ALU.add).then_inc(x_done, 1)

            attention(0, Steps(dve, dve_steps[0]))

            if STAGES > 1:
                st = Steps(dve, dve_steps[1])
                with dve.Fori(0, NB) as b:
                    st.loop(b, 0, 7)
                    dve.wait_ge(x_done, b + 1)
                    norm(b + NB, b, st)
                    dve.wait_ge(kv_psum, b + 1)
                    dve.tensor_tensor(kvj[:], bank[:, 1, 0:2 * DC].rearrange("p (r n) -> p r n", r=2),
                                      bk_row[:].unsqueeze(1).to_broadcast([P, 2, DC]), ALU.add).then_inc(kvj_ready, 1)
                    dve.wait_ge(sim_ready, b + 1)
                    for r in range(2):
                        st.mark(dve.bn_stats(stat[:, r, :], bank[:, 3, r * SEQ:(r + 1) * SEQ]))
                    st.wait_apart(scrap[:])
                    for r in range(2):
                        dve.bn_aggr(mv[:, r, :], stat[:, r, :]).then_inc(smv_ready, 1)
                    dve.wait_ge(smv_ready, 2 * b + 2)
                    dve.wait_ge(srstd_ready, b + 1)
                    for r in range(2):
                        st.mark(dve.tensor_scalar(simn[:, r, :], bank[:, 3, r * SEQ:(r + 1) * SEQ], mv[:, r, 0:1],
                                                  rstd[:, r:r + 1], ALU.subtract, ALU.mult))
                    st.wait()
                    st.mark(dve.tensor_tensor(simg, simn, gamma[:].unsqueeze(1).to_broadcast([P, 2, D]), ALU.mult))
                    st.wait()
                    dve.tensor_tensor(simg, simg, beta[:].unsqueeze(1).to_broadcast([P, 2, D]), ALU.add).then_inc(smax_pre, 1)
                    dve.wait_ge(smax_pre, b + 1)
                    dve.tensor_reduce(nmax[:, 0, 0:2], simg, AX.X, ALU.max, negate=True).then_inc(smax_ready, 1)
                    dve.wait_ge(sexp_ready, 2 * b + 2)
                    dve.reciprocal(rsum[:, :, 0], sums[:, :, 0]).then_inc(srcp_ready, 1)
                    dve.wait_ge(srcp_ready, b + 1)
                    for r in range(2):
                        xb = X[:, bass.ts(b, 2), :][:, r, :]
                        o = dve.scalar_tensor_tensor(xb, prob_x[:, r, :], rsum[:, r, 0:1], xb, ALU.mult, ALU.add)
                        if r:
                            o.then_inc(x_done, 1)
                        else:
                            o.then_inc(x_half, 1)
                st.end(NB, "cross attention 0")

            if STAGES > 2:
                dve.wait_ge(s_wff, 3 * 16)
                for n in range(3):
                    dve.tensor_reduce(wabs[:, n:n + 1], w_ff[:, 2048 * n:2048 * (n + 1)], AX.X, ALU.add,
                                      apply_absolute_value=True).then_inc(wabs_ready, 1)

                def scales(m, k):
                    st.mark(dve.tensor_scalar_max(gscl[:, m, 0:k], gmax[:, m, 0:k], 1e-5))
                    st.wait()
                    st.mark(dve.reciprocal(grcp[:, m, 0:k], gscl[:, m, 0:k]))
                    st.wait()
                    st.mark(dve.tensor_scalar_mul(grcp[:, m, 0:k], grcp[:, m, 0:k], QB))
                    st.mark(dve.tensor_scalar_mul(gscl[:, m, 0:k], gscl[:, m, 0:k], 1.0 / QB))
                    st.wait()

                st = Steps(dve, dve_steps[2])
                with dve.Fori(0, NB) as b:
                    st.loop(b, 0, 23)
                    dve.wait_ge(x_done, b + (NB + 1))
                    norm(b + 2 * NB, b, st)
                    dve.wait_ge(xn_ready, b * 2 + (4 * NB + 2))
                    xg = xn[:].rearrange("p r (g n) -> p (r g) n", n=GRP)
                    st.mark(dve.tensor_reduce(gmax[:, 0, 0:8], xg, AX.X, ALU.max, apply_absolute_value=True))
                    st.wait()
                    scales(0, 8)
                    st.mark(dve.tensor_tensor(xg, xg, grcp[:, 0, 0:8].unsqueeze(2).to_broadcast([P, 8, GRP]), ALU.mult))
                    st.wait()
                    st.mark(dve.tensor_scalar(xg, xg, ROUND, -ROUND, ALU.add, ALU.add))
                    st.wait()
                    dve.tensor_tensor(xg, xg, gscl[:, 0, 0:8].unsqueeze(2).to_broadcast([P, 8, GRP]),
                                      ALU.mult).then_inc(xq_ready, 1)
                    def hidden(r):
                        for c in range(2):
                            dve.wait_ge(gate_ready, b * 4 + (2 * r + c + 1))
                            o = slice(c * 512, (c + 1) * 512)
                            dve.scalar_tensor_tensor(hid[:, r, o], bank[:, 2 * c + 1, :], wmean[:, 1:2], gate_f[:, r, o],
                                                     ALU.mult, ALU.mult).then_inc(hid_used, 1)
                    def quant(r):
                        hg = hid[:, r, :].rearrange("p (g n) -> p g n", n=GRP)
                        dve.wait_ge(hid_used, b * 4 + (2 * r + 2))
                        st.mark(dve.tensor_reduce(gmax[:, r, :], hg, AX.X, ALU.max, apply_absolute_value=True))
                        st.wait()
                        scales(r, 16)
                        st.mark(dve.tensor_tensor(hg, hg, grcp[:, r, :].unsqueeze(2).to_broadcast([P, 16, GRP]), ALU.mult))
                        st.wait()
                        st.mark(dve.tensor_scalar(hg, hg, ROUND, -ROUND, ALU.add, ALU.add))
                        st.wait()
                        dve.tensor_tensor(hg, hg, gscl[:, r, :].unsqueeze(2).to_broadcast([P, 16, GRP]),
                                          ALU.mult).then_inc(hq_ready, 1)
                    hidden(0)
                    quant(0)
                    hidden(1)
                    quant(1)
                    add_y(b + NB, b, bank[:, 6, :], wmean[:, 2:3])
                st.end(NB, "feed forward 0")

            if STAGES > 3:
                dve.wait_ge(s_w1, 4 * 16)
                dve.wait_ge(x_done, 3 * NB)
                attention(1, Steps(dve, dve_steps[3]))

            if STAGES > 4:
                dve.wait_ge(s_wx, 10 * 16)
                st = Steps(dve, dve_steps[4])
                src = ctxk[:].rearrange("p (b r) n -> p b r n", b=NB)
                dve.tensor_tensor(kv_c, src, cosk[:].unsqueeze(1).to_broadcast([P, NB, 2, DC]), ALU.mult).then_inc(kv_parts, 1)
                for f in range(2):
                    o = DC // 2 * f
                    dve.tensor_tensor(kv_s[:, :, :, o:o + 32], src[:, :, :, 32 - o:64 - o],
                                      sink[:, :, o:o + 32].unsqueeze(1).to_broadcast([P, NB, 2, 32]), ALU.mult).then_inc(kv_parts, 1)
                dve.wait_ge(kv_parts, 3)
                for e in range(2):
                    dve.tensor_tensor(kvr[:, :, e, :], kv_c.rearrange("p b r n -> p (b r) n"),
                                      kv_s.rearrange("p b r n -> p (b r) n"), ALU.add).then_inc(kvr_ready, 1)

                def cross_stats(b):
                    for r in range(2):
                        st.mark(dve.bn_stats(stat[:, r, :], X[:, 2 * b + r, :]))
                    st.wait()
                    for r in range(2):
                        dve.bn_aggr(mv[:, r, :], stat[:, r, :]).then_inc(mv_ready, 1)

                def cross_apply(b):
                    dve.wait_ge(mv_ready, 2 * (4 * NB + b) + 2)
                    dve.wait_ge(rstd_ready, 4 * NB + b + 1)
                    for r in range(2):
                        dve.tensor_scalar(xns[:, b % 2, r, :], X[:, 2 * b + r, :], mv[:, r, 0:1], rstd[:, r:r + 1],
                                          ALU.subtract, ALU.mult).then_inc(xn_ready, 1)

                dve.wait_ge(x_done, 4 * NB)
                cross_stats(0)
                cross_apply(0)
                dve.wait_ge(kk_lead, 1)
                dve.tensor_tensor(kk[:, :, 1, :], bank[:, 5:7, :].rearrange("p a (b n) -> p (a b) n", b=2),
                                  kk[:, :, 0, :].bitcast(F32), ALU.subtract).then_inc(kk_ready, 1)
                for u, b, h in cross_slots():
                    w = u - 1
                    if 0 <= w < CROSS:
                        dve.wait_ge(sx_ready, w + 1)
                        dve.tensor_reduce(nmax[:, w % 2, 0:2], bank[:, 3 + w % 2, :].rearrange("p (r n) -> p r n", r=2),
                                          AX.X, ALU.max, negate=True).then_inc(mx_ready, 1)
                    w = u + 1
                    if w < CROSS:
                        dve.wait_ge(qx_psum, w + 1)
                        if w >= 2:
                            dve.wait_ge(qx_ready, 2 * (w - 1))
                        q = bank[0:HC, w % 2, :].rearrange("p (f n) -> p f n", f=2)
                        dve.tensor_tensor(qx_c[:, w % 2], q, cosq[:], ALU.mult).then_inc(qx_cs, 1)
                        dve.tensor_tensor(qx_s[:, w % 2], q, sinq[:], ALU.mult).then_inc(qx_cs, 1)
                    if 0 <= u < CROSS:
                        dve.wait_ge(z_ready, u + 1)
                        dve.tensor_tensor(zz[DC:P, u % 2], bank[DC:P, 2, 0:SEQ], zz[DC:P, u % 2].bitcast(F32),
                                          ALU.subtract).then_inc(z_split, 1)
                    w = u - 2
                    if 0 <= w < CROSS:
                        j, e, k = w // 2, w % 2, w % NH
                        dve.wait_ge(px_ready, 2 * (w + 1))
                        st.mark(dve.reciprocal(rsum[:, :, k], sums[:, :, k]))
                        dve.wait_ge(cx_psum, w + 1)
                        if e == 0 and j >= 2:
                            dve.wait_ge(cT_psum, j - 1)
                        st.wait()
                        dve.tensor_tensor(cn[:, j % 2, :, e * DC:(e + 1) * DC],
                                          bank[:, 6, 0:256].rearrange("p (r n) -> p r n", r=2)[:, :, e * DC:(e + 1) * DC],
                                          rsum[:, :, k:k + 1].to_broadcast([P, 2, DC]), ALU.mult).then_inc(cn_ready, 1)
                    if 0 <= b < NB - 1:
                        if h == 4:
                            cross_stats(b + 1)
                        if h == 6:
                            cross_apply(b + 1)
                    if b >= 1 and h == 3:
                        dve.wait_ge(y_ready, 3 * NB + b)
                        xb = X[:, 2 * b - 2:2 * b, :]
                        dve.tensor_tensor(xb, bank[:, 7, :].rearrange("p (r n) -> p r n", r=2), xb, ALU.add).then_inc(x_done, 1)

            if STAGES > 5:
                dve.wait_ge(s_wm, 6 * 16)
                st = Steps(dve, dve_steps[5])
                with dve.Fori(0, NB) as b:
                    st.loop(b, 0, 2)
                    dve.wait_ge(x_done, b + (4 * NB + 1))
                    norm(b + 5 * NB, b, st)
                    dve.wait_ge(shg_ready, b + 1)
                    dve.tensor_tensor(sh_h, bank[:, 2, :].rearrange("p (f n) -> p f n", f=2), sh_g, ALU.mult).then_inc(shh_ready, 1)
                    add_y(b + 4 * NB, b, bank[:, 3, :])
                st.end(NB, "shared expert")

                def step(ins):
                    st.mark(ins)
                    st.wait()

                dve.wait_ge(esig_ready, 1)
                step(dve.tensor_scalar_add(scb, scb, 1.0))
                step(dve.reciprocal(sc, scb))
                step(dve.tensor_tensor(scb, sc, gbias[:].unsqueeze(1).to_broadcast([P, NT, NE]), ALU.add))
                for g in range(NT * NG):
                    st.mark(dve.max(top_g[:, g, :], scb[:, g // NG, EG * (g % NG):EG * (g % NG + 1)]))
                st.wait()
                step(dve.tensor_tensor(gs, top_g.rearrange("p (t g) n -> p t g n", t=NT)[:, :, :, 0],
                                       top_g.rearrange("p (t g) n -> p t g n", t=NT)[:, :, :, 1], ALU.add))
                other = gs.unsqueeze(2).to_broadcast([P, NT, NG, NG])
                own = gs.unsqueeze(3).to_broadcast([P, NT, NG, NG])
                st.mark(dve.tensor_tensor(cmp_a, other, own, ALU.is_gt))
                step(dve.tensor_tensor(cmp_b, other, own, ALU.is_equal))
                step(dve.tensor_tensor(cmp_b, cmp_b, earlier.rearrange("p (g k) -> p g k", g=NG).unsqueeze(1).to_broadcast(
                    [P, NT, NG, NG]), ALU.mult))
                step(dve.tensor_tensor(cmp_a, cmp_a, cmp_b, ALU.add))
                step(dve.tensor_reduce(rank, cmp_a.rearrange("p t g k -> p (t g) k"), AX.X, ALU.add))
                step(dve.tensor_scalar(rank, rank, 2.0, None, ALU.is_lt))
                step(dve.tensor_tensor(tmp_e.rearrange("p t (g n) -> p (t g) n", g=NG),
                                       scb.rearrange("p t (g n) -> p (t g) n", g=NG),
                                       rank.unsqueeze(2).to_broadcast([P, NT * NG, EG]), ALU.mult))
                for t in range(NT):
                    st.mark(dve.max(top_e[:, t, :], tmp_e[:, t, :]))
                st.wait()
                for t in range(NT):
                    st.mark(dve.max_index(idx_u[:, t, :], top_e[:, t, :], tmp_e[:, t, :]))
                st.wait()
                step(dve.tensor_copy(idx_f, idx_u[:]))
                for t in range(NT):
                    st.mark(dve.tensor_tensor(pick[:, t], iota_e.unsqueeze(2).to_broadcast([P, NE, TOPK]),
                                              idx_f[:, t, 0:TOPK].unsqueeze(1).to_broadcast([P, NE, TOPK]), ALU.is_equal))
                st.wait()
                st.mark(dve.tensor_reduce(mask, pick, AX.X, ALU.add))
                st.wait()
                st.mark(dve.memset(seen[:, 0], 0.0))
                st.wait()
                for t in range(1, NT):
                    if t < NT - 1:
                        step(dve.tensor_tensor(seen[:, t], seen[:, t - 1], mask[:, t - 1], ALU.add))
                    else:
                        dve.tensor_tensor(seen[:, t], seen[:, t - 1], mask[:, t - 1], ALU.add).then_inc(mask_ready, 1)
                step(dve.tensor_tensor(wgt, sc, mask, ALU.mult))
                step(dve.tensor_reduce(wsum, wgt, AX.X, ALU.add))
                step(dve.tensor_scalar_add(wsum, wsum, 1e-20))
                step(dve.reciprocal(wrcp, wsum))
                step(dve.tensor_scalar_mul(wrcp, wrcp, 2.0))
                step(dve.tensor_tensor(wgt, wgt, wrcp.unsqueeze(2).to_broadcast([P, NT, NE]), ALU.mult))
                dve.wait_ge(pos_psum, 1)
                pos = bank[:, 4, 0:NT * NE].rearrange("p (t e) -> p t e", t=NT)
                step(dve.scalar_tensor_tensor(keep, pos, float(CAP), mask, ALU.is_lt, ALU.mult))
                step(dve.scalar_tensor_tensor(posm, pos, 1.0, keep, ALU.add, ALU.mult))
                step(dve.tensor_scalar_add(posm, posm, -1.0))
                for c in range(NC):
                    for t in range(NT):
                        if c > 0:
                            dve.wait_ge(hotw_ready, NT * (c - 1) + t + 1)
                        if c > 0 and t == 0:
                            dve.wait_ge(gat_psum, c)
                        dve.tensor_tensor(hot[:, t].rearrange("p (e n) -> p e n", e=EC),
                                          iota_s.unsqueeze(1).to_broadcast([P, EC, CAP]),
                                          posm[:, t, c * EC:(c + 1) * EC].unsqueeze(2).to_broadcast([P, EC, CAP]),
                                          ALU.is_equal).then_inc(hot_ready, 1)
                    dve.wait_ge(eg_ready, c + 1)
                    dve.tensor_tensor(h_T, bank[:, 5, :], h_g, ALU.mult).then_inc(eh_ready, 1)
                    for q in range(NT // 2):
                        n = c * (NT // 2) + q
                        dve.wait_ge(ey_psum, n + 1)
                        xb = X[:, 2 * q:2 * q + 2, :]
                        dve.wait_ge(x_done, 6 * NB + max(0, n - 3))
                        dve.tensor_tensor(xb, bank[:, 0 + n % 2, :].rearrange("p (r n) -> p r n", r=2), xb,
                                          ALU.add).then_inc(x_done, 1)

        @block.tensor
        def _(pe):
            mm, tr = pe.matmul, pe.transpose
            pe.wait_ge(s_const, 3 * 16)
            pe.wait_ge(casts, 2)

            def turn_xn(n, ready=None, count=None, then=None):
                pe.wait_ge(xn_ready if ready is None else ready, 2 * n + 2 if ready is None else count)
                for k in range(KD):
                    for r in range(2):
                        o = tr(bank[:, 7, k * SEQ + r * P:k * SEQ + (r + 1) * P], xn[:, r, k * P:(k + 1) * P], ident[:])
                o.then_inc(xnTp_ready, 1)
                if then:
                    then()
                pe.wait_ge(xnT_ready, n + 1)

            def attention(l):
                def score(u):
                    b, j, i = u // PAIRS, u % PAIRS, u % 2
                    g = j // 4
                    pe.wait_ge(kM_ready[l], 2 * (u + 1))
                    if j == 0:
                        pe.wait_ge(q_ready[l], b + 1)
                    if u >= 2:
                        pe.wait_ge(p_ready[l], 4 * (u - 1))
                    for r in range(2):
                        n = SEQ if r else P
                        view = bank[:, 2 * i + r, 0:2 * n].rearrange("p (e n) -> p e n", e=2)
                        mm(view, qT[:, b % 2, g, r * P:(r + 1) * P], kM[:, i, :, 0:n],
                           start=True, stop=False, skip_group_check=True)
                        mm(view[:, :, n - P:n], ident_h[:], causal_h[:].unsqueeze(1).to_broadcast([P, 2, P]),
                           start=False, stop=True, skip_group_check=True).then_inc(s_ready[l], 1)

                def turn(u):
                    pe.wait_ge(p_ready[l], 4 * (u + 1))
                    if u >= 1:
                        pe.wait_ge(pT4_ready[l], u)
                        pe.wait_ge(pT5_ready[l], u)
                    for m in range(6):
                        o = tr(bank[:, 4 + m // 4, (m % 4) * P:(m % 4 + 1) * P], prob[:, u % 2, m // 3, m % 3, :], ident[:])
                    o.then_inc(pT_psum[l], 1)

                def values(u):
                    b, j = u // PAIRS, u % PAIRS
                    pe.wait_ge(pT4_ready[l], u + 1)
                    pe.wait_ge(pT5_ready[l], u + 1)
                    if j == 0:
                        if l:
                            pe.wait_ge(rope_left, 2 * (b + 1))
                        else:
                            pe.wait_ge(v_ready[l], b + 1)
                        if b >= 1:
                            pe.wait_ge(on_ready[l], b)
                    for e in range(2):
                        h = 2 * j + e
                        v = h // 4 if l else h
                        for m in range(3):
                            r, k = (0, 0) if m == 0 else (1, m - 1)
                            o = mm(bank[:, 6, r * D + h * HD:r * D + (h + 1) * HD], probT[:, u % 2, 3 * e + m, :],
                                   V[:, b % 2, k, v * HD:(v + 1) * HD], start=(m < 2), stop=(m != 1), skip_group_check=True)
                    o.then_inc(av_done[l], 1)

                def turned(src, done):
                    for k in range(KD):
                        for r in range(2):
                            o = tr(bank[:, 7, k * SEQ + r * P:k * SEQ + (r + 1) * P], src[:, r, k * P:(k + 1) * P], ident[:])
                    o.then_inc(done, 1)

                def front(n, j):
                    if j == 0:
                        pe.wait_ge(xn_ready, 2 * (n + 3 * NB * l) + 2)
                        if n >= 3:
                            pe.wait_ge(x_done, 3 * NB * l + n - 2)
                        turned(xns[:, n % 2], xnTp_ready)
                    elif j == 1:
                        pe.wait_ge(xnT_ready, n + 3 * NB * l + 1)
                    if l == 0 and j in (1, 2):
                        if j == 2:
                            pe.wait_ge(q_ready[0], n + 1)
                        m = j - 1
                        for g in range(2):
                            for k in range(KD):
                                o = mm(bank[:, 7, g * SEQ:(g + 1) * SEQ], wqkv0[:, k, m * D + g * P:m * D + (g + 1) * P],
                                       xnT[:, k, :], start=(k == 0), stop=(k == KD - 1), skip_group_check=True)
                        o.then_inc(proj[0], 1)
                    if l == 0 and j == 3:
                        pe.wait_ge(k_ready[0], n + 1)
                        for r in range(2):
                            for k in range(KD):
                                o = mm(bank[:, 7, r * D:(r + 1) * D], xnT[:, k, r * P:(r + 1) * P], wqkv0[:, k, 2 * D:3 * D],
                                       start=(k == 0), stop=(k == KD - 1), skip_group_check=True)
                        o.then_inc(proj[0], 1)
                    if l and j in (1, 2):
                        r = j - 1
                        if r:
                            pe.wait_ge(rope_left, 2 * n + 1)
                        for k in range(KD):
                            o = mm(bank[:, 7, 0:384], xnT[:, k, r * P:(r + 1) * P], wqkv1[:, k, :],
                                   start=(k == 0), stop=(k == KD - 1))
                        o.then_inc(proj[1], 1)
                    if l and j == 3:
                        pe.wait_ge(rope_left, 2 * n + 2)
                        pe.wait_ge(roped, 4 * n + 4)
                        turned(q_r, proj[1])
                    if l and j == 4:
                        pe.wait_ge(q_ready[1], n + 1)
                        turned(k_r, proj[1])

                def back(n, j):
                    if j == 5:
                        pe.wait_ge(on_ready[l], n + 1)
                        if n + 2 < NB:
                            pe.wait_ge(k_ready[l] if l else v_ready[l], n + 3)
                        turned(On, oT_psum[l])
                    if j == 6:
                        pe.wait_ge(oT_ready[l], n + 1)
                        wo = wo1 if l else wo0
                        for r in range(2):
                            for k in range(KD):
                                o = mm(bank[:, 7, r * D:(r + 1) * D], OT[:, k, r * P:(r + 1) * P], wo[:, k, :],
                                       start=(k == 0), stop=(k == KD - 1), skip_group_check=True)
                        o.then_inc(y_ready, 1)

                for u, b, j in slots():
                    if 0 <= u + 1 < UNITS:
                        score(u + 1)
                    if 0 <= u < UNITS:
                        turn(u)
                    if 0 <= u - 1 < UNITS:
                        values(u - 1)
                    if 0 <= b + 1 < NB:
                        front(b + 1, j)
                    if 0 <= b - 1 < NB:
                        back(b - 1, j)

            pe.wait_ge(s_w0, 2 * 16)
            attention(0)

            if STAGES > 1:
                pe.wait_ge(s_ctx, 7 * 16)
                with pe.Fori(0, NB) as b:
                    pe.wait_ge(ctb_ready, b + 1)
                    for r in range(2):
                        mm(bank[:, 1, r * DC:(r + 1) * DC], ctb[:, r * P:(r + 1) * P], wk[:], start=True, stop=True,
                           skip_group_check=True)
                    mm(bank[0:DC, 0, 0:SEQ], wk[:], ctb[:], start=True, stop=True).then_inc(kv_psum, 1)
                    turn_xn(b + NB)
                    pe.wait_ge(kvj_ready, b + 1)
                    for k in range(2):
                        o = mm(bank[0:DC, 2, 0:SEQ], kvj[:, k, :], xnT[:, k, :], start=(k == 0), stop=(k == 1))
                    o.then_inc(outT_psum, 1)
                    pe.wait_ge(outT_ready, b + 1)
                    pe.wait_ge(kvT_ready, b + 1)
                    for r in range(2):
                        o = mm(bank[:, 3, r * SEQ:(r + 1) * SEQ], outT[:, r * P:(r + 1) * P], kvT[:], start=True, stop=True,
                               skip_group_check=True)
                    o.then_inc(sim_ready, 1)

            if STAGES > 2:
                pe.wait_ge(setup, 4)
                pe.wait_ge(wabs_ready, 3)
                mm(bank[:, 6, 0:3], ones[:], wabs[:], start=True, stop=True).then_inc(wmean_psum, 1)
                pe.wait_ge(sign_ready, 4)
                with pe.Fori(0, NB) as b:
                    turn_xn(b + 2 * NB, xq_ready, b + 1)
                    def hidden(r):
                        for c in range(2):
                            if r == 1:
                                pe.wait_ge(hid_used, b * 4 + (c + 1))
                            for w, src in enumerate((s1, s2)):
                                for k in range(KD):
                                    o = mm(bank[:, 2 * c + w, :], xnT[:, k, r * P:(r + 1) * P], src[:, k, c * 512:(c + 1) * 512],
                                           start=(k == 0), stop=(k == KD - 1))
                            o.then_inc(hid_psum, 1)
                    hidden(0)
                    hidden(1)
                    for r in range(2):
                        pe.wait_ge(hq_ready, b * 2 + (r + 1))
                        if r:
                            pe.wait_ge(hT_ready, b * 2 + 1)
                        for m in range(FF // P):
                            o = tr(bank[:, 4 + m // 4, (m % 4) * P:(m % 4 + 1) * P], hid[:, r, m * P:(m + 1) * P], ident[:])
                        o.then_inc(hT_psum, 1)
                        pe.wait_ge(hT_ready, b * 2 + (r + 1))
                        for m in range(FF // P):
                            o = mm(bank[:, 6, r * D:(r + 1) * D], hidT[:, r, m, :], s3[:, m, :], start=(m == 0),
                                   stop=(m == FF // P - 1), skip_group_check=True)
                    o.then_inc(y_ready, 1)

            if STAGES > 3:
                pe.wait_ge(s_w1, 4 * 16)
                attention(1)

            if STAGES > 4:
                pe.wait_ge(s_wx, 10 * 16)
                for h in range(NH):
                    if h >= 2:
                        pe.wait_ge(fold_act, h - 1)
                    for k in range(KD):
                        o = mm(bank[:, h % 2, k * CQ:(k + 1) * CQ], wq_x[:, h, k * P:(k + 1) * P], wcq[:, h, :],
                               start=True, stop=True, skip_group_check=True)
                    o.then_inc(fold_psum, 1)
                for g in range(NH // 4):
                    pe.wait_ge(fold_act, NH + g - 1)
                    for m in range(8):
                        h, f = 4 * g + m // 2, m % 2
                        o = mm(bank[0:HC, g % 2, m * DC:(m + 1) * DC], wqr[:, h, f * HC:(f + 1) * HC], wkr[:, h, :],
                               start=True, stop=True, skip_group_check=True)
                    o.then_inc(fold_psum, 1)
                for g in range(PAIRS // 2):
                    pe.wait_ge(fold_act, NH + NH // 4 + g - 1)
                    for m in range(4):
                        h, j = 4 * g + m, m // 2
                        o = mm(bank[DC * (m % 2):DC * (m % 2 + 1), g % 2, j * D:(j + 1) * D], wckv[:, h, :], wo_x[:, h, :],
                               start=True, stop=True, skip_group_check=True)
                    o.then_inc(fold_psum, 1)
                pe.wait_ge(fold_act, NH + NH // 4 + PAIRS // 2)
                pe.wait_ge(kvr_ready, 2)
                for t in range(NT):
                    o = tr(bank[:, 5 + t // 4, (t % 4) * P:(t % 4 + 1) * P], kvr[:, t].rearrange("p e n -> p (e n)"), ident[:])
                o.then_inc(kvrT_psum, 1)
                turn_xn(4 * NB)
                for u, b, h in cross_slots():
                    v = u + 1
                    if v < CROSS:
                        bv, hv = v // NH, v % NH
                        if v >= 2:
                            pe.wait_ge(qx_cs, 2 * (v - 1))
                        if hv == 10 and bv < NB - 1:
                            pe.wait_ge(xnT_ready, 4 * NB + bv + 2)
                        for f in range(2):
                            for k in range(KD):
                                o = mm(bank[0:HC, v % 2, f * SEQ:(f + 1) * SEQ], Aq[:, hv, k, f * HC:(f + 1) * HC],
                                       xnTs[:, bv % 2, k, :], start=(k == 0), stop=(k == KD - 1), skip_group_check=True)
                        o.then_inc(qx_psum, 1)
                    if 0 <= u < CROSS:
                        pe.wait_ge(qx_ready, 2 * (u + 1))
                        if u >= 1:
                            pe.wait_ge(z_split, u)
                        if u >= 5:
                            pe.wait_ge(cT_ready, (u - 3) // 2)
                        for f in range(2):
                            o = mm(bank[:, 2, 0:SEQ], Gq[:, 2 * h + f].rearrange("p e n -> p (e n)"), qx_r[:, u % 2, f, :],
                                   start=(f == 0), stop=(f == 1), skip_group_check=True)
                        o.then_inc(z_psum, 1)
                    w = u - 1
                    if 0 <= w < CROSS:
                        pe.wait_ge(px_ready, 2 * (w + 1))
                        if w >= 1:
                            pe.wait_ge(pxT_ready, w)
                        if w == 0:
                            pe.wait_ge(kk_ready, 1)
                        for k in range(2):
                            for r in range(2):
                                o = tr(bank[:, 5, k * SEQ + r * P:k * SEQ + (r + 1) * P],
                                       px[:, w % 2, r, k * P:(k + 1) * P], ident[:])
                        o.then_inc(pxT_psum, 1)
                    w = u - 2
                    if 0 <= w < CROSS:
                        e = w % 2
                        pe.wait_ge(pxT_ready, w + 1)
                        if w >= 1:
                            pe.wait_ge(cn_ready, w)
                        for r in range(2):
                            for k in range(2):
                                o = mm(bank[:, 6, r * P + e * DC:r * P + (e + 1) * DC], pxT[:, w % 2, k, r * P:(r + 1) * P],
                                       kvr[:, 2 * (w // NH) + k, 0, :], start=(k == 0), stop=(k == 1), skip_group_check=True)
                        o.then_inc(cx_psum, 1)
                    w = u - 4
                    if w >= 0 and w % 2 == 1:
                        j = w // 2
                        pe.wait_ge(cT_ready, j + 1)
                        if j % PAIRS == 0 and j:
                            pe.wait_ge(x_done, 4 * NB + j // PAIRS)
                        for r in range(2):
                            o = mm(bank[:, 7, r * D:(r + 1) * D], cT[:, j % 2, r * P:(r + 1) * P], Cx[:, j % PAIRS, :],
                                   start=(j % PAIRS == 0 and r == 0), stop=(j % PAIRS == PAIRS - 1), skip_group_check=True)
                        if j % PAIRS == PAIRS - 1:
                            o.then_inc(y_ready, 1)
                    if 0 <= u < CROSS:
                        if u == 0:
                            pe.wait_ge(kk_ready, 1)
                        pe.wait_ge(z_split, u + 1)
                        if u >= 2:
                            pe.wait_ge(px_ready, 2 * (u - 1))
                        for r in range(2):
                            for part in range(2):
                                o = mm(bank[:, 3 + u % 2, r * SEQ:(r + 1) * SEQ], zz[:, u % 2, r * P:(r + 1) * P],
                                       kk[:, b, part, :], start=(part == 0), stop=(part == 1), skip_group_check=True)
                        o.then_inc(sx_ready, 1)
                    w = u - 3
                    if 0 <= w < CROSS and w % 2 == 1:
                        j = w // 2
                        pe.wait_ge(cn_ready, w + 1)
                        pe.wait_ge(z_split, min(u + 1, CROSS))
                        for r in range(2):
                            o = tr(bank[:, 2, 256 + r * P:256 + (r + 1) * P], cn[:, j % 2, r, :], ident[:])
                        o.then_inc(cT_psum, 1)
                    if h == 8 and 0 <= b < NB - 1:
                        pe.wait_ge(xn_ready, 2 * (4 * NB + b + 1) + 2)
                        pe.wait_ge(qx_cs, 2 * (u + 1))
                        for k in range(KD):
                            for r in range(2):
                                o = tr(bank[:, u % 2, k * SEQ + r * P:k * SEQ + (r + 1) * P],
                                       xns[:, (b + 1) % 2, r, k * P:(k + 1) * P], ident[:])
                        o.then_inc(xnTp_ready, 1)

            if STAGES > 5:
                pe.wait_ge(s_wm, 6 * 16)
                with pe.Fori(0, NB) as b:
                    turn_xn(b + 5 * NB)
                    for r in range(2):
                        for k in range(KD):
                            o = mm(bank[:, 0, r * NE:(r + 1) * NE], xnT[:, k, r * P:(r + 1) * P], gw[:, k, :],
                                   start=(k == 0), stop=(k == KD - 1), skip_group_check=True)
                    o.then_inc(lg_psum, 1)
                    for w, src in enumerate((sg, su)):
                        for f in range(2):
                            for k in range(KD):
                                o = mm(bank[:, 1 + w, f * SEQ:(f + 1) * SEQ], src[:, k, f * P:(f + 1) * P], xnT[:, k, :],
                                       start=(k == 0), stop=(k == KD - 1), skip_group_check=True)
                    o.then_inc(sh_psum, 1)
                    pe.wait_ge(shh_ready, b + 1)
                    for r in range(2):
                        for f in range(2):
                            o = mm(bank[:, 3, r * D:(r + 1) * D], sh_h[:, f, r * P:(r + 1) * P], sd[:, f, :],
                                   start=(f == 0), stop=(f == 1), skip_group_check=True)
                    o.then_inc(y_ready, 1)
                pe.wait_ge(mask_ready, 1)
                mm(bank[:, 4, 0:NT * NE], before, mask.rearrange("p t e -> p (t e)"), start=True, stop=False)
                mm(bank[:, 4, 0:NT * NE], ones[:], seen.rearrange("p t e -> p (t e)"), start=False,
                   stop=True).then_inc(pos_psum, 1)
                for c in range(NC):
                    i = c % 2
                    if c > 0:
                        pe.wait_ge(x_done, 6 * NB + 4 * c)
                    else:
                        pe.wait_ge(xn_kept, NB)
                    for t in range(NT):
                        pe.wait_ge(hot_ready, NT * c + t + 1)
                        for k in range(KD):
                            o = mm(bank[:, k, :], XN[:, t, k * P:(k + 1) * P], hot[:, t, :], start=(t == 0), stop=(t == NT - 1))
                    o.then_inc(gat_psum, 1)
                    for t in range(NT):
                        n = NT * c + t
                        pe.wait_ge(hotw_ready, n + 1)
                        if n >= 2:
                            pe.wait_ge(hotT_ready, n - 1)
                        for k in range(KS):
                            o = tr(bank[:, 2 + t % 2, k * P:(k + 1) * P], hotw[:, t, k * P:(k + 1) * P], ident[:])
                        o.then_inc(hotT_psum, 1)
                    pe.wait_ge(buf_ready, c + 1)
                    pe.wait_ge(experts_in[i], 16 * 3 * (c // 2 + 1))
                    for w in range(2):
                        for e in range(EC):
                            for k in range(KD):
                                o = mm(bank[:, 4 + w, e * CAP:(e + 1) * CAP],
                                       ew[:, i, w, (KD * e + k) * FE:(KD * e + k + 1) * FE], bufT[:, k, e * CAP:(e + 1) * CAP],
                                       start=(k == 0), stop=(k == KD - 1), skip_group_check=True)
                    o.then_inc(eh_psum, 1)
                    pe.wait_ge(eh_ready, c + 1)
                    for e in range(EC):
                        s, half = e // 2, CAP * (e % 2)
                        o = mm(bank[half:half + CAP, 6 + s // 2, (s % 2) * D:(s % 2 + 1) * D], h_T[:, e * CAP:(e + 1) * CAP],
                               ew[:, i, 2, e * D:(e + 1) * D], start=True, stop=True, skip_group_check=True)
                    o.then_inc(ob_psum, 1)
                    pe.wait_ge(ob_ready, c + 1)
                    pe.wait_ge(hotT_ready, NT * (c + 1))
                    for q in range(NT // 2):
                        n = c * (NT // 2) + q
                        if q >= 2:
                            pe.wait_ge(x_done, 6 * NB + n - 1)
                        for r in range(2):
                            for s in range(KS):
                                o = mm(bank[:, n % 2, r * D:(r + 1) * D], hotT[:, 2 * q + r, s, :], ob[:, s, :],
                                       start=(s == 0), stop=(s == KS - 1), skip_group_check=True)
                        o.then_inc(ey_psum, 1)


def kernel(x, ctx_512, L0_attn_w_project, L0_attn_w_out, L0_xattn_W_k, L0_xattn_b_k, L0_xattn_ln_gamma, L0_xattn_ln_beta,
           L0_ffn_w1, L0_ffn_w2, L0_ffn_w3, L1_attn_Wq, L1_attn_Wk, L1_attn_Wv, L1_attn_Wproj, L1_xattn_Wq,
           L1_xattn_w_kc_q, L1_xattn_w_kc_kv, L1_xattn_W_qr, L1_xattn_W_kr, L1_xattn_Wo, L1_ffn_gate_w,
           L1_ffn_gate_bias, L1_ffn_w1, L1_ffn_w2, L1_ffn_w3, L1_ffn_shared_gate, L1_ffn_shared_up, L1_ffn_shared_down):
    import numpy as np
    import concourse.bacc as bacc
    from concourse.bass_utils import run_bass_kernel_spmd as run

    f = np.float32
    C = np.ascontiguousarray

    def angles(dim, length):
        inv = (f(1.0) / np.power(f(10000.0), np.arange(0, dim, 2, dtype=f) / f(dim))).astype(f)
        return np.arange(length, dtype=f)[:, None] * inv[None, :]

    t1 = np.concatenate([angles(HD, SEQ)] * 2, axis=1)
    sign1 = np.where(np.arange(HD) < HD // 2, f(-1), f(1))
    tq = np.repeat(angles(CQ, SEQ), 2, axis=1)
    sq = np.sin(tq)
    sinq = np.concatenate([sq[:, HC:], -sq[:, :HC]], axis=1)
    tk = np.repeat(angles(DC, SEQ), 2, axis=1)
    signk = np.where(np.arange(DC) < DC // 2, f(-1), f(1))
    n = np.arange(P)
    later = np.concatenate([
        (n[:, None] < n[None, :]).astype(f),
        np.broadcast_to(np.arange(NE, dtype=f), (P, NE)),
        np.broadcast_to(np.arange(CAP, dtype=f), (P, CAP)),
        np.broadcast_to((np.arange(NG)[None, :] < np.arange(NG)[:, None]).astype(f).ravel(), (P, NG * NG))], axis=1)
    consts = {
        "ident": np.eye(P, dtype=f),
        "causal": np.where(n[None, :] > n[:, None], f(-1e9), f(0)),
        "head_rows": (n[:, None] // HD == np.arange(8)[None, :]).astype(f),
        "cos1": np.cos(t1), "sin1": np.sin(t1) * sign1,
        "cosq": np.cos(tq).T, "sinq": sinq.T,
        "cosk": np.cos(tk), "sink": np.sin(tk) * signk,
        "later": later,
    }
    A = np.asarray

    def rows(w, k):
        return w.reshape(NC, EC, k, P, w.shape[2]).transpose(0, 3, 1, 2, 4).reshape(NC * P, EC * k * w.shape[2])

    arrays = {
        "x": A(x).reshape(NB * SEQ, D),
        "ctx": A(ctx_512).reshape(NB * SEQ, DC),
        "ctxT": A(ctx_512).reshape(NB * SEQ, DC).T,
        "w_qkv0": A(L0_attn_w_project).T, "w_o0": A(L0_attn_w_out).T,
        "w_k": A(L0_xattn_W_k).T, "b_k": A(L0_xattn_b_k), "gamma": A(L0_xattn_ln_gamma), "beta": A(L0_xattn_ln_beta),
        "w_f1": A(L0_ffn_w1).T, "w_f2": A(L0_ffn_w2).T, "w_f3": A(L0_ffn_w3).T,
        "w_qkv1": np.concatenate([A(L1_attn_Wq), A(L1_attn_Wk), A(L1_attn_Wv)], axis=1), "w_o1": A(L1_attn_Wproj),
        "w_xq": A(L1_xattn_Wq), "w_cq": A(L1_xattn_w_kc_q).reshape(NH * P, CQ),
        "w_ckv": A(L1_xattn_w_kc_kv).reshape(NH * P, DC), "w_xo": A(L1_xattn_Wo).T,
        "w_qr": A(L1_xattn_W_qr).transpose(2, 0, 1).reshape(64, NH * CQ),
        "w_kr": A(L1_xattn_W_kr).transpose(2, 0, 1).reshape(64, NH * DC),
        "w_gate": A(L1_ffn_gate_w).T, "b_gate": A(L1_ffn_gate_bias),
        "w_e": np.concatenate([rows(A(L1_ffn_w1), KD), rows(A(L1_ffn_w3), KD), rows(A(L1_ffn_w2), 1)], axis=1),
        "w_sg": A(L1_ffn_shared_gate), "w_su": A(L1_ffn_shared_up), "w_sd": A(L1_ffn_shared_down),
    }
    arrays.update({k: v.astype(f) for k, v in consts.items()})
    arrays = {k: C(v) for k, v in arrays.items()}
    nc = bacc.Bacc("TRN2", target_bir_lowering=False, num_devices=1)
    aps = {k: nc.dram_tensor("in_" + k, v.shape, mybir.dt.from_np(v.dtype), kind="ExternalInput").ap() for k, v in arrays.items()}
    out = nc.dram_tensor("out_x", (NB * SEQ, D), F32, kind="ExternalOutput").ap()
    build(nc, aps, out)
    r = run(nc, [{"in_" + k: v for k, v in arrays.items()}], core_ids=[0])
    return r.results[0]["out_x"].reshape(NB, SEQ, D)
```

```python
from contextlib import ExitStack

import concourse.bass as bass
from concourse import mybir

F32 = mybir.dt.float32
BF16 = mybir.dt.bfloat16
F32R = mybir.dt.float32r
U32 = mybir.dt.uint32
ALU = mybir.AluOpType
ACT = mybir.ActivationFunctionType
AX = mybir.AxisListType

P = 128
D = 256
NB = 4
SEQ = 256
KD = D // P
NT = NB * SEQ // P
NH = 16
HD = D // NH
PAIRS = NH // 2
FF = 1024
GRP = 64
QB = 127.0
ROUND = 12582912.0
DC = 64
CQ = 192
HC = CQ // 2
NE = 32
TOPK = 4
NG = 4
EG = NE // NG
FE = 128
FS = 256
CAP = 2 * (2 * 128 * TOPK // NE)
EC = 8
NC = NE // EC
SLOTS = EC * CAP
KS = SLOTS // P
STAGES = 6


class Steps:

    def __init__(self, eng, sem):
        self.eng, self.sem, self.done, self.shift = eng, sem, 0, 0

    def mark(self, ins):
        ins.then_inc(self.sem, 1)
        self.done += 1

    def wait(self):
        self.eng.wait_ge(self.sem, self.shift + self.done)

    def wait_apart(self, scrap):
        self.wait()
        self.eng.memset(scrap, 0.0)

    def loop(self, i, first, per):
        self.shift, self.done, self.first, self.per = i * per + first, 0, first, per

    def end(self, count, name):
        assert self.done == self.per, (name, "increments in an iteration:", self.done)
        self.shift, self.done = 0, self.first + count * self.per


UNITS = NB * PAIRS
CROSS = NB * NH


def slots():
    for u in range(-2 * PAIRS, UNITS + PAIRS):
        yield u, u // PAIRS, u % PAIRS


def cross_slots():
    for u in range(-1, CROSS + 4):
        yield u, u // NH, u % NH


def build(nc, a, out):
    ctx = ExitStack()
    with ctx:
        def sb(name, shape, dt=F32):
            return ctx.enter_context(nc.sbuf_tensor(name, shape, dt))

        def sem(name):
            return ctx.enter_context(nc.semaphore(name))

        room = (nc.sbuf_base + 31) // 32 * 32
        sb("shared_room", [P, 4096 + 8])

        def at(name, shape, start, dt=F32):
            return nc.alloc_sbuf_tensor_at(name, shape, dt, offset=room + start)

        bank = ctx.enter_context(nc.psum_tensor("bank", [P, 8, 512], F32))
        X = sb("X", [P, NT, D])
        ident = sb("ident", [P, P])
        ident_h = sb("ident_h", [P, P], BF16)
        causal = sb("causal", [P, P])
        causal_h = sb("causal_h", [P, P], BF16)
        head_rows = sb("head_rows", [P, 8])
        ones = sb("ones", [P, P])
        halfneg = sb("halfneg", [P, 2])
        epsilons = sb("epsilons", [P, 4])
        many_halves = sb("many_halves", [P, 2, NT])
        scrap = sb("scrap", [P, 1])
        stat = sb("stat", [P, 2, 6])
        mv = sb("mv", [P, 2, 2])
        veps = sb("veps", [P, 2])
        rstd = sb("rstd", [P, 2])
        xns = sb("xns", [P, 2, 2, D])
        xn = xns[:, 0]
        xnTs_at = (nc.sbuf_base + 31) // 32 * 32 - room
        xnTs = at("xnTs", [P, 2, KD, SEQ], xnTs_at)
        sb("xnTs_room", [P, 2 * KD * SEQ + 8])
        xnT = xnTs[:, 0]
        wqkv1 = sb("wqkv1", [P, KD, 384])
        wo1 = sb("wo1", [P, KD, D])
        cos1 = sb("cos1", [P, 2, HD])
        sin1 = sb("sin1", [P, 2, HD])
        q_lead = at("q_lead", [P, 2, KD, SEQ], 0, F32R)
        kT = at("kT", [P, 2, KD, SEQ], 4096)
        V = at("V", [P, 2, 2, D], 8192)
        nmax = sb("nmax", [P, 2, 4])
        asums = sb("asums", [P, 2, 2, NH])
        sums = sb("sums", [P, 2, NH])
        rsum = sb("rsum", [P, 2, NH])
        work_at = (nc.sbuf_base + 31) // 32 * 32 - room
        work = at("work", [P, 14 * 512], work_at)
        sb("work_room", [P, 14 * 512 + 8])
        prob = work[:, 0:1536].rearrange("p (i e k n) -> p i e k n", i=2, e=2, k=3)
        probT = work[:, 1536:3072].rearrange("p (i m n) -> p i m n", i=2, m=6)
        On = at("On", [P, 2, D], 12288)
        OT = at("OT", [P, KD, SEQ], 14336)
        kM = at("kM", [P, 2, 2, 2, SEQ], work_at + 4096 * 4, F32R)
        q_trail = at("q_trail", [P, 2, KD, SEQ], work_at + 6144 * 4, F32R)
        ctxT = sb("ctxT", [DC, NB, SEQ])
        ctxk = sb("ctxk", [P, NT, DC])
        wk = sb("wk", [DC, DC])
        bk_col = sb("bk_col", [DC, 1])
        bk_row = sb("bk_row", [P, DC])
        gamma = sb("gamma", [P, D])
        beta = sb("beta", [P, D])
        simn = work[:, 0:1024].rearrange("p (i r n) -> p i r n", i=2, r=2)
        simg = work[:, 1024:2048].rearrange("p (i r n) -> p i r n", i=2, r=2)
        prob_x = work[:, 2048:3072].rearrange("p (i r n) -> p i r n", i=2, r=2)
        kvT = work[0:DC, 3072:4096].rearrange("p (b n) -> p b n", b=NB)
        outT = work[0:DC, 4096:4608].rearrange("p (i n) -> p i n", i=2)
        kvj = work[:, 4608:5120].rearrange("p (t n) -> p t n", t=NT)
        sstat = sb("sstat", [P, 2, 6])
        smv = sb("smv", [P, 2, 2, 2])
        sveps = sb("sveps", [P, 2, 2])
        srstd = sb("srstd", [P, 2, 2])
        early_at = (nc.sbuf_base + 31) // 32 * 32 - room
        early = at("early", [P, 2 * EC * 768], early_at)
        sb("early_room", [P, 2 * EC * 768 + 8])
        qk_c = early[:, 0:640].rearrange("p (r n) -> p r n", r=2)
        qk_s = early[:, 640:1280].rearrange("p (r n) -> p r n", r=2)
        q_r = early[:, 10240:10752].rearrange("p (r n) -> p r n", r=2)
        k_r = early[:, 10752:11264].rearrange("p (r n) -> p r n", r=2)
        wqkv0 = early[:, 0:1536].rearrange("p (k n) -> p k n", k=KD)
        wo0 = early[:, 1536:2048].rearrange("p (k n) -> p k n", k=KD)
        w_ff = early[:, 2048:2048 + 6144]
        w_in = [w_ff[:, 2048 * i:2048 * (i + 1)].rearrange("p (k n) -> p k n", k=KD) for i in range(2)]
        s_in = [at(f"s_in{i}", [P, KD, FF], early_at + (2048 + 2048 * i) * 4, F32R) for i in range(2)]
        s3 = w_ff[:, 4096:6144].rearrange("p (k n) -> p k n", k=FF // P)
        xqT = at("xqT", [P, 2, 2, KD, SEQ], early_at + 8192 * 4, F32R)
        Gq = early[0:HC, 6144:10240].rearrange("p (m e n) -> p m e n", m=2 * NH, e=2)
        Cx = early[:, 10240:12288].rearrange("p (j n) -> p j n", j=PAIRS)
        hot = [at(f"hot{i}", [P, NT, SLOTS], early_at + i * NT * SLOTS * 4, F32R) for i in range(2)]
        hotT = at("hotT", [P, NT, KS, P], early_at + 2 * NT * SLOTS * 4, F32R)
        xm = early[:, 8192:8192 + NT * D].rearrange("p (t n) -> p t n", t=NT)
        wabs = sb("wabs", [P, 3])
        wmean = sb("wmean", [P, 3])
        gmax = sb("gmax", [P, 2, 16])
        grcp = sb("grcp", [P, 2, 16])
        gscl = sb("gscl", [P, 2, 16])
        gscl_h = sb("gscl_h", [P, 2, 16])
        gate_f = work[:, 0:2048].rearrange("p (r n) -> p r n", r=2)
        hid = work[:, 2048:4096].rearrange("p (r n) -> p r n", r=2)
        hidT = work[:, 4096:6144].rearrange("p (r m n) -> p r m n", r=2, m=8)
        raw_at = (nc.sbuf_base + 31) // 32 * 32 - room
        raw = at("raw", [P, 16384], raw_at)
        sb("raw_room", [P, 16384 + 8])
        wq_x = raw[:, 0:4096].rearrange("p (h n) -> p h n", h=NH)
        wcq = raw[:, 4096:7168].rearrange("p (h n) -> p h n", h=NH)
        wckv = raw[:, 7168:8192].rearrange("p (h n) -> p h n", h=NH)
        wo_x = raw[:, 8192:12288].rearrange("p (h n) -> p h n", h=NH)
        wqr = raw[0:64, 12288:15360].rearrange("p (h n) -> p h n", h=NH)
        wkr = raw[0:64, 15360:16384].rearrange("p (h n) -> p h n", h=NH)
        Aq = [at("A_lead", [P, NH, KD, CQ], early_at, F32R),
              at("A_trail", [P, NH, KD, CQ], raw_at + 7168 * 4, F32R)]
        xT_lead = at("xT_lead", [P, 2, KD, SEQ], xnTs_at, F32R)
        xT_trail = [at("xT_trail0", [P, KD, SEQ], 14336, F32R), at("xT_trail1", [P, KD, SEQ], work_at + 3328 * 4, F32R)]
        cosq = sb("cosq", [HC, 2, SEQ])
        sinq = sb("sinq", [HC, 2, SEQ])
        cosk = sb("cosk", [P, 2, DC])
        sink = sb("sink", [P, 2, DC])
        kvr = at("kvr", [P, NT, 2, DC], 10240)
        kk = at("kk", [P, NB, 2, SEQ], 0, F32R)
        zz = at("zz", [P, 2, SEQ], 8192, F32R)
        kv_c = work[:, 0:512].rearrange("p (b r n) -> p b r n", b=NB, r=2)
        kv_s = work[:, 512:1024].rearrange("p (b r n) -> p b r n", b=NB, r=2)
        qx_c = work[0:HC, 256:1280].rearrange("p (i f n) -> p i f n", i=2, f=2)
        qx_s = work[0:HC, 1280:2304].rearrange("p (i f n) -> p i f n", i=2, f=2)
        qx_r = work[0:HC, 2304:3328].rearrange("p (i f n) -> p i f n", i=2, f=2)
        px = work[:, 3840:4864].rearrange("p (i r n) -> p i r n", i=2, r=2)
        pxT = work[:, 4864:5888].rearrange("p (i k n) -> p i k n", i=2, k=2)
        cn = work[:, 5888:6400].rearrange("p (i r n) -> p i r n", i=2, r=2)
        cT = work[:, 6400:6912].rearrange("p (i n) -> p i n", i=2)
        ew = raw[:, 0:12288].rearrange("p (i w n) -> p i w n", i=2, w=3)
        XN = [at(f"XN{i}", [P, NT, D], raw_at + (12288 + i * NT * D) * 4, F32R) for i in range(2)]
        ob = [at(f"ob{i}", [P, KS, D], i * KS * D * 4, F32R) for i in range(2)]
        xmT = at("xmT", [P, NB, KD, SEQ], 2 * KS * D * 4)
        wgts = [sb(f"wgts{i}", [P, NT, NE], F32R) for i in range(2)]
        ws_row = work[0:NE, 5840:5840 + SLOTS]
        wslot = sb("wslot", [P, KS])
        mstat = sb("mstat", [P, NT, 6])
        mmv = sb("mmv", [P, NT, 2])
        mveps = sb("mveps", [P, NT])
        mrstd = sb("mrstd", [P, NT])
        gw = sb("gw", [P, KD, NE])
        gbias = sb("gbias", [P, NE])
        sg = sb("sg", [P, KD, FS])
        su = sb("su", [P, KD, FS])
        sd = sb("sd", [P, KD, D])
        later = sb("later", [P, 128 + 32 + 64 + 16])
        before = later[:, 0:128]
        iota_e = later[:, 128:160]
        iota_s = later[:, 160:224]
        earlier = later[:, 224:240]
        sh_g = work[:, 4816:5840].rearrange("p (i f n) -> p i f n", i=2, f=2)
        sh_h = work[:, 5840:6864].rearrange("p (i f n) -> p i f n", i=2, f=2)
        bufT = work[:, 4816:5840].rearrange("p (k n) -> p k n", k=KD)
        h_g = work[:, 0:512]
        h_T = work[:, 512:1024]
        sc = work[:, 1024:1280].rearrange("p (t e) -> p t e", t=NT)
        scb = work[:, 1280:1536].rearrange("p (t e) -> p t e", t=NT)
        top_g = work[:, 1536:1792].rearrange("p (g n) -> p g n", g=NT * NG)
        gs = work[:, 1792:1824].rearrange("p (t g) -> p t g", t=NT)
        cmp_a = work[:, 1824:1952].rearrange("p (t g k) -> p t g k", t=NT, g=NG)
        cmp_b = work[:, 1952:2080].rearrange("p (t g k) -> p t g k", t=NT, g=NG)
        rank = work[:, 2080:2112]
        tmp_e = work[:, 2112:2368].rearrange("p (t e) -> p t e", t=NT)
        top_e = work[:, 2368:2432].rearrange("p (t k) -> p t k", t=NT)
        idx_f = work[:, 2432:2496].rearrange("p (t k) -> p t k", t=NT)
        pick = work[:, 2496:3520].rearrange("p (t e k) -> p t e k", t=NT, e=NE)
        mask = work[:, 3520:3776].rearrange("p (t e) -> p t e", t=NT)
        seen = work[:, 3776:4032].rearrange("p (t e) -> p t e", t=NT)
        wsum = work[:, 4032:4040]
        wrcp = work[:, 4040:4048]
        wgt = work[:, 4048:4304].rearrange("p (t e) -> p t e", t=NT)
        keep = work[:, 4304:4560].rearrange("p (t e) -> p t e", t=NT)
        posm = work[:, 4560:4816].rearrange("p (t e) -> p t e", t=NT)
        idx_u = sb("idx_u", [P, NT, 8], U32)

        s_x0 = sem("s_x0")
        s_x = sem("s_x")
        s_const = sem("s_const")
        s_w0 = sem("s_w0")
        s_ctx = sem("s_ctx")
        s_wff = sem("s_wff")
        s_w1 = sem("s_w1")
        s_wx = sem("s_wx")
        s_wm = sem("s_wm")
        experts_in = [sem(f"experts_in{i}") for i in range(2)]
        s_out = sem("s_out")
        setup = sem("setup")
        casts = sem("casts")
        mv_ready = sem("mv_ready")
        veps_ready = sem("veps_ready")
        rstd_ready = sem("rstd_ready")
        xn_ready = sem("xn_ready")
        xnTp_ready = sem("xnTp_ready")
        xnT_ready = sem("xnT_ready")
        x_done = sem("x_done")
        dve_steps = [sem(f"dve_steps{p}") for p in range(6)]
        proj = [sem(f"proj{l}") for l in range(2)]
        rope_parts = sem("rope_parts")
        rope_left = sem("rope_left")
        roped = sem("roped")
        q_ready = [sem(f"q_ready{l}") for l in range(2)]
        q_split = [sem(f"q_split{l}") for l in range(2)]
        kM_split = [sem(f"kM_split{l}") for l in range(2)]
        k_ready = [sem(f"k_ready{l}") for l in range(2)]
        v_ready = [sem(f"v_ready{l}") for l in range(2)]
        kM_ready = [sem(f"kM_ready{l}") for l in range(2)]
        s_ready = [sem(f"s_ready{l}") for l in range(2)]
        max_ready = [sem(f"max_ready{l}") for l in range(2)]
        p_ready = [sem(f"p_ready{l}") for l in range(2)]
        pT_psum = [sem(f"pT_psum{l}") for l in range(2)]
        pT4_ready = [sem(f"pT4_ready{l}") for l in range(2)]
        pT5_ready = [sem(f"pT5_ready{l}") for l in range(2)]
        av_done = [sem(f"av_done{l}") for l in range(2)]
        on_ready = [sem(f"on_ready{l}") for l in range(2)]
        oT_psum = [sem(f"oT_psum{l}") for l in range(2)]
        oT_ready = [sem(f"oT_ready{l}") for l in range(2)]
        y_ready = sem("y_ready")
        kv_psum = sem("kv_psum")
        kvT_ready = sem("kvT_ready")
        kvj_ready = sem("kvj_ready")
        outT_psum = sem("outT_psum")
        outT_ready = sem("outT_ready")
        sim_ready = sem("sim_ready")
        smv_ready = sem("smv_ready")
        sveps_ready = sem("sveps_ready")
        srstd_ready = sem("srstd_ready")
        simn_ready = sem("simn_ready")
        simg_ready = sem("simg_ready")
        simb_ready = sem("simb_ready")
        smax_ready = sem("smax_ready")
        srcp_ready = sem("srcp_ready")
        x_half = sem("x_half")
        sexp_ready = sem("sexp_ready")
        wabs_ready = sem("wabs_ready")
        wmean_psum = sem("wmean_psum")
        sign_ready = sem("sign_ready")
        xq_ready = sem("xq_ready")
        xqT_psum = sem("xqT_psum")
        xqT_lead = sem("xqT_lead")
        xqT_ready = sem("xqT_ready")
        hq_rounded = sem("hq_rounded")
        hid_psum = sem("hid_psum")
        gate_ready = sem("gate_ready")
        hid_used = sem("hid_used")
        hq_ready = sem("hq_ready")
        hT_psum = sem("hT_psum")
        hT_ready = sem("hT_ready")
        fold_psum = sem("fold_psum")
        fold_act = sem("fold_act")
        fold_dve = sem("fold_dve")
        xT_split = sem("xT_split")
        ctk_ready = sem("ctk_ready")
        kvr_ready = sem("kvr_ready")
        kvrT_psum = sem("kvrT_psum")
        kk_lead = sem("kk_lead")
        kk_ready = sem("kk_ready")
        qx_psum = sem("qx_psum")
        qx_cs = sem("qx_cs")
        qx_ready = sem("qx_ready")
        z_psum = sem("z_psum")
        z_ready = sem("z_ready")
        z_split = sem("z_split")
        kv_parts = sem("kv_parts")
        sx_ready = sem("sx_ready")
        mx_ready = sem("mx_ready")
        px_ready = sem("px_ready")
        pxT_psum = sem("pxT_psum")
        pxT_ready = sem("pxT_ready")
        cx_psum = sem("cx_psum")
        cn_ready = sem("cn_ready")
        cT_psum = sem("cT_psum")
        cT_ready = sem("cT_ready")
        mmv_ready = sem("mmv_ready")
        mveps_ready = sem("mveps_ready")
        mrstd_ready = sem("mrstd_ready")
        xm_ready = sem("xm_ready")
        xmT_psum = sem("xmT_psum")
        xmT_ready = sem("xmT_ready")
        XN_lead = sem("XN_lead")
        XN_trail = sem("XN_trail")
        lg_psum = sem("lg_psum")
        sh_psum = sem("sh_psum")
        shy_psum = sem("shy_psum")
        weights_ready = sem("weights_ready")
        ws_psum = sem("ws_psum")
        ws_copied = sem("ws_copied")
        ws_turned = sem("ws_turned")
        ws_ready = sem("ws_ready")
        ob_lead = sem("ob_lead")
        hotT_even = sem("hotT_even")
        hotT_odd = sem("hotT_odd")
        shg_ready = sem("shg_ready")
        shh_ready = sem("shh_ready")
        esig_ready = sem("esig_ready")
        mask_ready = sem("mask_ready")
        pos_psum = sem("pos_psum")
        hot_ready = sem("hot_ready")
        gat_psum = sem("gat_psum")
        buf_ready = sem("buf_ready")
        hotT_psum = sem("hotT_psum")
        eh_psum = sem("eh_psum")
        eg_ready = sem("eg_ready")
        eh_ready = sem("eh_ready")
        ob_psum = sem("ob_psum")
        ob_ready = sem("ob_ready")
        ey_psum = sem("ey_psum")
        ey_used = sem("ey_used")

        block = ctx.enter_context(nc.Block())

        @block.sync
        def _(sp):
            def load(dst, src, s):
                sp.dma_start(dst, src).then_inc(s, 16)

            xd = a["x"].rearrange("(t p) d -> p t d", p=P)
            load(X[:, 0:2, :], xd[:, 0:2, :], s_x0)
            load(ident[:], a["ident"], s_const)
            load(wqkv0, a["w_qkv0"].rearrange("(k p) n -> p k n", p=P), s_w0)
            load(X[:, 2:NT, :], xd[:, 2:NT, :], s_x)
            load(causal[:], a["causal"], s_const)
            load(head_rows[:], a["head_rows"], s_const)
            load(wo0, a["w_o0"].rearrange("(k p) n -> p k n", p=P), s_w0)
            load(ctxT[:], a["ctxT"].rearrange("d (b s) -> d b s", b=NB), s_ctx)
            load(ctxk[:], a["ctx"].rearrange("(t p) d -> p t d", p=P), s_ctx)
            load(wk[:], a["w_k"], s_ctx)
            load(bk_col[:], a["b_k"].rearrange("(d o) -> d o", o=1), s_ctx)
            load(bk_row[:], a["b_k"].rearrange("(o d) -> o d", o=1).to_broadcast([P, DC]), s_ctx)
            load(gamma[:], a["gamma"].rearrange("(o d) -> o d", o=1).to_broadcast([P, D]), s_ctx)
            load(beta[:], a["beta"].rearrange("(o d) -> o d", o=1).to_broadcast([P, D]), s_ctx)
            load(w_in[0], a["w_f1"].rearrange("(k p) n -> p k n", p=P), s_wff)
            load(w_in[1], a["w_f2"].rearrange("(k p) n -> p k n", p=P), s_wff)
            load(s3, a["w_f3"].rearrange("(k p) n -> p k n", p=P), s_wff)
            load(wqkv1[:], a["w_qkv1"].rearrange("(k p) n -> p k n", p=P), s_w1)
            load(wo1[:], a["w_o1"].rearrange("(k p) n -> p k n", p=P), s_w1)
            load(cos1[:], a["cos1"].rearrange("(r p) n -> p r n", p=P), s_w1)
            load(sin1[:], a["sin1"].rearrange("(r p) n -> p r n", p=P), s_w1)
            load(wq_x, a["w_xq"].rearrange("(h p) n -> p h n", p=P), s_wx)
            load(wcq, a["w_cq"].rearrange("(h p) n -> p h n", p=P), s_wx)
            load(wckv, a["w_ckv"].rearrange("(h p) n -> p h n", p=P), s_wx)
            load(wo_x, a["w_xo"].rearrange("(h p) n -> p h n", p=P), s_wx)
            load(wqr, a["w_qr"].rearrange("r (h n) -> r h n", h=NH), s_wx)
            load(wkr, a["w_kr"].rearrange("r (h n) -> r h n", h=NH), s_wx)
            load(cosq[:], a["cosq"].rearrange("(f j) s -> j f s", j=HC), s_wx)
            load(sinq[:], a["sinq"].rearrange("(f j) s -> j f s", j=HC), s_wx)
            load(cosk[:], a["cosk"].rearrange("(r p) n -> p r n", p=P), s_wx)
            load(sink[:], a["sink"].rearrange("(r p) n -> p r n", p=P), s_wx)
            load(gw[:], a["w_gate"].rearrange("(k p) n -> p k n", p=P), s_wm)
            load(gbias[:], a["b_gate"].rearrange("(o d) -> o d", o=1).to_broadcast([P, NE]), s_wm)
            load(sg[:], a["w_sg"].rearrange("(k p) n -> p k n", p=P), s_wm)
            load(su[:], a["w_su"].rearrange("(k p) n -> p k n", p=P), s_wm)
            load(sd[:], a["w_sd"].rearrange("(k p) n -> p k n", p=P), s_wm)
            load(later[:], a["later"], s_wm)

            if STAGES > 5:
                sp.wait_ge(fold_act, NH + NH // 4 + PAIRS // 2)
                def load_chunk(i, c):
                    for w in range(3):
                        sp.dma_start(ew[:, i, w, :], a["w_e"][c * P:(c + 1) * P, w * 2048:(w + 1) * 2048]
                                     ).then_inc(experts_in[i], 16)
                load_chunk(0, 0)
                sp.wait_ge(qx_psum, CROSS)
                load_chunk(1, 1)
                for c in range(2, NC):
                    sp.wait_ge(ob_psum, c - 1)
                    load_chunk(c % 2, c)
            od = out.rearrange("(t p) d -> p t d", p=P)
            for b in range(NB):
                sp.wait_ge(x_done, NB * (STAGES + NC - 1) + b + 1 if STAGES > 5 else NB * STAGES)
                sp.dma_start(od[:, 2 * b:2 * b + 2, :], X[:, 2 * b:2 * b + 2, :]).then_inc(s_out, 16)
            sp.wait_ge(s_out, NB * 16)

        @block.gpsimd
        def _(pool):
            pool.memset(ones[:], 1.0).then_inc(setup, 1)
            pool.memset(halfneg[:], -0.5).then_inc(setup, 1)
            pool.memset(epsilons[:, 0:2], 1e-5).then_inc(setup, 1)
            pool.memset(epsilons[:, 2:4], 1e-6).then_inc(setup, 1)
            pool.memset(many_halves[:, 0], -0.5).then_inc(setup, 1)
            pool.memset(many_halves[:, 1], 1e-5).then_inc(setup, 1)
            pool.wait_ge(setup, 6)

            def rstd_of(n, eps, mv_s, veps_s, rstd_s):
                pool.wait_ge(mv_s, 2 * (n + 1))
                pool.tensor_tensor(veps[:], mv[:, :, 1], epsilons[:, 0:2] if eps == 1e-5 else epsilons[:, 2:4],
                                   ALU.add).then_inc(veps_s, 1)
                pool.wait_ge(veps_s, n + 1)
                pool.tensor_tensor(rstd[:], veps[:], halfneg[:], ALU.pow).then_inc(rstd_s, 1)

            def norm(n):
                rstd_of(n, 1e-5, mv_ready, veps_ready, rstd_ready)

            def attention(l):
                for u, b, j in slots():
                    v = u + 2
                    if 0 <= v < UNITS:
                        if v % PAIRS == 0:
                            pool.wait_ge(k_ready[l], v // PAIRS + 1)
                        if v >= 2:
                            pool.wait_ge(s_ready[l], 2 * (v - 1))
                        g, pj = (v % PAIRS) // 4, v % 4
                        for e in range(2):
                            pool.tensor_tensor(kM[:, v % 2, 0, e, :], kT[:, (v // PAIRS) % 2, g, :],
                                               head_rows[:, 2 * pj + e:2 * pj + e + 1].to_broadcast([P, SEQ]),
                                               ALU.mult).then_inc(kM_ready[l], 1)
                    if j == 5 and 2 * l <= b + 2 < NB:
                        norm(b + 2 + 3 * NB * l)
                    if STAGES > 1 and l == 0 and b == NB and j == 1:
                        context_rstd(0, NB - 1)

            def context_rstd(b0, b1):
                t0, t1 = 2 * b0, 2 * b1
                pool.wait_ge(mv_ready, 2 * (NB + b1))
                pool.tensor_tensor(mveps[:, t0:t1], mmv[:, t0:t1, 1], many_halves[:, 1, t0:t1], ALU.add).then_inc(veps_ready, b1 - b0)
                pool.wait_ge(veps_ready, NB + b1)
                pool.tensor_tensor(mrstd[:, t0:t1], mveps[:, t0:t1], many_halves[:, 0, t0:t1], ALU.pow).then_inc(rstd_ready, b1 - b0)

            def expert_rstd(t0, t1):
                pool.wait_ge(mmv_ready, t1)
                pool.tensor_tensor(mveps[:, t0:t1], mmv[:, t0:t1, 1], many_halves[:, 1, t0:t1], ALU.add).then_inc(mveps_ready, t1 - t0)
                pool.wait_ge(mveps_ready, t1)
                pool.tensor_tensor(mrstd[:, t0:t1], mveps[:, t0:t1], many_halves[:, 0, t0:t1], ALU.pow).then_inc(mrstd_ready, t1 - t0)

            pool.wait_ge(s_const, 3 * 16)
            attention(0)
            if STAGES > 1:
                pool.wait_ge(s_ctx, 7 * 16)
                for b in range(NB):
                    i = b % 2
                    pool.wait_ge(smv_ready, 2 * (b + 1))
                    pool.tensor_tensor(sveps[:, i], smv[:, i, :, 1], epsilons[:, 2:4], ALU.add).then_inc(sveps_ready, 1)
                    pool.wait_ge(sveps_ready, b + 1)
                    pool.tensor_tensor(srstd[:, i], sveps[:, i], halfneg[:], ALU.pow).then_inc(srstd_ready, 1)
                    pool.wait_ge(simn_ready, 2 * (b + 1))
                    if b >= 2:
                        pool.wait_ge(sexp_ready, 2 * (b - 1))
                    pool.tensor_tensor(simg[:, i], simn[:, i], gamma[:].unsqueeze(1).to_broadcast([P, 2, D]),
                                       ALU.mult).then_inc(simg_ready, 1)
                    if b == 0:
                        context_rstd(NB - 1, NB)
                    if STAGES > 2 and b == 2:
                        norm(2 * NB)

            if STAGES > 2:
                for t in range(-1, NT):
                    if t % 2 == 1 and (t + 1) // 2 + 1 < NB:
                        norm(2 * NB + (t + 1) // 2 + 1)
                    if STAGES > 3 and t in (5, 6):
                        norm(3 * NB + t - 5)
                    if t >= 0:
                        pool.wait_ge(hq_rounded, t + 1)
                        hg = hid[:, t % 2, :].rearrange("p (g n) -> p g n", n=GRP)
                        pool.tensor_tensor(hg, hg, gscl_h[:, t % 2, :].unsqueeze(2).to_broadcast([P, 16, GRP]),
                                           ALU.mult).then_inc(hq_ready, 1)
            if STAGES > 3:
                attention(1)
            if STAGES > 4:
                norm(4 * NB)
                for u, b, h in cross_slots():
                    v = u + 1
                    if 0 <= v < CROSS:
                        pool.wait_ge(qx_cs, 2 * (v + 1))
                        if v >= 2:
                            pool.wait_ge(z_psum, v - 1)
                        for f in range(2):
                            pool.tensor_tensor(qx_r[:, v % 2, f], qx_c[:, v % 2, f], qx_s[:, v % 2, 1 - f],
                                               ALU.add).then_inc(qx_ready, 1)
                    if h == 4 and 0 <= b < NB - 1:
                        norm(4 * NB + b + 1)
                    if STAGES > 5 and u == CROSS:
                        expert_rstd(0, NT - 2)
            if STAGES > 5:
                expert_rstd(NT - 2, NT)
                for b in range(NB):
                    pool.wait_ge(xm_ready, 2 * b + 2)
                    pool.wait_ge(XN_lead, b + 1)
                    ts = slice(2 * b, 2 * b + 2)
                    pool.tensor_tensor(XN[1][:, ts, :], xm[:, ts, :], XN[0][:, ts, :].bitcast(F32),
                                       ALU.subtract).then_inc(XN_trail, 1)

        @block.scalar
        def _(act):
            act.preload_act_table(ACT.Exp)

            def copy_xnT(n):
                act.wait_ge(xnTp_ready, n + 1)
                act.activation(xnT[:], bank[:, 7, :].rearrange("p (k n) -> p k n", k=KD), ACT.Copy).then_inc(xnT_ready, 1)

            shared = bank[:, 7, :].rearrange("p (k n) -> p k n", k=KD)

            def front(l, n, j):
                i = n % 2
                if j == 0:
                    copy_xnT(n + 2 * NB * l)
                if j == (3 if l else 1):
                    act.wait_ge(proj[l], (4 * n + 3) if l else (3 * n + 1))
                    act.activation(q_lead[:, i], shared, ACT.Copy, scale=float(HD) ** -0.5).then_inc(q_ready[l], 1)
                if j == (4 if l else 2):
                    act.wait_ge(proj[l], (4 * n + 4) if l else (3 * n + 2))
                    act.activation(kT[:, i], shared, ACT.Copy).then_inc(k_ready[l], 1)
                if l == 0 and j == 3:
                    act.wait_ge(proj[l], 3 * n + 3)
                    act.activation(V[:, i], shared, ACT.Copy).then_inc(v_ready[l], 1)

            def attention(l):
                def exps(u):
                    i, b, j = u % 2, u // PAIRS, u % PAIRS
                    for r in range(2):
                        act.wait_ge(max_ready[l], 2 * u + r + 1)
                        if r == 0 and u >= 2:
                            act.wait_ge(pT_psum[l], u - 1)
                        if r == 0 and j == 0 and b >= 2:
                            act.wait_ge(on_ready[l], b - 1)
                        for e in range(2):
                            n = SEQ if r else P
                            dst = prob[:, i, e, 1:3, :].rearrange("p k n -> p (k n)") if r else prob[:, i, e, 0, :]
                            act.activation(dst, bank[:, 2 * i + r, e * n:(e + 1) * n], ACT.Exp,
                                           bias=nmax[:, i, 2 * r + e:2 * r + e + 1],
                                           accum_out=asums[:, b % 2, r, 2 * j + e:2 * j + e + 1]).then_inc(p_ready[l], 1)

                for u, b, j in slots():
                    if 0 <= u + 1 < UNITS:
                        exps(u + 1)
                    if 0 <= u < UNITS:
                        act.wait_ge(pT_psum[l], u + 1)
                        if u >= 2:
                            act.wait_ge(av_done[l], u - 1)
                        act.activation(probT[:, u % 2, 4:6, :], bank[:, 5, 0:256].rearrange("p (m n) -> p m n", m=2),
                                       ACT.Copy).then_inc(pT5_ready[l], 1)
                    if l <= b + 1 < NB:
                        front(l, b + 1, j)
                    if l == 0 and b == NB - 1 and 1 <= j <= 3:
                        act.wait_ge(wabs_ready, j)
                        act.activation(s_in[j - 1][:] if j < 3 else s3, w_in[j - 1] if j < 3 else s3,
                                       ACT.Sign).then_inc(sign_ready, 1)
                    if STAGES > 1 and l == 0 and b == NB:
                        if j == 1:
                            context_weights()
                        if j in (2, 4, 5):
                            context_copy((2, 4, 5).index(j))
                    if 0 <= b - 1 < NB and j == (1 if STAGES > 1 and l == 0 and b == NB else 5):
                        act.wait_ge(oT_psum[l], b)
                        act.activation(OT[:], shared, ACT.Copy).then_inc(oT_ready[l], 1)

            def copy_xm(b):
                ts = slice(2 * b, 2 * b + 2)
                act.wait_ge(xmT_psum, b + 1)
                act.activation(xmT[:, b], bank[:, 3 + b % 2, :].rearrange("p (k n) -> p k n", k=KD), ACT.Copy).then_inc(xmT_ready, 1)
                act.activation(XN[0][:, ts, :], xm[:, ts, :], ACT.Copy).then_inc(XN_lead, 1)

            def context_weights():
                act.wait_ge(kv_psum, 2)
                for g in range(2):
                    act.activation(kvT[:, 2 * g:2 * g + 2, :], bank[0:DC, g, :].rearrange("p (b n) -> p b n", b=2),
                                   ACT.Identity, bias=bk_col[:, 0:1]).then_inc(kvT_ready, 1)
                act.wait_ge(wmean_psum, 1)
                act.activation(wmean[:], bank[:, 3, 0:3], ACT.Copy, scale=1.0 / (D * FF)).then_inc(sign_ready, 1)

            def context_copy(b):
                act.wait_ge(xnTp_ready, NB + b + 1)
                act.activation(xnTs[:, b % 2], bank[:, 4 + b % 2, :].rearrange("p (k n) -> p k n", k=KD),
                               ACT.Copy).then_inc(xnT_ready, 1)
                act.wait_ge(outT_psum, b + 1)
                if b >= 2:
                    act.wait_ge(sim_ready, b - 1)
                act.activation(outT[:, b % 2], bank[0:DC, 6, 0:SEQ], ACT.Copy,
                               scale=float(D) ** -0.5).then_inc(outT_ready, 1)

            attention(0)

            if STAGES > 1:
                context_copy(NB - 1)

                def lead_xqT(b):
                    act.wait_ge(xqT_psum, b + 1)
                    if b >= 2:
                        act.wait_ge(hid_psum, 2 * (2 * b - 2))
                    act.activation(xqT[:, b % 2, 0], bank[:, 7, :].rearrange("p (k n) -> p k n", k=KD), ACT.Copy).then_inc(xqT_lead, 1)

                for b in range(NB):
                    act.wait_ge(smax_ready, b + 1)
                    if b >= 2:
                        act.wait_ge(x_done, NB + b - 1)
                    for r in range(2):
                        act.activation(prob_x[:, b % 2, r, :], simg[:, b % 2, r, :], ACT.Exp, bias=nmax[:, b % 2, r:r + 1],
                                       accum_out=sums[:, r, b:b + 1]).then_inc(sexp_ready, 1)
                    if STAGES > 2 and b == 2:
                        lead_xqT(0)

            if STAGES > 2:
                act.preload_act_table(ACT.Silu)
                act.wait_ge(sign_ready, 4)
                for t in range(-1, NT):
                    if t + 1 < NT:
                        for c in range(2):
                            act.wait_ge(hid_psum, 2 * (t + 1) + c + 1)
                            if t >= 1:
                                act.wait_ge(hid_used, 2 * (t - 1) + c + 1)
                            act.activation(gate_f[:, (t + 1) % 2, c * 512:(c + 1) * 512], bank[:, 2 * c, :], ACT.Silu,
                                           scale=wmean[:, 0:1]).then_inc(gate_ready, 1)
                    if t >= 0:
                        act.wait_ge(hT_psum, t + 1)
                        act.activation(hidT[:, t % 2], bank[:, 4:6, :].rearrange("p a (m n) -> p (a m) n", m=4),
                                       ACT.Copy).then_inc(hT_ready, 1)
                    if t >= 0 and t % 2 == 0 and t // 2 + 1 < NB:
                        lead_xqT(t // 2 + 1)
                    if STAGES > 3 and t == 5:
                        front(1, 0, 0)
                if STAGES > 3:
                    front(1, 0, 3)
                    front(1, 0, 4)

            if STAGES > 3:
                act.preload_act_table(ACT.Exp)
                attention(1)

            if STAGES > 4:
                for g in range(PAIRS // 2):
                    act.wait_ge(fold_psum, g + 1)
                    act.activation(Cx[:, 2 * g:2 * g + 2], bank[:, g % 2, :].rearrange("p (j n) -> p j n", j=2),
                                   ACT.Copy).then_inc(fold_act, 1)
                for g in range(NH // 4):
                    act.wait_ge(fold_psum, PAIRS // 2 + g + 1)
                    act.activation(Gq[:, 8 * g:8 * g + 8], bank[0:HC, g % 2, :].rearrange("p (m n) -> p m n", m=8).unsqueeze(
                        2).to_broadcast([HC, 8, 2, DC]), ACT.Copy).then_inc(fold_act, 1)
                for h in range(NH):
                    act.wait_ge(fold_psum, PAIRS // 2 + NH // 4 + h + 1)
                    act.activation(Aq[0][:, h], bank[:, h % 4, 0:2 * CQ].rearrange("p (k n) -> p k n", k=KD),
                                   ACT.Copy).then_inc(fold_act, 1)
                act.wait_ge(kvrT_psum, 1)
                act.activation(kk[:, :, 0, :], bank[:, 5:7, :].rearrange("p a (b n) -> p (a b) n", b=2), ACT.Copy).then_inc(kk_lead, 1)
                act.wait_ge(xnTp_ready, 3 * NB + 1)
                act.activation(xT_lead[:, 0], bank[:, 7, :].rearrange("p (k n) -> p k n", k=KD), ACT.Copy).then_inc(xnT_ready, 1)
                for u, b, h in cross_slots():
                    w = u - 4
                    if w >= 0 and w % 2 == 1:
                        j = w // 2
                        act.wait_ge(cT_psum, j + 1)
                        act.activation(cT[:, j % 2], bank[:, 2, 256:512], ACT.Copy).then_inc(cT_ready, 1)
                    w = u - 1
                    if 0 <= w < CROSS:
                        act.wait_ge(mx_ready, w + 1)
                        if w >= 2:
                            act.wait_ge(pxT_psum, w - 1)
                        for r in range(2):
                            act.activation(px[:, w % 2, r, :], bank[:, 3 + w % 2, r * SEQ:(r + 1) * SEQ], ACT.Exp,
                                           bias=nmax[:, w % 2, r:r + 1],
                                           accum_out=sums[:, r, w % NH:w % NH + 1]).then_inc(px_ready, 1)
                    if 0 <= u < CROSS:
                        act.wait_ge(z_psum, u + 1)
                        if u >= 2:
                            act.wait_ge(sx_ready, u - 1)
                        act.activation(zz[:, u % 2], bank[:, 2, 0:SEQ], ACT.Copy).then_inc(z_ready, 1)
                    if 0 <= w < CROSS:
                        act.wait_ge(pxT_psum, w + 1)
                        if w >= 2:
                            act.wait_ge(cx_psum, w - 1)
                        act.activation(pxT[:, w % 2], bank[:, 5, :].rearrange("p (k n) -> p k n", k=2), ACT.Copy).then_inc(pxT_ready, 1)
                    if STAGES > 5 and b == NB and h >= 1:
                        copy_xm(h - 1)
                    if h == 8 and 0 <= b < NB - 1:
                        act.wait_ge(xnTp_ready, 3 * NB + b + 2)
                        act.activation(xT_lead[:, (b + 1) % 2], bank[:, u % 2, :].rearrange("p (k n) -> p k n", k=KD),
                                       ACT.Copy).then_inc(xnT_ready, 1)

            if STAGES > 5:
                copy_xm(NB - 1)
                act.wait_ge(lg_psum, 1)
                act.activation(scb, bank[:, 0, 0:NT * NE].rearrange("p (t e) -> p t e", t=NT), ACT.Exp, scale=-1.0).then_inc(esig_ready, 1)
                act.preload_act_table(ACT.Silu)
                for b in range(NB):
                    act.wait_ge(sh_psum, b + 1)
                    if b >= 2:
                        act.wait_ge(shh_ready, b - 1)
                    act.activation(sh_g[:, b % 2], bank[:, 1 + 2 * (b % 2), :].rearrange("p (f n) -> p f n", f=2), ACT.Silu).then_inc(shg_ready, 1)
                act.wait_ge(gat_psum, 1)
                act.activation(bufT, bank[:, 0:2, :], ACT.Copy).then_inc(buf_ready, 1)
                for c in range(NC):
                    act.wait_ge(eh_psum, c + 1)
                    act.activation(h_g, bank[:, 4, :], ACT.Silu).then_inc(eg_ready, 1)
                    for t in range(0, NT, 2):
                        act.wait_ge(hotT_psum, NT * c + t + 1)
                        act.activation(hotT[:, t], bank[:, 2, :].rearrange("p (k n) -> p k n", k=KS), ACT.Copy).then_inc(hotT_even, 1)
                    act.wait_ge(ob_psum, c + 1)
                    act.wait_ge(ws_ready, 2 * (c + 1))
                    for s in range(KS):
                        act.activation(ob[0][:, s, :], bank[:, 6 + s // 2, (s % 2) * D:(s % 2 + 1) * D], ACT.Copy,
                                       scale=wslot[:, s:s + 1]).then_inc(ob_lead, 1)
                    if c + 1 < NC:
                        act.wait_ge(gat_psum, c + 2)
                        act.activation(bufT, bank[:, 0:2, :], ACT.Copy).then_inc(buf_ready, 1)

        @block.vector
        def _(dve):
            dve.wait_ge(s_x0, 16)

            def norm(n, b, st):
                for r in range(2):
                    st.mark(dve.bn_stats(stat[:, r, :], X[:, bass.ts(b, 2), :][:, r, :]))
                st.wait_apart(scrap[:])
                for r in range(2):
                    dve.bn_aggr(mv[:, r, :], stat[:, r, :]).then_inc(mv_ready, 1)
                dve.wait_ge(mv_ready, 2 * n + 2)
                dve.wait_ge(rstd_ready, n + 1)
                for r in range(2):
                    dve.tensor_scalar(xn[:, r, :], X[:, bass.ts(b, 2), :][:, r, :], mv[:, r, 0:1], rstd[:, r:r + 1],
                                      ALU.subtract, ALU.mult).then_inc(xn_ready, 1)

            def add_y(n, b, col, scale=None):
                dve.wait_ge(y_ready, n + 1)
                xb = X[:, bass.ts(b, 2), :]
                y = col.rearrange("p (r n) -> p r n", r=2)
                if scale is None:
                    dve.tensor_tensor(xb, y, xb, ALU.add).then_inc(x_done, 1)
                else:
                    dve.scalar_tensor_tensor(xb, y, scale, xb, ALU.mult, ALU.add).then_inc(x_done, 1)

            def context_stats(st, tiles):
                dve.wait_ge(x_done, tiles[-1] // 2 + 1)
                for t in tiles:
                    st.mark(dve.bn_stats(mstat[:, t, :], X[:, t, :]))
                st.wait()
                for t in tiles:
                    dve.bn_aggr(mmv[:, t, :], mstat[:, t, :]).then_inc(mv_ready, 1)

            def stats(n, st):
                for r in range(2):
                    st.mark(dve.bn_stats(stat[:, r, :], X[:, 2 * n + r, :]))
                st.wait()
                for r in range(2):
                    dve.bn_aggr(mv[:, r, :], stat[:, r, :]).then_inc(mv_ready, 1)

            def apply(l, n):
                c = n + 3 * NB * l
                dve.wait_ge(mv_ready, 2 * c + 2)
                dve.wait_ge(rstd_ready, c + 1)
                for r in range(2):
                    dve.tensor_scalar(xns[:, n % 2, r, :], X[:, 2 * n + r, :], mv[:, r, 0:1], rstd[:, r:r + 1],
                                      ALU.subtract, ALU.mult).then_inc(xn_ready, 1)

            def rope(n, r):
                dve.wait_ge(proj[1], 4 * n + r + 1)
                src = bank[:, 7, 0:320].rearrange("p (h n) -> p h n", n=HD)
                c = qk_c[:, r, :].rearrange("p (h n) -> p h n", n=HD)
                s = qk_s[:, r, :].rearrange("p (h n) -> p h n", n=HD)
                dve.tensor_tensor(c, src, cos1[:, r, :].unsqueeze(1).to_broadcast([P, 20, HD]),
                                  ALU.mult).then_inc(rope_parts, 1)
                for f in range(2):
                    o = 8 * f
                    dve.tensor_tensor(s[:, :, o:o + 8], src[:, :, 8 - o:16 - o],
                                      sin1[:, r, o:o + 8].unsqueeze(1).to_broadcast([P, 20, 8]),
                                      ALU.mult).then_inc(rope_parts, 1)
                dve.tensor_copy(V[:, n % 2, r, 0:64], bank[:, 7, 320:384]).then_inc(rope_left, 1)
                dve.wait_ge(rope_parts, 6 * n + 3 * r + 3)
                dve.tensor_tensor(q_r[:, r, :], qk_c[:, r, 0:256], qk_s[:, r, 0:256], ALU.add).then_inc(roped, 1)
                kc, ks = (v[:, r, 256:320].rearrange("p (g n) -> p g n", n=HD).unsqueeze(2).to_broadcast([P, 4, 4, HD])
                          for v in (qk_c, qk_s))
                dve.tensor_tensor(k_r[:, r, :].rearrange("p (g m n) -> p g m n", g=4, m=4), kc, ks,
                                  ALU.add).then_inc(roped, 1)

            def context_apply(tiles):
                dve.wait_ge(mv_ready, 2 * NB + tiles[-1] + 1)
                dve.wait_ge(rstd_ready, NB + tiles[-1] // 2 + 1)
                for t in tiles:
                    dve.tensor_scalar(xm[:, t, :], X[:, t, :], mmv[:, t, 0:1], mrstd[:, t:t + 1], ALU.subtract,
                                      ALU.mult).then_inc(xn_ready, 1)

            def context_keys():
                dve.wait_ge(kv_psum, 2)
                dve.wait_ge(s_ctx, 7 * 16)
                dve.tensor_tensor(kvj, bank[:, 2, :].rearrange("p (t n) -> p t n", t=NT),
                                  bk_row[:].unsqueeze(1).to_broadcast([P, NT, DC]), ALU.add).then_inc(kvj_ready, 1)

            def context_variance(st, b):
                dve.wait_ge(sim_ready, b + 1)
                for r in range(2):
                    st.mark(dve.bn_stats(sstat[:, r, :], bank[:, b, r * SEQ:(r + 1) * SEQ]))
                st.wait()
                for r in range(2):
                    dve.bn_aggr(smv[:, b % 2, r, :], sstat[:, r, :]).then_inc(smv_ready, 1)

            def context_center(b):
                i = b % 2
                dve.wait_ge(smv_ready, 2 * b + 2)
                dve.wait_ge(srstd_ready, b + 1)
                if b >= 2:
                    dve.wait_ge(simg_ready, b - 1)
                for r in range(2):
                    dve.tensor_scalar(simn[:, i, r, :], bank[:, b, r * SEQ:(r + 1) * SEQ], smv[:, i, r, 0:1],
                                      srstd[:, i, r:r + 1], ALU.subtract, ALU.mult).then_inc(simn_ready, 1)

            def trail_q(l, n):
                dve.wait_ge(q_ready[l], n + 1)
                dve.scalar_tensor_tensor(q_trail[:, n % 2], bank[:, 7, :].rearrange("p (k n) -> p k n", k=KD), float(HD) ** -0.5,
                                         q_lead[:, n % 2].bitcast(F32), ALU.mult, ALU.subtract).then_inc(q_split[l], 1)

            def attention(l, st):
                def row_max(u):
                    i = u % 2
                    for r in range(2):
                        dve.wait_ge(s_ready[l], 2 * u + r + 1)
                        n = SEQ if r else P
                        dve.tensor_reduce(nmax[:, i, 2 * r:2 * r + 2],
                                          bank[:, 2 * i + r, 0:2 * n].rearrange("p (e n) -> p e n", e=2),
                                          AX.X, ALU.max, negate=True).then_inc(max_ready[l], 1)

                for u, b, j in slots():
                    if 0 <= u + 1 < UNITS:
                        row_max(u + 1)
                    v = u + 2
                    if 0 <= v < UNITS:
                        dve.wait_ge(kM_ready[l], 2 * (v + 1))
                        for e in range(2):
                            m = 2 * (v % 4) + e
                            dve.scalar_tensor_tensor(kM[:, v % 2, 1, e, :], kT[:, (v // PAIRS) % 2, (v % PAIRS) // 4, :],
                                                     head_rows[:, m:m + 1], kM[:, v % 2, 0, e, :].bitcast(F32), ALU.mult,
                                                     ALU.subtract).then_inc(kM_split[l], 1)
                    if 0 <= u < UNITS:
                        dve.wait_ge(pT_psum[l], u + 1)
                        if u >= 2:
                            dve.wait_ge(av_done[l], u - 1)
                        dve.tensor_copy(probT[:, u % 2, 0:4, :], bank[:, 4, :].rearrange("p (m n) -> p m n", m=4)).then_inc(pT4_ready[l], 1)
                    n = b - 1
                    if 0 <= n < NB and j == 0:
                        dve.wait_ge(p_ready[l], 4 * PAIRS * (n + 1))
                        st.mark(dve.reciprocal(rsum[:], asums[:, n % 2]))
                        dve.wait_ge(av_done[l], PAIRS * (n + 1))
                        st.wait()
                        dve.tensor_tensor(On[:].rearrange("p r (h n) -> p r h n", h=NH),
                                          bank[:, 6, :].rearrange("p (r h n) -> p r h n", r=2, h=NH),
                                          rsum[:].unsqueeze(3).to_broadcast([P, 2, NH, HD]), ALU.mult).then_inc(on_ready[l], 1)
                    if l == 0 and b == 2 and 1 <= j <= 3:
                        dve.wait_ge(s_wff, 3 * 16)
                        dve.tensor_reduce(wabs[:, j - 1:j], w_ff[:, 2048 * (j - 1):2048 * j], AX.X, ALU.add,
                                          apply_absolute_value=True).then_inc(wabs_ready, 1)
                    if STAGES > 1 and l == 0 and b == NB and j == 1:
                        context_stats(st, range(0, NT - 2))
                        context_apply(range(0, NT - 2))
                    if STAGES > 1 and l == 0 and b == NB and j == 2:
                        context_keys()
                        context_variance(st, 0)
                        context_center(0)
                    if l and j in (1, 2) and 1 <= b + 1 < NB:
                        rope(b + 1, j - 1)
                    if j == (3 if l else 1) and l <= b + 1 < NB:
                        trail_q(l, b + 1)
                    if l == 0 and b == -2 and j == 7:
                        dve.wait_ge(s_const, 3 * 16)
                        dve.tensor_copy(ident_h[:], ident[:]).then_inc(casts, 1)
                        dve.tensor_copy(causal_h[:], causal[:]).then_inc(casts, 1)
                        dve.wait_ge(s_x, 16)
                    if 2 * l <= b + 2 < NB:
                        if j == 5:
                            stats(b + 2, st)
                        if j == 6:
                            apply(l, b + 2)
                    if 0 <= n < NB and j == (3 if STAGES > 1 and l == 0 and b == NB else 7):
                        dve.wait_ge(y_ready, n + 1 + 2 * NB * l)
                        dve.tensor_tensor(X[:, 2 * n:2 * n + 2, :], bank[:, 7, :].rearrange("p (r n) -> p r n", r=2),
                                          X[:, 2 * n:2 * n + 2, :], ALU.add).then_inc(x_done, 1)

            attention(0, Steps(dve, dve_steps[0]))

            if STAGES > 1:
                st = Steps(dve, dve_steps[1])
                context_stats(st, range(NT - 2, NT))
                context_apply(range(NT - 2, NT))

                def step(ins):
                    st.mark(ins)
                    st.wait()

                def scales(m, k, keep):
                    step(dve.tensor_scalar_max(gscl[:, m, 0:k], gmax[:, m, 0:k], 1e-5))
                    step(dve.reciprocal(grcp[:, m, 0:k], gscl[:, m, 0:k]))
                    st.mark(dve.tensor_scalar_mul(grcp[:, m, 0:k], grcp[:, m, 0:k], QB))
                    step(dve.tensor_scalar_mul(keep, gscl[:, m, 0:k], 1.0 / QB))

                def ffn_stats(b):
                    dve.wait_ge(x_done, NB + b + 1)
                    for r in range(2):
                        st.mark(dve.bn_stats(stat[:, r, :], X[:, 2 * b + r, :]))
                    st.wait()
                    for r in range(2):
                        dve.bn_aggr(mv[:, r, :], stat[:, r, :]).then_inc(mv_ready, 1)

                def ffn_tokens(b):
                    dve.wait_ge(mv_ready, 2 * (2 * NB + b) + 2)
                    dve.wait_ge(rstd_ready, 2 * NB + b + 1)
                    x = xns[:, b % 2]
                    for r in range(2):
                        dve.tensor_scalar(x[:, r, :], X[:, 2 * b + r, :], mv[:, r, 0:1], rstd[:, r:r + 1],
                                          ALU.subtract, ALU.mult).then_inc(xn_ready, 1)
                    dve.wait_ge(xn_ready, 2 * (2 * NB + b) + 2)
                    xg = x.rearrange("p r (g n) -> p (r g) n", n=GRP)
                    step(dve.tensor_reduce(gmax[:, 0, 0:8], xg, AX.X, ALU.max, apply_absolute_value=True))
                    scales(0, 8, gscl[:, 0, 8:16])
                    step(dve.tensor_tensor(xg, xg, grcp[:, 0, 0:8].unsqueeze(2).to_broadcast([P, 8, GRP]), ALU.mult))
                    step(dve.tensor_scalar(xg, xg, ROUND, -ROUND, ALU.add, ALU.add))
                    dve.tensor_tensor(xg, xg, gscl[:, 0, 8:16].unsqueeze(2).to_broadcast([P, 8, GRP]),
                                      ALU.mult).then_inc(xq_ready, 1)

                def trail_xqT(b):
                    dve.wait_ge(xqT_lead, b + 1)
                    dve.tensor_tensor(xqT[:, b % 2, 1], bank[:, 7, :].rearrange("p (k n) -> p k n", k=KD),
                                      xqT[:, b % 2, 0].bitcast(F32), ALU.subtract).then_inc(xqT_ready, 1)

                for s in range(1, NB + 2):
                    if s < NB:
                        context_variance(st, s)
                    b, i = s - 1, (s - 1) % 2
                    if 0 <= b < NB:
                        dve.wait_ge(simg_ready, b + 1)
                        dve.tensor_tensor(simg[:, i], simg[:, i], beta[:].unsqueeze(1).to_broadcast([P, 2, D]),
                                          ALU.add).then_inc(simb_ready, 1)
                        dve.wait_ge(simb_ready, b + 1)
                        dve.tensor_reduce(nmax[:, i, 0:2], simg[:, i], AX.X, ALU.max, negate=True).then_inc(smax_ready, 1)
                    if s < NB:
                        context_center(s)
                    b, i = s - 2, s % 2
                    if 0 <= b < NB:
                        dve.wait_ge(sexp_ready, 2 * b + 2)
                        dve.reciprocal(rsum[:, :, b], sums[:, :, b]).then_inc(srcp_ready, 1)
                        dve.wait_ge(srcp_ready, b + 1)
                        for r in range(2):
                            xb = X[:, 2 * b + r, :]
                            dve.scalar_tensor_tensor(xb, prob_x[:, i, r, :], rsum[:, r, b:b + 1], xb, ALU.mult,
                                                     ALU.add).then_inc(x_done if r else x_half, 1)
                    if STAGES > 2 and s == 2:
                        ffn_stats(0)
                    if STAGES > 2 and s == 3:
                        ffn_tokens(0)
                    if STAGES > 2 and s == 4:
                        trail_xqT(0)

            if STAGES > 2:
                st = Steps(dve, dve_steps[2])

                def ffn_hidden(t):
                    for c in range(2):
                        dve.wait_ge(gate_ready, 2 * t + c + 1)
                        if t >= 2 and c == 0:
                            dve.wait_ge(hT_psum, t - 1)
                        o = slice(c * 512, (c + 1) * 512)
                        dve.scalar_tensor_tensor(hid[:, t % 2, o], bank[:, 2 * c + 1, :], wmean[:, 1:2], gate_f[:, t % 2, o],
                                                 ALU.mult, ALU.mult).then_inc(hid_used, 1)

                def ffn_quant(t):
                    hg = hid[:, t % 2, :].rearrange("p (g n) -> p g n", n=GRP)
                    dve.wait_ge(hid_used, 2 * t + 2)
                    step(dve.tensor_reduce(gmax[:, 1, :], hg, AX.X, ALU.max, apply_absolute_value=True))
                    scales(1, 16, gscl_h[:, t % 2, :])
                    step(dve.tensor_tensor(hg, hg, grcp[:, 1, :].unsqueeze(2).to_broadcast([P, 16, GRP]), ALU.mult))
                    dve.tensor_scalar(hg, hg, ROUND, -ROUND, ALU.add, ALU.add).then_inc(hq_rounded, 1)

                dve.wait_ge(sign_ready, 4)
                for t in range(-1, NT + 1):
                    if t % 2 == 1 and (t + 1) // 2 + 1 < NB:
                        ffn_stats((t + 1) // 2 + 1)
                    if STAGES > 3 and t in (5, 6):
                        dve.wait_ge(x_done, 2 * NB + t - 4)
                        stats(t - 5, st)
                    if 0 <= t < NT:
                        ffn_quant(t)
                    if STAGES > 3 and t in (5, 6):
                        dve.wait_ge(xqT_psum, NB)
                        apply(1, t - 5)
                    if STAGES > 3 and t in (7, 8):
                        rope(0, t - 7)
                    if STAGES > 3 and t == 8:
                        trail_q(1, 0)
                    n = t // 2 + 1
                    prepare = t >= 0 and t % 2 == 0 and n < NB
                    if prepare:
                        ffn_tokens(n)
                    if t >= 2 and t % 2 == 0:
                        b = t // 2 - 1
                        dve.wait_ge(y_ready, NB + b + 1)
                        xb = X[:, 2 * b:2 * b + 2, :]
                        dve.scalar_tensor_tensor(xb, bank[:, 6, :].rearrange("p (r n) -> p r n", r=2), wmean[:, 2:3], xb,
                                                 ALU.mult, ALU.add).then_inc(x_done, 1)
                    if t + 1 < NT:
                        ffn_hidden(t + 1)
                    if prepare:
                        trail_xqT(n)

            if STAGES > 3:
                dve.wait_ge(s_w1, 4 * 16)
                dve.wait_ge(x_done, 3 * NB)
                attention(1, Steps(dve, dve_steps[3]))

            if STAGES > 4:
                dve.wait_ge(s_wx, 10 * 16)
                st = Steps(dve, dve_steps[4])
                src = ctxk[:].rearrange("p (b r) n -> p b r n", b=NB)
                dve.tensor_tensor(kv_c, src, cosk[:].unsqueeze(1).to_broadcast([P, NB, 2, DC]), ALU.mult).then_inc(kv_parts, 1)
                for f in range(2):
                    o = DC // 2 * f
                    dve.tensor_tensor(kv_s[:, :, :, o:o + 32], src[:, :, :, 32 - o:64 - o],
                                      sink[:, :, o:o + 32].unsqueeze(1).to_broadcast([P, NB, 2, 32]), ALU.mult).then_inc(kv_parts, 1)
                dve.wait_ge(kv_parts, 3)
                for e in range(2):
                    dve.tensor_tensor(kvr[:, :, e, :], kv_c.rearrange("p b r n -> p (b r) n"),
                                      kv_s.rearrange("p b r n -> p (b r) n"), ALU.add).then_inc(kvr_ready, 1)

                def cross_stats(b):
                    for r in range(2):
                        st.mark(dve.bn_stats(stat[:, r, :], X[:, 2 * b + r, :]))
                    st.wait()
                    for r in range(2):
                        dve.bn_aggr(mv[:, r, :], stat[:, r, :]).then_inc(mv_ready, 1)

                def cross_apply(b):
                    dve.wait_ge(mv_ready, 2 * (4 * NB + b) + 2)
                    dve.wait_ge(rstd_ready, 4 * NB + b + 1)
                    for r in range(2):
                        dve.tensor_scalar(xns[:, b % 2, r, :], X[:, 2 * b + r, :], mv[:, r, 0:1], rstd[:, r:r + 1],
                                          ALU.subtract, ALU.mult).then_inc(xn_ready, 1)

                def expert_stats(tiles):
                    dve.wait_ge(x_done, 4 * NB + tiles[-1] // 2 + 1)
                    for t in tiles:
                        st.mark(dve.bn_stats(mstat[:, t, :], X[:, t, :]))
                    st.wait()
                    for t in tiles:
                        dve.bn_aggr(mmv[:, t, :], mstat[:, t, :]).then_inc(mmv_ready, 1)

                def expert_apply(tiles):
                    dve.wait_ge(mmv_ready, tiles[-1] + 1)
                    dve.wait_ge(mrstd_ready, tiles[-1] + 1)
                    dve.wait_ge(z_psum, CROSS)
                    for t in tiles:
                        dve.tensor_scalar(xm[:, t, :], X[:, t, :], mmv[:, t, 0:1], mrstd[:, t:t + 1], ALU.subtract,
                                          ALU.mult).then_inc(xm_ready, 1)

                dve.wait_ge(x_done, 4 * NB)
                cross_stats(0)
                cross_apply(0)
                for h in range(NH):
                    dve.wait_ge(fold_act, PAIRS // 2 + NH // 4 + h + 1)
                    dve.tensor_tensor(Aq[1][:, h], bank[:, h % 4, 0:2 * CQ].rearrange("p (k n) -> p k n", k=KD),
                                      Aq[0][:, h].bitcast(F32), ALU.subtract).then_inc(fold_dve, 1)

                def trail_xT(b, col):
                    dve.wait_ge(xnT_ready, 3 * NB + b + 1)
                    dve.tensor_tensor(xT_trail[b % 2][:], col.rearrange("p (k n) -> p k n", k=KD),
                                      xT_lead[:, b % 2].bitcast(F32), ALU.subtract).then_inc(xT_split, 1)

                dve.wait_ge(kk_lead, 1)
                dve.tensor_tensor(kk[:, :, 1, :], bank[:, 5:7, :].rearrange("p a (b n) -> p (a b) n", b=2),
                                  kk[:, :, 0, :].bitcast(F32), ALU.subtract).then_inc(kk_ready, 1)
                trail_xT(0, bank[:, 7, :])
                for u, b, h in cross_slots():
                    if h == 9 and 0 <= b < NB - 1:
                        trail_xT(b + 1, bank[:, (u - 1) % 2, :])
                    w = u - 1
                    if 0 <= w < CROSS:
                        dve.wait_ge(sx_ready, w + 1)
                        dve.tensor_reduce(nmax[:, w % 2, 0:2], bank[:, 3 + w % 2, :].rearrange("p (r n) -> p r n", r=2),
                                          AX.X, ALU.max, negate=True).then_inc(mx_ready, 1)
                    w = u + 1
                    if w < CROSS:
                        dve.wait_ge(qx_psum, w + 1)
                        if w >= 2:
                            dve.wait_ge(qx_ready, 2 * (w - 1))
                        q = bank[0:HC, w % 2, :].rearrange("p (f n) -> p f n", f=2)
                        dve.tensor_tensor(qx_c[:, w % 2], q, cosq[:], ALU.mult).then_inc(qx_cs, 1)
                        dve.tensor_tensor(qx_s[:, w % 2], q, sinq[:], ALU.mult).then_inc(qx_cs, 1)
                    if 0 <= u < CROSS:
                        dve.wait_ge(z_ready, u + 1)
                        dve.tensor_tensor(zz[DC:P, u % 2], bank[DC:P, 2, 0:SEQ], zz[DC:P, u % 2].bitcast(F32),
                                          ALU.subtract).then_inc(z_split, 1)
                    w = u - 2
                    if 0 <= w < CROSS:
                        j, e, k = w // 2, w % 2, w % NH
                        dve.wait_ge(px_ready, 2 * (w + 1))
                        st.mark(dve.reciprocal(rsum[:, :, k], sums[:, :, k]))
                        dve.wait_ge(cx_psum, w + 1)
                        if e == 0 and j >= 2:
                            dve.wait_ge(cT_psum, j - 1)
                        st.wait()
                        dve.tensor_tensor(cn[:, j % 2, :, e * DC:(e + 1) * DC],
                                          bank[:, 6, 0:256].rearrange("p (r n) -> p r n", r=2)[:, :, e * DC:(e + 1) * DC],
                                          rsum[:, :, k:k + 1].to_broadcast([P, 2, DC]), ALU.mult).then_inc(cn_ready, 1)
                    if 0 <= b < NB - 1:
                        if h == 4:
                            cross_stats(b + 1)
                        if h == 6:
                            cross_apply(b + 1)
                    if STAGES > 5 and b == NB and h == 0:
                        expert_stats(range(0, NT - 2))
                    if STAGES > 5 and b == NB and h == 1:
                        expert_apply(range(0, NT - 2))
                    if b >= 1 and h == 3:
                        dve.wait_ge(y_ready, 3 * NB + b)
                        xb = X[:, 2 * b - 2:2 * b, :]
                        dve.tensor_tensor(xb, bank[:, 7, :].rearrange("p (r n) -> p r n", r=2), xb, ALU.add).then_inc(x_done, 1)

            if STAGES > 5:
                dve.wait_ge(s_wm, 6 * 16)
                expert_stats(range(NT - 2, NT))
                st = Steps(dve, dve_steps[5])
                expert_apply(range(NT - 2, NT))

                def step(ins):
                    st.mark(ins)
                    st.wait()

                def shared_hidden(b):
                    dve.wait_ge(shg_ready, b + 1)
                    dve.tensor_tensor(sh_h[:, b % 2], bank[:, 2 + 3 * (b % 2), :].rearrange("p (f n) -> p f n", f=2),
                                      sh_g[:, b % 2], ALU.mult).then_inc(shh_ready, 1)

                def shared_add(b):
                    dve.wait_ge(shy_psum, b + 1)
                    dve.tensor_tensor(X[:, 2 * b:2 * b + 2, :], bank[:, 6 + b % 2, :].rearrange("p (r n) -> p r n", r=2),
                                      X[:, 2 * b:2 * b + 2, :], ALU.add).then_inc(x_done, 1)

                dve.wait_ge(esig_ready, 1)
                step(dve.tensor_scalar_add(scb, scb, 1.0))
                step(dve.reciprocal(sc, scb))
                step(dve.tensor_tensor(scb, sc, gbias[:].unsqueeze(1).to_broadcast([P, NT, NE]), ALU.add))
                for g in range(NT * NG):
                    st.mark(dve.max(top_g[:, g, :], scb[:, g // NG, EG * (g % NG):EG * (g % NG + 1)]))
                st.wait()
                shared_hidden(0)
                step(dve.tensor_tensor(gs, top_g.rearrange("p (t g) n -> p t g n", t=NT)[:, :, :, 0],
                                       top_g.rearrange("p (t g) n -> p t g n", t=NT)[:, :, :, 1], ALU.add))
                other = gs.unsqueeze(2).to_broadcast([P, NT, NG, NG])
                own = gs.unsqueeze(3).to_broadcast([P, NT, NG, NG])
                st.mark(dve.tensor_tensor(cmp_a, other, own, ALU.is_gt))
                step(dve.tensor_tensor(cmp_b, other, own, ALU.is_equal))
                step(dve.tensor_tensor(cmp_b, cmp_b, earlier.rearrange("p (g k) -> p g k", g=NG).unsqueeze(1).to_broadcast(
                    [P, NT, NG, NG]), ALU.mult))
                step(dve.tensor_tensor(cmp_a, cmp_a, cmp_b, ALU.add))
                step(dve.tensor_reduce(rank, cmp_a.rearrange("p t g k -> p (t g) k"), AX.X, ALU.add))
                step(dve.tensor_scalar(rank, rank, 2.0, None, ALU.is_lt))
                step(dve.tensor_tensor(tmp_e.rearrange("p t (g n) -> p (t g) n", g=NG),
                                       scb.rearrange("p t (g n) -> p (t g) n", g=NG),
                                       rank.unsqueeze(2).to_broadcast([P, NT * NG, EG]), ALU.mult))
                shared_hidden(1)
                for t in range(NT):
                    st.mark(dve.max(top_e[:, t, :], tmp_e[:, t, :]))
                st.wait()
                for t in range(NT):
                    st.mark(dve.max_index(idx_u[:, t, :], top_e[:, t, :], tmp_e[:, t, :]))
                st.wait()
                shared_add(0)
                shared_hidden(2)
                step(dve.tensor_copy(idx_f, idx_u[:]))
                for t in range(NT):
                    st.mark(dve.tensor_tensor(pick[:, t], iota_e.unsqueeze(2).to_broadcast([P, NE, TOPK]),
                                              idx_f[:, t, 0:TOPK].unsqueeze(1).to_broadcast([P, NE, TOPK]), ALU.is_equal))
                st.wait()
                st.mark(dve.tensor_reduce(mask, pick, AX.X, ALU.add))
                st.wait()
                shared_add(1)
                shared_hidden(3)
                st.mark(dve.memset(seen[:, 0], 0.0))
                st.wait()
                for t in range(1, NT):
                    if t < NT - 1:
                        step(dve.tensor_tensor(seen[:, t], seen[:, t - 1], mask[:, t - 1], ALU.add))
                    else:
                        dve.tensor_tensor(seen[:, t], seen[:, t - 1], mask[:, t - 1], ALU.add).then_inc(mask_ready, 1)
                dve.wait_ge(pos_psum, 1)
                pos = bank[:, 4, 0:NT * NE].rearrange("p (t e) -> p t e", t=NT)
                step(dve.scalar_tensor_tensor(keep, pos, float(CAP), mask, ALU.is_lt, ALU.mult))
                step(dve.scalar_tensor_tensor(posm, pos, 1.0, keep, ALU.add, ALU.mult))
                step(dve.tensor_scalar_add(posm, posm, -1.0))
                def one_hot(c, t):
                    if c >= 2:
                        dve.wait_ge(hotT_psum, NT * (c - 2) + t + 1)
                    dve.tensor_tensor(hot[c % 2][:, t].rearrange("p (e n) -> p e n", e=EC),
                                      iota_s.unsqueeze(1).to_broadcast([P, EC, CAP]),
                                      posm[:, t, c * EC:(c + 1) * EC].unsqueeze(2).to_broadcast([P, EC, CAP]),
                                      ALU.is_equal).then_inc(hot_ready, 1)

                for t in range(NT):
                    one_hot(0, t)
                shared_add(2)
                shared_add(3)
                step(dve.tensor_tensor(wgt, sc, mask, ALU.mult))
                step(dve.tensor_reduce(wsum, wgt, AX.X, ALU.add))
                step(dve.tensor_scalar_add(wsum, wsum, 1e-20))
                step(dve.reciprocal(wrcp, wsum))
                step(dve.tensor_scalar_mul(wrcp, wrcp, 2.0))
                step(dve.tensor_tensor(wgt, wgt, wrcp.unsqueeze(2).to_broadcast([P, NT, NE]), ALU.mult))
                step(dve.tensor_copy(wgts[0][:], wgt))
                dve.tensor_tensor(wgts[1][:], wgt, wgts[0][:].bitcast(F32), ALU.subtract).then_inc(weights_ready, 1)
                for c in range(NC):
                    if c == 0:
                        for t in range(NT):
                            one_hot(1, t)
                    dve.wait_ge(ws_psum, c + 1)
                    dve.tensor_copy(ws_row, bank[0:NE, 2, :]).then_inc(ws_copied, 1)
                    dve.wait_ge(ws_turned, c + 1)
                    for e in range(2):
                        rows = slice(CAP * e, CAP * (e + 1))
                        for s in range(KS):
                            o = dve.tensor_copy(wslot[rows, s:s + 1], bank[rows, 3, s * NE + EC * c + 2 * s + e:
                                                                           s * NE + EC * c + 2 * s + e + 1])
                        o.then_inc(ws_ready, 1)
                    dve.wait_ge(eg_ready, c + 1)
                    dve.tensor_tensor(h_T, bank[:, 5, :], h_g, ALU.mult).then_inc(eh_ready, 1)
                    for t in range(1, NT, 2):
                        dve.wait_ge(hotT_psum, NT * c + t + 1)
                        dve.tensor_copy(hotT[:, t], bank[:, 3, :].rearrange("p (k n) -> p k n", k=KS)).then_inc(hotT_odd, 1)
                    dve.wait_ge(ws_ready, 2 * (c + 1))
                    for s in range(KS):
                        dve.wait_ge(ob_lead, KS * c + 2 * (s // 2) + 2)
                        dve.scalar_tensor_tensor(ob[1][:, s, :], bank[:, 6 + s // 2, (s % 2) * D:(s % 2 + 1) * D],
                                                 wslot[:, s:s + 1], ob[0][:, s, :].bitcast(F32), ALU.mult,
                                                 ALU.subtract).then_inc(ob_ready, 1)
                    for q in range(NT // 2):
                        n = c * (NT // 2) + q
                        if c + 2 < NC:
                            one_hot(c + 2, 2 * q)
                            one_hot(c + 2, 2 * q + 1)
                        dve.wait_ge(ey_psum, n + 1)
                        xb = X[:, 2 * q:2 * q + 2, :]
                        dve.wait_ge(x_done, 6 * NB + max(0, n - 3))
                        dve.tensor_tensor(xb, bank[:, 6 + n % 2, :].rearrange("p (r n) -> p r n", r=2), xb,
                                          ALU.add).then_inc(x_done, 1)

        @block.tensor
        def _(pe):
            mm, tr = pe.matmul, pe.transpose
            pe.wait_ge(s_const, 3 * 16)

            def turn_xn(n, ready=None, count=None, then=None):
                pe.wait_ge(xn_ready if ready is None else ready, 2 * n + 2 if ready is None else count)
                for k in range(KD):
                    for r in range(2):
                        o = tr(bank[:, 7, k * SEQ + r * P:k * SEQ + (r + 1) * P], xn[:, r, k * P:(k + 1) * P], ident[:])
                o.then_inc(xnTp_ready, 1)
                if then:
                    then()
                pe.wait_ge(xnT_ready, n + 1)

            def turned(src, done):
                for k in range(KD):
                    for r in range(2):
                        o = tr(bank[:, 7, k * SEQ + r * P:k * SEQ + (r + 1) * P], src[:, r, k * P:(k + 1) * P], ident[:])
                o.then_inc(done, 1)

            def front(l, n, j):
                if j == 0:
                    pe.wait_ge(xn_ready, 2 * (n + 3 * NB * l) + 2)
                    if l and n == 0:
                        pe.wait_ge(xqT_ready, NB)
                    if n >= 3:
                        pe.wait_ge(x_done, 3 * NB * l + n - 2)
                    turned(xns[:, n % 2], xnTp_ready)
                elif j == 1:
                    pe.wait_ge(xnT_ready, n + 2 * NB * l + 1)
                if l == 0 and j in (1, 2):
                    if j == 2:
                        pe.wait_ge(q_split[0], n + 1)
                    m = j - 1
                    for g in range(2):
                        for k in range(KD):
                            o = mm(bank[:, 7, g * SEQ:(g + 1) * SEQ], wqkv0[:, k, m * D + g * P:m * D + (g + 1) * P],
                                   xnT[:, k, :], start=(k == 0), stop=(k == KD - 1), skip_group_check=True)
                    o.then_inc(proj[0], 1)
                if l == 0 and j == 3:
                    pe.wait_ge(k_ready[0], n + 1)
                    for r in range(2):
                        for k in range(KD):
                            o = mm(bank[:, 7, r * D:(r + 1) * D], xnT[:, k, r * P:(r + 1) * P], wqkv0[:, k, 2 * D:3 * D],
                                   start=(k == 0), stop=(k == KD - 1), skip_group_check=True)
                    o.then_inc(proj[0], 1)
                if l and j in (1, 2):
                    r = j - 1
                    if r:
                        pe.wait_ge(rope_left, 2 * n + 1)
                    for k in range(KD):
                        o = mm(bank[:, 7, 0:384], xnT[:, k, r * P:(r + 1) * P], wqkv1[:, k, :],
                               start=(k == 0), stop=(k == KD - 1))
                    o.then_inc(proj[1], 1)
                if l and j == 3:
                    pe.wait_ge(rope_left, 2 * n + 2)
                    pe.wait_ge(roped, 4 * n + 4)
                    turned(q_r, proj[1])
                if l and j == 4:
                    pe.wait_ge(q_split[1], n + 1)
                    turned(k_r, proj[1])

            def turn_xm(b):
                pe.wait_ge(xm_ready, 2 * b + 2)
                if b >= 2:
                    pe.wait_ge(xmT_ready, b - 1)
                for k in range(KD):
                    for r in range(2):
                        o = tr(bank[:, 3 + b % 2, k * SEQ + r * P:k * SEQ + (r + 1) * P],
                               xm[:, 2 * b + r, k * P:(k + 1) * P], ident[:])
                o.then_inc(xmT_psum, 1)

            def logits(b):
                pe.wait_ge(xmT_ready, b + 1)
                for r in range(2):
                    t = 2 * b + r
                    for k in range(KD):
                        o = mm(bank[:, 0, t * NE:(t + 1) * NE], xmT[:, b, k, r * P:(r + 1) * P], gw[:, k, :],
                               start=(k == 0), stop=(k == KD - 1), skip_group_check=True)
                if b == NB - 1:
                    o.then_inc(lg_psum, 1)

            def context_weights():
                pe.wait_ge(s_ctx, 7 * 16)
                pe.wait_ge(p_ready[0], 4 * UNITS)
                for g in range(2):
                    o = mm(bank[0:DC, g, :], wk[:], ctxT[:, 2 * g:2 * g + 2, :].rearrange("p b n -> p (b n)"),
                           start=True, stop=True)
                o.then_inc(kv_psum, 1)
                for t in range(NT):
                    o = mm(bank[:, 2, t * DC:(t + 1) * DC], ctxT[:, t // 2, (t % 2) * P:(t % 2 + 1) * P], wk[:],
                           start=True, stop=True, skip_group_check=True)
                o.then_inc(kv_psum, 1)
                pe.wait_ge(setup, 6)
                pe.wait_ge(wabs_ready, 3)
                mm(bank[:, 3, 0:3], ones[:], wabs[:], start=True, stop=True).then_inc(wmean_psum, 1)

            def context_turn(b):
                pe.wait_ge(xn_ready, 2 * NB + 2 * b + 2)
                if b == 0:
                    pe.wait_ge(pT4_ready[0], UNITS)
                    pe.wait_ge(pT5_ready[0], UNITS)
                if b >= 2:
                    pe.wait_ge(xnT_ready, NB + b - 1)
                for k in range(KD):
                    for r in range(2):
                        o = tr(bank[:, 4 + b % 2, k * SEQ + r * P:k * SEQ + (r + 1) * P],
                               xm[:, 2 * b + r, k * P:(k + 1) * P], ident[:])
                o.then_inc(xnTp_ready, 1)

            def context_front(b):
                context_turn(b)
                pe.wait_ge(kvj_ready, 1)
                pe.wait_ge(xnT_ready, NB + b + 1)
                if b >= 1:
                    pe.wait_ge(outT_ready, b)
                if b == 0:
                    pe.wait_ge(on_ready[0], NB)
                for k in range(2):
                    o = mm(bank[0:DC, 6, 0:SEQ], kvj[:, 2 * b + k, :], xnTs[:, b % 2, k, :], start=(k == 0), stop=(k == 1))
                o.then_inc(outT_psum, 1)
                pe.wait_ge(outT_ready, b + 1)
                pe.wait_ge(kvT_ready, 2)
                if b == 3:
                    pe.wait_ge(sign_ready, 4)
                for r in range(2):
                    o = mm(bank[:, b, r * SEQ:(r + 1) * SEQ], outT[:, b % 2, r * P:(r + 1) * P], kvT[:, b, :],
                           start=True, stop=True, skip_group_check=True)
                o.then_inc(sim_ready, 1)

            def attention(l):
                def score(u):
                    b, j, i = u // PAIRS, u % PAIRS, u % 2
                    g = j // 4
                    if u == 0 and l == 0:
                        pe.wait_ge(casts, 2)
                    pe.wait_ge(kM_split[l], 2 * (u + 1))
                    if j == 0:
                        pe.wait_ge(q_split[l], b + 1)
                    if u >= 2:
                        pe.wait_ge(p_ready[l], 4 * (u - 1))
                    for r in range(2):
                        n = SEQ if r else P
                        view = bank[:, 2 * i + r, 0:2 * n].rearrange("p (e n) -> p e n", e=2)
                        q = [x[:, b % 2, g, r * P:(r + 1) * P] for x in (q_lead, q_trail)]
                        mm(view, q[0], kM[:, i, 0, :, 0:n], start=True, stop=False, skip_group_check=True)
                        mm(view, q[0], kM[:, i, 1, :, 0:n], start=False, stop=False, skip_group_check=True)
                        mm(view, q[1], kM[:, i, 0, :, 0:n], start=False, stop=False, skip_group_check=True)
                        mm(view[:, :, n - P:n], ident_h[:], causal_h[:].unsqueeze(1).to_broadcast([P, 2, P]),
                           start=False, stop=True, skip_group_check=True).then_inc(s_ready[l], 1)

                def turn(u):
                    pe.wait_ge(p_ready[l], 4 * (u + 1))
                    if u >= 1:
                        pe.wait_ge(pT4_ready[l], u)
                        pe.wait_ge(pT5_ready[l], u)
                    for m in range(6):
                        o = tr(bank[:, 4 + m // 4, (m % 4) * P:(m % 4 + 1) * P], prob[:, u % 2, m // 3, m % 3, :], ident[:])
                    o.then_inc(pT_psum[l], 1)

                def values(u):
                    b, j = u // PAIRS, u % PAIRS
                    pe.wait_ge(pT4_ready[l], u + 1)
                    pe.wait_ge(pT5_ready[l], u + 1)
                    if j == 0:
                        if l:
                            pe.wait_ge(rope_left, 2 * (b + 1))
                        else:
                            pe.wait_ge(v_ready[l], b + 1)
                        if b >= 1:
                            pe.wait_ge(on_ready[l], b)
                    for e in range(2):
                        h = 2 * j + e
                        v = h // 4 if l else h
                        for m in range(3):
                            r, k = (0, 0) if m == 0 else (1, m - 1)
                            o = mm(bank[:, 6, r * D + h * HD:r * D + (h + 1) * HD], probT[:, u % 2, 3 * e + m, :],
                                   V[:, b % 2, k, v * HD:(v + 1) * HD], start=(m < 2), stop=(m != 1), skip_group_check=True)
                    o.then_inc(av_done[l], 1)

                def back(n, j):
                    if j == 5:
                        pe.wait_ge(on_ready[l], n + 1)
                        if n + 2 < NB:
                            pe.wait_ge(k_ready[l] if l else v_ready[l], n + 3)
                        turned(On, oT_psum[l])
                    if j == 6:
                        pe.wait_ge(oT_ready[l], n + 1)
                        wo = wo1 if l else wo0
                        for r in range(2):
                            for k in range(KD):
                                o = mm(bank[:, 7, r * D:(r + 1) * D], OT[:, k, r * P:(r + 1) * P], wo[:, k, :],
                                       start=(k == 0), stop=(k == KD - 1), skip_group_check=True)
                        o.then_inc(y_ready, 1)

                for u, b, j in slots():
                    if 0 <= u + 1 < UNITS:
                        score(u + 1)
                    if 0 <= u < UNITS:
                        turn(u)
                    if 0 <= u - 1 < UNITS:
                        values(u - 1)
                    if l <= b + 1 < NB:
                        front(l, b + 1, j)
                    if STAGES > 1 and l == 0 and b == NB:
                        if j == 0:
                            context_weights()
                        if j == 1:
                            back(b - 1, 5)
                        if j == 3:
                            back(b - 1, 6)
                        if j in (2, 4, 5):
                            context_front((2, 4, 5).index(j))
                    elif 0 <= b - 1 < NB:
                        back(b - 1, j)

            pe.wait_ge(s_w0, 2 * 16)
            attention(0)

            if STAGES > 1:
                context_front(NB - 1)

            if STAGES > 2:
                pe.wait_ge(sign_ready, 4)

                def turn_xq(b):
                    pe.wait_ge(xq_ready, b + 1)
                    if b >= 1:
                        pe.wait_ge(xqT_ready, b)
                    for k in range(KD):
                        for r in range(2):
                            o = tr(bank[:, 7, k * SEQ + r * P:k * SEQ + (r + 1) * P], xns[:, b % 2, r, k * P:(k + 1) * P], ident[:])
                    o.then_inc(xqT_psum, 1)

                def ffn_in(t):
                    b, r = t // 2, t % 2
                    pe.wait_ge(xqT_ready, b + 1)
                    for c in range(2):
                        if t >= 1:
                            pe.wait_ge(hid_used, 2 * (t - 1) + c + 1)
                        for w in range(2):
                            for k in range(KD):
                                for part in range(2):
                                    o = mm(bank[:, 2 * c + w, :], xqT[:, b % 2, part, k, r * P:(r + 1) * P],
                                           s_in[w][:, k, c * 512:(c + 1) * 512], start=(k == 0 and part == 0),
                                           stop=(k == KD - 1 and part == 1))
                        o.then_inc(hid_psum, 1)

                def ffn_out(t):
                    pe.wait_ge(hT_ready, t + 1)
                    if t >= 2 and t % 2 == 0:
                        pe.wait_ge(x_done, 2 * NB + t // 2)
                    r = t % 2
                    for m in range(FF // P):
                        o = mm(bank[:, 6, r * D:(r + 1) * D], hidT[:, r, m, :], s3[:, m, :], start=(m == 0),
                               stop=(m == FF // P - 1), skip_group_check=True)
                    if r:
                        o.then_inc(y_ready, 1)

                turn_xq(0)
                for t in range(-1, NT + 1):
                    if t > 0 and t % 2 == 1:
                        ffn_out(t - 1)
                    if t + 1 < NT:
                        ffn_in(t + 1)
                    if STAGES > 3 and t == 5:
                        pe.wait_ge(s_w1, 4 * 16)
                    if STAGES > 3 and t >= 6:
                        front(1, 0, t - 5)
                    if t > 0 and t % 2 == 0:
                        ffn_out(t - 1)
                    if 0 <= t < NT:
                        pe.wait_ge(hq_ready, t + 1)
                        if t >= 1:
                            pe.wait_ge(hT_ready, t)
                        for m in range(FF // P):
                            o = tr(bank[:, 4 + m // 4, (m % 4) * P:(m % 4 + 1) * P], hid[:, t % 2, m * P:(m + 1) * P], ident[:])
                        o.then_inc(hT_psum, 1)
                    if t >= 0 and t % 2 == 0 and t // 2 + 1 < NB:
                        turn_xq(t // 2 + 1)
                    if STAGES > 3 and t == 5:
                        front(1, 0, 0)
                if STAGES > 3:
                    front(1, 0, 4)

            if STAGES > 3:
                pe.wait_ge(s_w1, 4 * 16)
                attention(1)

            if STAGES > 4:
                pe.wait_ge(s_wx, 10 * 16)
                for g in range(PAIRS // 2):
                    if g >= 2:
                        pe.wait_ge(fold_act, g - 1)
                    for m in range(4):
                        h, j = 4 * g + m, m // 2
                        o = mm(bank[DC * (m % 2):DC * (m % 2 + 1), g % 2, j * D:(j + 1) * D], wckv[:, h, :], wo_x[:, h, :],
                               start=True, stop=True, skip_group_check=True)
                    o.then_inc(fold_psum, 1)
                for g in range(NH // 4):
                    pe.wait_ge(fold_act, PAIRS // 2 + g - 1)
                    for m in range(8):
                        h, f = 4 * g + m // 2, m % 2
                        o = mm(bank[0:HC, g % 2, m * DC:(m + 1) * DC], wqr[:, h, f * HC:(f + 1) * HC], wkr[:, h, :],
                               start=True, stop=True, skip_group_check=True)
                    o.then_inc(fold_psum, 1)
                for h in range(NH):
                    if h < 2:
                        pe.wait_ge(fold_act, PAIRS // 2 + NH // 4 - 1 + h)
                    elif h >= 4:
                        pe.wait_ge(fold_dve, h - 3)
                    for k in range(KD):
                        o = mm(bank[:, h % 4, k * CQ:(k + 1) * CQ], wq_x[:, h, k * P:(k + 1) * P], wcq[:, h, :],
                               start=True, stop=True, skip_group_check=True)
                    o.then_inc(fold_psum, 1)
                pe.wait_ge(kvr_ready, 2)
                for t in range(NT):
                    o = tr(bank[:, 5 + t // 4, (t % 4) * P:(t % 4 + 1) * P], kvr[:, t].rearrange("p e n -> p (e n)"), ident[:])
                o.then_inc(kvrT_psum, 1)
                turn_xn(3 * NB, xn_ready, 2 * (4 * NB) + 2)
                pe.wait_ge(xT_split, 1)
                pe.wait_ge(fold_dve, NH)
                for u, b, h in cross_slots():
                    v = u + 1
                    if v < CROSS:
                        bv, hv = v // NH, v % NH
                        if v >= 2:
                            pe.wait_ge(qx_cs, 2 * (v - 1))
                        if hv == 10 and bv < NB - 1:
                            pe.wait_ge(xT_split, bv + 2)
                        for f in range(2):
                            for k in range(KD):
                                w = [Aq[part][:, hv, k, f * HC:(f + 1) * HC] for part in range(2)]
                                q = bank[0:HC, v % 2, f * SEQ:(f + 1) * SEQ]
                                mm(q, w[0], xT_lead[:, bv % 2, k, :], start=(k == 0), stop=False, skip_group_check=True)
                                mm(q, w[0], xT_trail[bv % 2][:, k, :], start=False, stop=False, skip_group_check=True)
                                o = mm(q, w[1], xT_lead[:, bv % 2, k, :], start=False, stop=(k == KD - 1),
                                       skip_group_check=True)
                        o.then_inc(qx_psum, 1)
                    if 0 <= u < CROSS:
                        pe.wait_ge(qx_ready, 2 * (u + 1))
                        if u >= 1:
                            pe.wait_ge(z_split, u)
                        if u >= 5:
                            pe.wait_ge(cT_ready, (u - 3) // 2)
                        for f in range(2):
                            o = mm(bank[:, 2, 0:SEQ], Gq[:, 2 * h + f].rearrange("p e n -> p (e n)"), qx_r[:, u % 2, f, :],
                                   start=(f == 0), stop=(f == 1), skip_group_check=True)
                        o.then_inc(z_psum, 1)
                    w = u - 1
                    if 0 <= w < CROSS:
                        pe.wait_ge(px_ready, 2 * (w + 1))
                        if w >= 1:
                            pe.wait_ge(pxT_ready, w)
                        if w == 0:
                            pe.wait_ge(kk_ready, 1)
                        for k in range(2):
                            for r in range(2):
                                o = tr(bank[:, 5, k * SEQ + r * P:k * SEQ + (r + 1) * P],
                                       px[:, w % 2, r, k * P:(k + 1) * P], ident[:])
                        o.then_inc(pxT_psum, 1)
                    w = u - 2
                    if 0 <= w < CROSS:
                        e = w % 2
                        pe.wait_ge(pxT_ready, w + 1)
                        if w >= 1:
                            pe.wait_ge(cn_ready, w)
                        for r in range(2):
                            for k in range(2):
                                o = mm(bank[:, 6, r * P + e * DC:r * P + (e + 1) * DC], pxT[:, w % 2, k, r * P:(r + 1) * P],
                                       kvr[:, 2 * (w // NH) + k, 0, :], start=(k == 0), stop=(k == 1), skip_group_check=True)
                        o.then_inc(cx_psum, 1)
                    w = u - 4
                    if w >= 0 and w % 2 == 1:
                        j = w // 2
                        pe.wait_ge(cT_ready, j + 1)
                        if j % PAIRS == 0 and j:
                            pe.wait_ge(x_done, 4 * NB + j // PAIRS)
                        for r in range(2):
                            o = mm(bank[:, 7, r * D:(r + 1) * D], cT[:, j % 2, r * P:(r + 1) * P], Cx[:, j % PAIRS, :],
                                   start=(j % PAIRS == 0 and r == 0), stop=(j % PAIRS == PAIRS - 1), skip_group_check=True)
                        if j % PAIRS == PAIRS - 1:
                            o.then_inc(y_ready, 1)
                    if 0 <= u < CROSS:
                        if u == 0:
                            pe.wait_ge(kk_ready, 1)
                        pe.wait_ge(z_split, u + 1)
                        if u >= 2:
                            pe.wait_ge(px_ready, 2 * (u - 1))
                        for r in range(2):
                            for part in range(2):
                                o = mm(bank[:, 3 + u % 2, r * SEQ:(r + 1) * SEQ], zz[:, u % 2, r * P:(r + 1) * P],
                                       kk[:, b, part, :], start=(part == 0), stop=(part == 1), skip_group_check=True)
                        o.then_inc(sx_ready, 1)
                    w = u - 3
                    if 0 <= w < CROSS and w % 2 == 1:
                        j = w // 2
                        pe.wait_ge(cn_ready, w + 1)
                        pe.wait_ge(z_split, min(u + 1, CROSS))
                        for r in range(2):
                            o = tr(bank[:, 2, 256 + r * P:256 + (r + 1) * P], cn[:, j % 2, r, :], ident[:])
                        o.then_inc(cT_psum, 1)
                    if STAGES > 5 and b == NB and h >= 1:
                        if h == 1:
                            pe.wait_ge(s_wm, 6 * 16)
                        turn_xm(h - 1)
                        if h >= 2:
                            logits(h - 2)
                    if h == 8 and 0 <= b < NB - 1:
                        pe.wait_ge(xn_ready, 2 * (4 * NB + b + 1) + 2)
                        pe.wait_ge(qx_cs, 2 * (u + 1))
                        for k in range(KD):
                            for r in range(2):
                                o = tr(bank[:, u % 2, k * SEQ + r * P:k * SEQ + (r + 1) * P],
                                       xns[:, (b + 1) % 2, r, k * P:(k + 1) * P], ident[:])
                        o.then_inc(xnTp_ready, 1)

            if STAGES > 5:
                pe.wait_ge(s_wm, 6 * 16)
                def shared_in(b):
                    if b >= 2:
                        pe.wait_ge(shg_ready, b - 1)
                        pe.wait_ge(shh_ready, b - 1)
                    for w, src in enumerate((sg, su)):
                        for f in range(2):
                            for k in range(KD):
                                o = mm(bank[:, (1, 2, 3, 5)[2 * (b % 2) + w], f * SEQ:(f + 1) * SEQ],
                                       src[:, k, f * P:(f + 1) * P], xmT[:, b, k, :],
                                       start=(k == 0), stop=(k == KD - 1), skip_group_check=True)
                    o.then_inc(sh_psum, 1)

                def shared_out(b):
                    pe.wait_ge(shh_ready, b + 1)
                    if b >= 2:
                        pe.wait_ge(x_done, 5 * NB + b - 1)
                    for r in range(2):
                        for f in range(2):
                            o = mm(bank[:, 6 + b % 2, r * D:(r + 1) * D], sh_h[:, b % 2, f, r * P:(r + 1) * P], sd[:, f, :],
                                   start=(f == 0), stop=(f == 1), skip_group_check=True)
                    o.then_inc(shy_psum, 1)

                turn_xm(NB - 1)
                logits(NB - 2)
                logits(NB - 1)
                shared_in(0)
                shared_in(1)
                pe.wait_ge(xmT_ready, NB)
                shared_out(0)
                shared_in(2)
                shared_out(1)
                shared_in(3)
                pe.wait_ge(mask_ready, 1)
                mm(bank[:, 4, 0:NT * NE], before, mask.rearrange("p t e -> p (t e)"), start=True, stop=False)
                mm(bank[:, 4, 0:NT * NE], ones[:], seen.rearrange("p t e -> p (t e)"), start=False,
                   stop=True).then_inc(pos_psum, 1)
                shared_out(2)
                shared_out(3)

                def gather(c, k, t):
                    if k == 0 and t == 0:
                        if c > 0:
                            pe.wait_ge(buf_ready, c)
                        else:
                            pe.wait_ge(XN_lead, NB)
                            pe.wait_ge(XN_trail, NB)
                            pe.wait_ge(esig_ready, 1)
                    pe.wait_ge(hot_ready, NT * c + t + 1)
                    for part in range(2):
                        o = mm(bank[:, k, :], XN[part][:, t, k * P:(k + 1) * P], hot[c % 2][:, t, :],
                               start=(t == 0 and part == 0), stop=(t == NT - 1 and part == 1), skip_group_check=True)
                    if k == KD - 1 and t == NT - 1:
                        o.then_inc(gat_psum, 1)

                for t in range(NT):
                    for k in range(KD):
                        gather(0, k, t)
                for c in range(NC):
                    i = c % 2
                    pe.wait_ge(weights_ready, 1)
                    if c > 0:
                        pe.wait_ge(hotT_even, NT // 2 * c)
                    for t in range(NT):
                        for part in range(2):
                            o = mm(bank[0:NE, 2, :], wgts[part][:, t, :], hot[i][:, t, :],
                                   start=(t == 0 and part == 0), stop=(t == NT - 1 and part == 1))
                    o.then_inc(ws_psum, 1)
                    pe.wait_ge(buf_ready, c + 1)
                    pe.wait_ge(experts_in[i], 16 * 3 * (c // 2 + 1))
                    for w in range(2):
                        for e in range(EC):
                            for k in range(KD):
                                o = mm(bank[:, 4 + w, e * CAP:(e + 1) * CAP],
                                       ew[:, i, w, (KD * e + k) * FE:(KD * e + k + 1) * FE], bufT[:, k, e * CAP:(e + 1) * CAP],
                                       start=(k == 0), stop=(k == KD - 1), skip_group_check=True)
                    o.then_inc(eh_psum, 1)
                    pe.wait_ge(ws_copied, c + 1)
                    if c > 0:
                        pe.wait_ge(hotT_odd, NT // 2 * c)
                    for s in range(KS):
                        o = mm(bank[:, 3, s * NE:(s + 1) * NE], ws_row[:, s * P:(s + 1) * P], ident[0:NE, 0:NE],
                               start=True, stop=True, skip_group_check=True)
                    o.then_inc(ws_turned, 1)
                    for t in range(NT):
                        if t == 1:
                            pe.wait_ge(ws_ready, 2 * (c + 1))
                        elif t >= 2 and t % 2 == 0:
                            pe.wait_ge(hotT_even, NT // 2 * c + t // 2)
                        elif t >= 3:
                            pe.wait_ge(hotT_odd, NT // 2 * c + t // 2)
                        for k in range(KS):
                            o = tr(bank[:, 2 + t % 2, k * P:(k + 1) * P], hot[i][:, t, k * P:(k + 1) * P].bitcast(F32), ident[:])
                        o.then_inc(hotT_psum, 1)
                        if c + 1 < NC:
                            gather(c + 1, 0, t)
                    pe.wait_ge(eh_ready, c + 1)
                    pe.wait_ge(x_done, 6 * NB + c * (NT // 2))
                    for e in range(EC):
                        s, half = e // 2, CAP * (e % 2)
                        o = mm(bank[half:half + CAP, 6 + s // 2, (s % 2) * D:(s % 2 + 1) * D], h_T[:, e * CAP:(e + 1) * CAP],
                               ew[:, i, 2, e * D:(e + 1) * D], start=True, stop=True, skip_group_check=True)
                    o.then_inc(ob_psum, 1)
                    if c + 1 < NC:
                        for t in range(NT):
                            gather(c + 1, 1, t)
                    pe.wait_ge(ob_ready, KS * (c + 1))
                    pe.wait_ge(hotT_even, NT // 2 * (c + 1))
                    pe.wait_ge(hotT_odd, NT // 2 * (c + 1))
                    for q in range(NT // 2):
                        n = c * (NT // 2) + q
                        if q >= 2:
                            pe.wait_ge(x_done, 6 * NB + n - 1)
                        for r in range(2):
                            for s in range(KS):
                                for part in range(2):
                                    o = mm(bank[:, 6 + n % 2, r * D:(r + 1) * D], hotT[:, 2 * q + r, s, :], ob[part][:, s, :],
                                           start=(s == 0 and part == 0), stop=(s == KS - 1 and part == 1), skip_group_check=True)
                        o.then_inc(ey_psum, 1)


def kernel(x, ctx_512, L0_attn_w_project, L0_attn_w_out, L0_xattn_W_k, L0_xattn_b_k, L0_xattn_ln_gamma, L0_xattn_ln_beta,
           L0_ffn_w1, L0_ffn_w2, L0_ffn_w3, L1_attn_Wq, L1_attn_Wk, L1_attn_Wv, L1_attn_Wproj, L1_xattn_Wq,
           L1_xattn_w_kc_q, L1_xattn_w_kc_kv, L1_xattn_W_qr, L1_xattn_W_kr, L1_xattn_Wo, L1_ffn_gate_w,
           L1_ffn_gate_bias, L1_ffn_w1, L1_ffn_w2, L1_ffn_w3, L1_ffn_shared_gate, L1_ffn_shared_up, L1_ffn_shared_down):
    import numpy as np
    import concourse.bacc as bacc
    from concourse.bass_utils import run_bass_kernel_spmd as run

    f = np.float32
    C = np.ascontiguousarray

    def angles(dim, length):
        inv = (f(1.0) / np.power(f(10000.0), np.arange(0, dim, 2, dtype=f) / f(dim))).astype(f)
        return np.arange(length, dtype=f)[:, None] * inv[None, :]

    t1 = np.concatenate([angles(HD, SEQ)] * 2, axis=1)
    sign1 = np.where(np.arange(HD) < HD // 2, f(-1), f(1))
    tq = np.repeat(angles(CQ, SEQ), 2, axis=1)
    sq = np.sin(tq)
    sinq = np.concatenate([sq[:, HC:], -sq[:, :HC]], axis=1)
    tk = np.repeat(angles(DC, SEQ), 2, axis=1)
    signk = np.where(np.arange(DC) < DC // 2, f(-1), f(1))
    n = np.arange(P)
    later = np.concatenate([
        (n[:, None] < n[None, :]).astype(f),
        np.broadcast_to(np.arange(NE, dtype=f), (P, NE)),
        np.broadcast_to(np.arange(CAP, dtype=f), (P, CAP)),
        np.broadcast_to((np.arange(NG)[None, :] < np.arange(NG)[:, None]).astype(f).ravel(), (P, NG * NG))], axis=1)
    consts = {
        "ident": np.eye(P, dtype=f),
        "causal": np.where(n[None, :] > n[:, None], f(-1e9), f(0)),
        "head_rows": (n[:, None] // HD == np.arange(8)[None, :]).astype(f),
        "cos1": np.cos(t1), "sin1": np.sin(t1) * sign1,
        "cosq": np.cos(tq).T, "sinq": sinq.T,
        "cosk": np.cos(tk), "sink": np.sin(tk) * signk,
        "later": later,
    }
    A = np.asarray

    def rows(w, k):
        return w.reshape(NC, EC, k, P, w.shape[2]).transpose(0, 3, 1, 2, 4).reshape(NC * P, EC * k * w.shape[2])

    arrays = {
        "x": A(x).reshape(NB * SEQ, D),
        "ctx": A(ctx_512).reshape(NB * SEQ, DC),
        "ctxT": A(ctx_512).reshape(NB * SEQ, DC).T,
        "w_qkv0": A(L0_attn_w_project).T, "w_o0": A(L0_attn_w_out).T,
        "w_k": A(L0_xattn_W_k).T, "b_k": A(L0_xattn_b_k), "gamma": A(L0_xattn_ln_gamma), "beta": A(L0_xattn_ln_beta),
        "w_f1": A(L0_ffn_w1).T, "w_f2": A(L0_ffn_w2).T, "w_f3": A(L0_ffn_w3).T,
        "w_qkv1": np.concatenate([A(L1_attn_Wq), A(L1_attn_Wk), A(L1_attn_Wv)], axis=1), "w_o1": A(L1_attn_Wproj),
        "w_xq": A(L1_xattn_Wq), "w_cq": A(L1_xattn_w_kc_q).reshape(NH * P, CQ),
        "w_ckv": A(L1_xattn_w_kc_kv).reshape(NH * P, DC), "w_xo": A(L1_xattn_Wo).T,
        "w_qr": A(L1_xattn_W_qr).transpose(2, 0, 1).reshape(64, NH * CQ),
        "w_kr": A(L1_xattn_W_kr).transpose(2, 0, 1).reshape(64, NH * DC),
        "w_gate": A(L1_ffn_gate_w).T, "b_gate": A(L1_ffn_gate_bias),
        "w_e": np.concatenate([rows(A(L1_ffn_w1), KD), rows(A(L1_ffn_w3), KD), rows(A(L1_ffn_w2), 1)], axis=1),
        "w_sg": A(L1_ffn_shared_gate), "w_su": A(L1_ffn_shared_up), "w_sd": A(L1_ffn_shared_down),
    }
    arrays.update({k: v.astype(f) for k, v in consts.items()})
    arrays = {k: C(v) for k, v in arrays.items()}
    nc = bacc.Bacc("TRN2", target_bir_lowering=False, num_devices=1)
    aps = {k: nc.dram_tensor("in_" + k, v.shape, mybir.dt.from_np(v.dtype), kind="ExternalInput").ap() for k, v in arrays.items()}
    out = nc.dram_tensor("out_x", (NB * SEQ, D), F32, kind="ExternalOutput").ap()
    build(nc, aps, out)
    r = run(nc, [{"in_" + k: v for k, v in arrays.items()}], core_ids=[0])
    return r.results[0]["out_x"].reshape(NB, SEQ, D)
```
